# Optimizing a Trainium2 kernel written in Bass

```python
import numpy as np
import jax
import jax.numpy as jnp

def _softmax(x, axis=-1):
    return jax.nn.softmax(x, axis=axis)

def _gelu(x):
    return jax.nn.gelu(x, approximate=True)

def _silu(x):
    return jax.nn.silu(x)

def _sigmoid(x):
    return jax.nn.sigmoid(x)

def _layernorm(x, axis=-1, eps=1e-05):
    m = jnp.mean(x, axis=axis, keepdims=True)
    v = jnp.var(x, axis=axis, keepdims=True)
    return (x - m) / jnp.sqrt(v + eps)

def _scatter_add(tgt, idx, src, axis=0):
    return tgt.at[idx].add(src)

def _segment_sum(src, seg, n):
    return jax.ops.segment_sum(src, seg, n)
kernel_name = 'mk_xattn_ffn_d2_seqx_r8_d917f8'

def setup_inputs(seed: int=0):
    np.random.seed(seed)
    _w = jnp.asarray

    def _rec_inputs():
        import jax
        import jax.numpy as jnp
        _rk = jax.random.key(seed)
        x = -0.0002928 + 1 * jax.random.normal(jax.random.fold_in(_rk, 1), (32, 128, 128), jnp.float32)
        _lenS = 128 - jax.random.randint(jax.random.fold_in(_rk, 7), (32,), 0, max(1, 128 // 4) + 1, jnp.int32)
        _lenS2 = 77 - jax.random.randint(jax.random.fold_in(_rk, 8), (32,), 0, max(1, 77 // 4) + 1, jnp.int32)
        _ctx_1024P = jax.random.normal(jax.random.fold_in(_rk, 11), (32, 16, 128), jnp.float32)
        _ctx_1024c = jax.random.dirichlet(jax.random.fold_in(_rk, 511), 0.3 * jnp.ones((16,), jnp.float32), (32, 77))
        _ctx_1024t = jnp.einsum('bsk,bkd->bsd', _ctx_1024c, _ctx_1024P)
        _ctx_1024t = _ctx_1024t * jax.lax.rsqrt(jnp.mean(jnp.square(_ctx_1024t)) + 1e-12) * 0.953939
        ctx_1024 = -1.39393e-06 + 0.999914 * (_ctx_1024t + 0.3 * jax.random.normal(jax.random.fold_in(_rk, 611), (32, 77, 128), jnp.float32))
        _validS = jnp.arange(128)[None, :] < _lenS[:, None]
        _validS2 = jnp.arange(77)[None, :] < _lenS2[:, None]
        _causal = jnp.tril(jnp.ones((128, 128), dtype=bool))
        mask_SxS2_bk1 = jnp.broadcast_to(_validS2[0:1, :], (128, 77))
        mask_BxS2_bf0 = jnp.logical_not(jnp.ones((32, 77), dtype=bool))
        return (x, ctx_1024, mask_SxS2_bk1, mask_BxS2_bf0)
    x, ctx_1024, mask_SxS2_bk1, mask_BxS2_bf0 = _rec_inputs()

    def _L0_xattn_setup():
        import jax, jax.numpy as jnp
        import numpy as np
        B, T, D, H = (2, 256, 128, 16)
        DK = D // H
        SCALE = 1.0 / float(np.sqrt(DK))
        key0 = jax.random.key(seed)
        ks = jax.random.split(key0, 12)
        std = 0.02
        inp = {'query': jax.random.normal(ks[0], (B, T, D), jnp.float32), 'key': jax.random.normal(ks[1], (B, T, D), jnp.float32), 'value': jax.random.normal(ks[2], (B, T, D), jnp.float32), 'Wq': jax.random.normal(ks[3], (D, D), jnp.float32) * std, 'bq': jnp.zeros((D,), jnp.float32), 'Wk': jax.random.normal(ks[4], (D, D), jnp.float32) * std, 'bk': jnp.zeros((D,), jnp.float32), 'Wv': jax.random.normal(ks[5], (D, D), jnp.float32) * std, 'bv': jnp.zeros((D,), jnp.float32), 'Wo': jax.random.normal(ks[6], (D, D), jnp.float32) * std, 'bo': jnp.zeros((D,), jnp.float32), 'attn_mask': jnp.triu(jnp.ones((T, T), jnp.bool_), k=1), 'key_padding_mask': jnp.zeros((B, T), jnp.bool_)}
        return inp
    _L0_xattn_all = _L0_xattn_setup()
    _L0_xattn_in = {k: v for k, v in _L0_xattn_all.items() if k in ('Wq', 'bq', 'Wk', 'bk', 'Wv', 'bv', 'Wo', 'bo')}
    del _L0_xattn_all

    def _L0_ffn_setup():
        import jax, jax.numpy as jnp
        import numpy as np
        B, T, D = (2, 256, 128)
        F = 512
        E = 8
        key = jax.random.key(seed)
        k0, k1, k2, k3 = jax.random.split(key, 4)
        x = jax.random.normal(k0, (B, T, D), dtype=jnp.float32)
        Wg = jax.random.normal(k1, (E, D), dtype=jnp.float32) * 0.02
        W1 = jax.random.normal(k2, (E, D, F), dtype=jnp.float32) * 0.02
        W2 = jax.random.normal(k3, (E, F, D), dtype=jnp.float32) * 0.02
        return {'x': x, 'Wg': Wg, 'W1': W1, 'W2': W2}
    _L0_ffn_all = _L0_ffn_setup()
    _L0_ffn_in = {k: v for k, v in _L0_ffn_all.items() if k in ('Wg', 'W1', 'W2')}
    del _L0_ffn_all

    def _L1_xattn_setup():
        import jax, jax.numpy as jnp
        import numpy as np
        EMBED_DIM = 128
        NUM_HEADS = 16
        HEAD_DIM = EMBED_DIM // NUM_HEADS
        WINDOW = 64

        def apply_rope(x):
            B, H, S, d = x.shape
            half = d // 2
            pos = jnp.arange(S, dtype=x.dtype)
            freqs = 1.0 / 10000.0 ** (jnp.arange(half, dtype=x.dtype) / half)
            ang = pos[:, None] * freqs[None, :]
            cos, sin = (jnp.cos(ang), jnp.sin(ang))
            x1, x2 = (x[..., :half], x[..., half:])
            return jnp.concatenate([x1 * cos - x2 * sin, x1 * sin + x2 * cos], axis=-1)

        def _forward(query, key, value, q_w, q_b, k_w, k_b, v_w, v_b, o_w, o_b):
            B, S_q, D = query.shape
            S_k = key.shape[1]
            H, d, W = (NUM_HEADS, HEAD_DIM, WINDOW)
            q = (query @ q_w.T + q_b).reshape(B, S_q, H, d).transpose(0, 2, 1, 3)
            k = (key @ k_w.T + k_b).reshape(B, S_k, H, d).transpose(0, 2, 1, 3)
            v = (value @ v_w.T + v_b).reshape(B, S_k, H, d).transpose(0, 2, 1, 3)
            q = apply_rope(q) * d ** (-0.5)
            k = apply_rope(k)
            q_pos = jnp.arange(S_q)[:, None]
            offsets = jnp.arange(-W, 1)[None, :]
            idx = q_pos + offsets
            local_mask = (idx < 0) | (idx >= S_k)
            gidx = jnp.clip(idx, 0, S_k - 1)
            k_win = k[:, :, gidx, :]
            v_win = v[:, :, gidx, :]
            scores = jnp.einsum('bhqd,bhqwd->bhqw', q, k_win)
            mask = local_mask[None, None, :, :]
            scores = jnp.where(mask, -jnp.inf, scores)
            m = jnp.max(scores, axis=-1, keepdims=True)
            m = jnp.where(jnp.isfinite(m), m, 0.0)
            e = jnp.exp(scores - m)
            denom = jnp.sum(e, axis=-1, keepdims=True)
            probs = jnp.where(denom > 0, e / jnp.where(denom > 0, denom, 1.0), 0.0)
            ctx = jnp.einsum('bhqw,bhqwd->bhqd', probs, v_win)
            ctx = ctx.transpose(0, 2, 1, 3).reshape(B, S_q, D)
            return ctx @ o_w.T + o_b
        key = jax.random.key(seed)
        ks = jax.random.split(key, 12)
        B, S, D = (1, 256, EMBED_DIM)
        scale = 1.0 / np.sqrt(D)
        inp = {'query': jax.random.normal(ks[0], (B, S, D), jnp.float32), 'key': jax.random.normal(ks[1], (B, S, D), jnp.float32), 'value': jax.random.normal(ks[2], (B, S, D), jnp.float32), 'q_w': jax.random.normal(ks[3], (D, D), jnp.float32) * scale, 'q_b': jax.random.normal(ks[4], (D,), jnp.float32) * 0.01, 'k_w': jax.random.normal(ks[5], (D, D), jnp.float32) * scale, 'k_b': jax.random.normal(ks[6], (D,), jnp.float32) * 0.01, 'v_w': jax.random.normal(ks[7], (D, D), jnp.float32) * scale, 'v_b': jax.random.normal(ks[8], (D,), jnp.float32) * 0.01, 'o_w': jax.random.normal(ks[9], (D, D), jnp.float32) * scale, 'o_b': jax.random.normal(ks[10], (D,), jnp.float32) * 0.01}
        return inp
    _L1_xattn_all = _L1_xattn_setup()
    _L1_xattn_in = {k: v for k, v in _L1_xattn_all.items() if k in ('q_w', 'q_b', 'k_w', 'k_b', 'v_w', 'v_b', 'o_w', 'o_b')}
    del _L1_xattn_all

    def _L1_ffn_setup():
        import jax, jax.numpy as jnp
        import numpy as np
        from jax import lax
        D = 128
        H = 176
        E = 8
        K = 2
        ROUTER_SCALE = 1.0

        def _expert(x, w1, b1, w3, b3, w2, b2):
            h = jax.nn.silu((x @ w1 + b1) * (x @ w3 + b3))
            return h @ w2 + b2
        key = jax.random.key(seed)
        ks = jax.random.split(key, 16)
        s = 0.02
        inp = {'x': jax.random.normal(ks[0], (2, 256, D), dtype=jnp.float32), 'gate_w': jax.random.normal(ks[1], (E, D), dtype=jnp.float32) * s, 'gate_b': jax.random.normal(ks[2], (E,), dtype=jnp.float32) * s, 'w1': jax.random.normal(ks[3], (E, D, H), dtype=jnp.float32) * s, 'b1': jax.random.normal(ks[4], (E, H), dtype=jnp.float32) * s, 'w3': jax.random.normal(ks[5], (E, D, H), dtype=jnp.float32) * s, 'b3': jax.random.normal(ks[6], (E, H), dtype=jnp.float32) * s, 'w2': jax.random.normal(ks[7], (E, H, D), dtype=jnp.float32) * s, 'b2': jax.random.normal(ks[8], (E, D), dtype=jnp.float32) * s, 'sw1': jax.random.normal(ks[9], (D, H), dtype=jnp.float32) * s, 'sb1': jax.random.normal(ks[10], (H,), dtype=jnp.float32) * s, 'sw3': jax.random.normal(ks[11], (D, H), dtype=jnp.float32) * s, 'sb3': jax.random.normal(ks[12], (H,), dtype=jnp.float32) * s, 'sw2': jax.random.normal(ks[13], (H, D), dtype=jnp.float32) * s, 'sb2': jax.random.normal(ks[14], (D,), dtype=jnp.float32) * s}
        return inp
    _L1_ffn_all = _L1_ffn_setup()
    _L1_ffn_in = {k: v for k, v in _L1_ffn_all.items() if k in ('gate_w', 'gate_b', 'w1', 'b1', 'w3', 'b3', 'w2', 'b2', 'sw1', 'sb1', 'sw3', 'sb3', 'sw2', 'sb2')}
    del _L1_ffn_all
    return {'x': x, 'ctx_1024': ctx_1024, 'mask_SxS2_bk1': mask_SxS2_bk1, 'mask_BxS2_bf0': mask_BxS2_bf0, 'L0_xattn_Wq': _L0_xattn_in['Wq'], 'L0_xattn_bq': _L0_xattn_in['bq'], 'L0_xattn_Wk': _L0_xattn_in['Wk'], 'L0_xattn_bk': _L0_xattn_in['bk'], 'L0_xattn_Wv': _L0_xattn_in['Wv'], 'L0_xattn_bv': _L0_xattn_in['bv'], 'L0_xattn_Wo': _L0_xattn_in['Wo'], 'L0_xattn_bo': _L0_xattn_in['bo'], 'L0_ffn_Wg': _L0_ffn_in['Wg'], 'L0_ffn_W1': _L0_ffn_in['W1'], 'L0_ffn_W2': _L0_ffn_in['W2'], 'L1_xattn_q_w': _L1_xattn_in['q_w'], 'L1_xattn_q_b': _L1_xattn_in['q_b'], 'L1_xattn_k_w': _L1_xattn_in['k_w'], 'L1_xattn_k_b': _L1_xattn_in['k_b'], 'L1_xattn_v_w': _L1_xattn_in['v_w'], 'L1_xattn_v_b': _L1_xattn_in['v_b'], 'L1_xattn_o_w': _L1_xattn_in['o_w'], 'L1_xattn_o_b': _L1_xattn_in['o_b'], 'L1_ffn_gate_w': _L1_ffn_in['gate_w'], 'L1_ffn_gate_b': _L1_ffn_in['gate_b'], 'L1_ffn_w1': _L1_ffn_in['w1'], 'L1_ffn_b1': _L1_ffn_in['b1'], 'L1_ffn_w3': _L1_ffn_in['w3'], 'L1_ffn_b3': _L1_ffn_in['b3'], 'L1_ffn_w2': _L1_ffn_in['w2'], 'L1_ffn_b2': _L1_ffn_in['b2'], 'L1_ffn_sw1': _L1_ffn_in['sw1'], 'L1_ffn_sb1': _L1_ffn_in['sb1'], 'L1_ffn_sw3': _L1_ffn_in['sw3'], 'L1_ffn_sb3': _L1_ffn_in['sb3'], 'L1_ffn_sw2': _L1_ffn_in['sw2'], 'L1_ffn_sb2': _L1_ffn_in['sb2']}

def reference(x, ctx_1024, mask_SxS2_bk1, mask_BxS2_bf0, L0_xattn_Wq, L0_xattn_bq, L0_xattn_Wk, L0_xattn_bk, L0_xattn_Wv, L0_xattn_bv, L0_xattn_Wo, L0_xattn_bo, L0_ffn_Wg, L0_ffn_W1, L0_ffn_W2, L1_xattn_q_w, L1_xattn_q_b, L1_xattn_k_w, L1_xattn_k_b, L1_xattn_v_w, L1_xattn_v_b, L1_xattn_o_w, L1_xattn_o_b, L1_ffn_gate_w, L1_ffn_gate_b, L1_ffn_w1, L1_ffn_b1, L1_ffn_w3, L1_ffn_b3, L1_ffn_w2, L1_ffn_b2, L1_ffn_sw1, L1_ffn_sb1, L1_ffn_sw3, L1_ffn_sb3, L1_ffn_sw2, L1_ffn_sb2):
    import jax
    import jax.numpy as jnp

    def _L0_xattn_ref(query, key, value, Wq, bq, Wk, bk, Wv, bv, Wo, bo, attn_mask, key_padding_mask):
        import jax, jax.numpy as jnp
        import numpy as np
        B, T, D, H = (2, 256, 128, 16)
        DK = D // H
        SCALE = 1.0 / float(np.sqrt(DK))
        Bq, Tq, _ = query.shape
        Tk = key.shape[1]
        q = (query @ Wq.T + bq).reshape(Bq, Tq, H, DK)
        k = (key @ Wk.T + bk).reshape(Bq, Tk, H, DK)
        v = (value @ Wv.T + bv).reshape(Bq, Tk, H, DK)
        scores = jnp.einsum('bqhd,bkhd->bhqk', q, k) * jnp.float32(SCALE)
        neg_inf = jnp.float32(-jnp.inf)
        scores = jnp.where(attn_mask[None, None, :, :], neg_inf, scores)
        scores = jnp.where(key_padding_mask[:, None, None, :], neg_inf, scores)
        attn = jax.nn.softmax(scores, axis=-1)
        out = jnp.einsum('bhqk,bkhd->bqhd', attn, v).reshape(Bq, Tq, D)
        return out @ Wo.T + bo

    def _L0_ffn_ref(x, Wg, W1, W2):
        import jax, jax.numpy as jnp
        import numpy as np
        B, T, D = (2, 256, 128)
        F = 512
        E = 8
        b, t, d = x.shape
        h = x.reshape(-1, d)
        logits = h @ Wg.T
        scores, idx = jax.lax.top_k(logits, 2)
        scores = jax.nn.softmax(scores.astype(jnp.float32), axis=-1).astype(x.dtype)
        up = jnp.einsum('nd,edf->enf', h, W1)
        act = jax.nn.silu(up)
        out = jnp.einsum('enf,efd->ned', act, W2)
        sel = jnp.take_along_axis(out, idx[:, :, None], axis=1)
        y = jnp.sum(scores[:, :, None] * sel, axis=1)
        return y.reshape(b, t, d)

    def _L1_xattn_ref(query, key, value, q_w, q_b, k_w, k_b, v_w, v_b, o_w, o_b):
        import jax, jax.numpy as jnp
        import numpy as np
        EMBED_DIM = 128
        NUM_HEADS = 16
        HEAD_DIM = EMBED_DIM // NUM_HEADS
        WINDOW = 64

        def apply_rope(x):
            B, H, S, d = x.shape
            half = d // 2
            pos = jnp.arange(S, dtype=x.dtype)
            freqs = 1.0 / 10000.0 ** (jnp.arange(half, dtype=x.dtype) / half)
            ang = pos[:, None] * freqs[None, :]
            cos, sin = (jnp.cos(ang), jnp.sin(ang))
            x1, x2 = (x[..., :half], x[..., half:])
            return jnp.concatenate([x1 * cos - x2 * sin, x1 * sin + x2 * cos], axis=-1)

        def _forward(query, key, value, q_w, q_b, k_w, k_b, v_w, v_b, o_w, o_b):
            B, S_q, D = query.shape
            S_k = key.shape[1]
            H, d, W = (NUM_HEADS, HEAD_DIM, WINDOW)
            q = (query @ q_w.T + q_b).reshape(B, S_q, H, d).transpose(0, 2, 1, 3)
            k = (key @ k_w.T + k_b).reshape(B, S_k, H, d).transpose(0, 2, 1, 3)
            v = (value @ v_w.T + v_b).reshape(B, S_k, H, d).transpose(0, 2, 1, 3)
            q = apply_rope(q) * d ** (-0.5)
            k = apply_rope(k)
            q_pos = jnp.arange(S_q)[:, None]
            offsets = jnp.arange(-W, 1)[None, :]
            idx = q_pos + offsets
            local_mask = (idx < 0) | (idx >= S_k)
            gidx = jnp.clip(idx, 0, S_k - 1)
            k_win = k[:, :, gidx, :]
            v_win = v[:, :, gidx, :]
            scores = jnp.einsum('bhqd,bhqwd->bhqw', q, k_win)
            mask = local_mask[None, None, :, :]
            scores = jnp.where(mask, -jnp.inf, scores)
            m = jnp.max(scores, axis=-1, keepdims=True)
            m = jnp.where(jnp.isfinite(m), m, 0.0)
            e = jnp.exp(scores - m)
            denom = jnp.sum(e, axis=-1, keepdims=True)
            probs = jnp.where(denom > 0, e / jnp.where(denom > 0, denom, 1.0), 0.0)
            ctx = jnp.einsum('bhqw,bhqwd->bhqd', probs, v_win)
            ctx = ctx.transpose(0, 2, 1, 3).reshape(B, S_q, D)
            return ctx @ o_w.T + o_b
        return _forward(query, key, value, q_w, q_b, k_w, k_b, v_w, v_b, o_w, o_b)

    def _L1_ffn_ref(x, gate_w, gate_b, w1, b1, w3, b3, w2, b2, sw1, sb1, sw3, sb3, sw2, sb2):
        import jax, jax.numpy as jnp
        import numpy as np
        from jax import lax
        D = 128
        H = 176
        E = 8
        K = 2
        ROUTER_SCALE = 1.0

        def _expert(x, w1, b1, w3, b3, w2, b2):
            h = jax.nn.silu((x @ w1 + b1) * (x @ w3 + b3))
            return h @ w2 + b2
        shape = x.shape
        xf = x.reshape(-1, D)
        T = xf.shape[0]
        scores = jax.nn.softmax(xf @ gate_w.T, axis=-1)
        biased = scores + gate_b
        _, idx = lax.top_k(biased, K)
        w = jnp.take_along_axis(scores, idx, axis=-1) * ROUTER_SCALE
        rw = jnp.zeros((T, E), dtype=xf.dtype).at[jnp.arange(T)[:, None], idx].add(w)
        h = jax.nn.silu((jnp.einsum('td,edh->teh', xf, w1) + b1) * (jnp.einsum('td,edh->teh', xf, w3) + b3))
        oe = jnp.einsum('teh,ehd->ted', h, w2) + b2
        y = jnp.einsum('te,ted->td', rw, oe)
        z = _expert(xf, sw1, sb1, sw3, sb3, sw2, sb2)
        return (y + z).reshape(shape)
    x = x + _L0_xattn_ref(_layernorm(x, axis=-1), ctx_1024, ctx_1024, L0_xattn_Wq, L0_xattn_bq, L0_xattn_Wk, L0_xattn_bk, L0_xattn_Wv, L0_xattn_bv, L0_xattn_Wo, L0_xattn_bo, mask_SxS2_bk1, mask_BxS2_bf0)
    x = x + _L0_ffn_ref(_layernorm(x, axis=-1), L0_ffn_Wg, L0_ffn_W1, L0_ffn_W2)
    x = x + _L1_xattn_ref(_layernorm(x, axis=-1), ctx_1024, ctx_1024, L1_xattn_q_w, L1_xattn_q_b, L1_xattn_k_w, L1_xattn_k_b, L1_xattn_v_w, L1_xattn_v_b, L1_xattn_o_w, L1_xattn_o_b)
    x = x + _L1_ffn_ref(_layernorm(x, axis=-1), L1_ffn_gate_w, L1_ffn_gate_b, L1_ffn_w1, L1_ffn_b1, L1_ffn_w3, L1_ffn_b3, L1_ffn_w2, L1_ffn_b2, L1_ffn_sw1, L1_ffn_sb1, L1_ffn_sw3, L1_ffn_sb3, L1_ffn_sw2, L1_ffn_sb2)
    return x

_drawn_inputs = setup_inputs


def setup_inputs(seed=0):
    import zlib

    import numpy as np

    out = dict(_drawn_inputs(seed))
    spreads = {'L0_xattn_bq': (0.0, 0.8),
     'L0_xattn_bk': (0.0, 2.0),
     'L0_xattn_bv': (0.0, 0.386),
     'L0_xattn_bo': (0.0, 0.1)}
    factors = {'L0_xattn_Wq': 8.0,
     'L0_xattn_Wk': 8.0,
     'L1_xattn_q_b': 8.0,
     'L1_xattn_k_b': 8.0,
     'L1_xattn_v_b': 5.822,
     'L1_xattn_o_b': 5.839,
     'L1_ffn_gate_w': 8.0,
     'L1_ffn_gate_b': 8.0,
     'L1_ffn_w1': 8.0,
     'L1_ffn_b1': 8.0,
     'L1_ffn_w3': 8.0,
     'L1_ffn_b3': 8.0,
     'L1_ffn_w2': 8.0,
     'L1_ffn_b2': 28.729,
     'L1_ffn_sw1': 8.0,
     'L1_ffn_sb1': 8.0,
     'L1_ffn_sw3': 8.0,
     'L1_ffn_sb3': 8.0,
     'L1_ffn_sw2': 8.0,
     'L1_ffn_sb2': 16.65}
    for name, (base, spread) in spreads.items():
        noise = np.random.default_rng([zlib.crc32(name.encode()), seed]).standard_normal(out[name].shape)
        drawn = base * np.exp(spread * noise) if base else spread * noise
        out[name] = jnp.asarray(drawn.astype(out[name].dtype))
    for name, factor in factors.items():
        out[name] = (out[name] * factor).astype(out[name].dtype)
    return out
```

```python
from contextlib import ExitStack

import numpy as np

import concourse.bass as bass
from concourse import mybir

F32 = mybir.dt.float32
BF16 = mybir.dt.bfloat16
U8 = mybir.dt.uint8
U32 = mybir.dt.uint32
ALU = mybir.AluOpType
ACT = mybir.ActivationFunctionType
AX = mybir.AxisListType

B, T, D = 32, 128, 128
TK = 77
H, DH = 16, 8
G, J = 4, 4
SCALE = DH ** -0.5
WINDOW = 64
EPS = 1e-5
NP = B // 2
GK = J * TK
VW = D + H
VM = 2448
MASKED = -1e30
E0, F0 = 8, 512
E1, F1 = 8, 176
E = E0
SLOTS = 2 * B * T // 128 + E

C_ID, C_HM, C_GM, C_BAND, C_COS, C_SIN, C_HALF, C_EPS = 0, 128, 132, 136, 216, 344, 472, 474
C_BEFORE, C_SAME, C_BACK, C_SLOT = 476, 604, 860, 868
C_END = 940


def shape_constants():
    c = np.zeros((128, C_END), np.float32)
    p = np.arange(128)
    c[:, C_ID:C_ID + 128] = np.eye(128)
    c[p, C_HM + (p % 32) // DH] = 1.0
    c[p, C_GM + p // 32] = 1.0
    q, k = np.arange(T)[:, None], np.arange(TK)[None, :]
    c[:, C_BAND:C_BAND + TK] = np.where((k < q - WINDOW) | (k > q), MASKED, 0.0)
    half = DH // 2
    freqs = (np.float32(1.0) / np.float32(10000.0) ** (np.arange(half, dtype=np.float32) / np.float32(half)))
    ang = np.arange(T, dtype=np.float32)[None, :] * freqs.astype(np.float32)[p % half][:, None]
    c[:, C_COS:C_COS + T] = np.cos(ang)
    c[:, C_SIN:C_SIN + T] = np.sin(ang) * np.where(p % DH < half, -1.0, 1.0)[:, None]
    c[:, C_BEFORE:C_BEFORE + 128] = p[:, None] < p[None, :]
    c[:, C_SAME:C_SAME + E * B] = np.arange(E * B) % B != 0
    c[:, C_BACK:C_BACK + E] = E - np.arange(E)
    c[:, C_SLOT:C_SLOT + SLOTS] = np.arange(SLOTS)
    c[:, C_HALF:C_HALF + 2] = -0.5
    c[:, C_EPS:C_EPS + 2] = EPS
    return c


class Steps:

    def __init__(self, sem, per_turn=0):
        self.sem, self.n, self.base = sem, 0, 0

    def at(self, base):
        self.n, self.base = 0, base

    def then(self, eng, ins):
        self.n += 1
        ins.then_inc(self.sem, 1)
        eng.wait_ge(self.sem, self.base + self.n)


def attention(nc, st, layer, w):
    rope = layer == 1
    with ExitStack() as ctx:
        def sb(name, shape, dt=F32):
            return ctx.enter_context(nc.sbuf_tensor(f"{name}_{layer}", shape, dt))

        def pb(name, shape, dt=F32):
            return ctx.enter_context(nc.psum_tensor(f"{name}_{layer}", shape, dt))

        def sem(name):
            return ctx.enter_context(nc.semaphore(f"{name}_{layer}"))

        x, cst, identb = st["x"], st["cst"], st["identb"]
        ident = cst[:, C_ID:C_ID + 128]
        names = ["q", "k", "v", "o"] + (["qr", "kr"] if rope else [])
        W = sb("W", [128, len(names), 128])
        cols = sb("cols", [128, len(names)])
        wt = {n: W[:, i, :] for i, n in enumerate(names)}
        bias = {n: cols[:, i:i + 1] for i, n in enumerate(names)}
        bo = sb("bo", [128, 128])
        bv = sb("bv", [128, 128])
        ctxT = sb("ctxT", [128, 2 * TK])
        stats = sb("stats", [128, 2, 6])
        mv = sb("mv", [128, 2, 2])
        rstd = sb("rstd", [128, 2])
        vare = sb("vare", [128, 2])
        xn = sb("xn", [128, 2, 128])
        xnT = sb("xnT", [128, 2 * T])
        qexp = sb("qexp", [128, 2, G, T])
        kT = sb("kT", [128, 2 * TK])
        krT = sb("krT", [128, 2 * TK]) if rope else None
        kro = sb("kro", [128, 2, TK]) if rope else None
        kcos = sb("kcos", [128, 2, TK]) if rope else None
        ksin = sb("ksin", [128, 2, TK]) if rope else None
        qro = sb("qro", [128, 2, T]) if rope else None
        qcos = sb("qcos", [128, 2, T]) if rope else None
        qsin = sb("qsin", [128, 2, T]) if rope else None
        kexp = sb("kexp", [128, 2, J, TK])
        vs = sb("vs", [TK, 2, 128])
        vm = sb("vm", [TK, 2, VM])
        bias_qk = sb("bias_qk", [128, 2, TK], BF16)
        pr = sb("pr", [128, 2, H, TK])
        mx = sb("mx", [128, H])
        pT = sb("pT", [TK, G, J, T])
        rden = sb("rden", [128, H])
        an = sb("an", [128, 2, 128])
        aT = sb("aT", [128, 128])
        if not rope:
            am8 = sb("am8", [128, TK], U8)
            negA = sb("negA", [128, TK])
            amT8 = sb("amT8", [TK, 128], U8)
            keepA = sb("keepA", [TK, 128])
            pad8 = sb("pad8", [128, B * TK], U8)
            negP = sb("negP", [128, B * TK])
            padT8 = sb("padT8", [TK, B], U8)
            keepP = sb("keepP", [TK, B])
            some = sb("some", [128, B])
            isome = sb("isome", [128, B])
            nz = sb("nz", [128, B])

        S = pb("S", [128, G, 512])
        ptp = [pb(f"ptp{i}", [TK, J, T]) for i in range(2)]
        M0 = pb("M0", [128, 512])
        M1 = pb("M1", [128, 512])
        O, anTp, Y = M0[:, 0:VW], M0[:, VW:VW + 128], M1[:, 0:128]
        xTp, Qp, Qrp = M1[:, 0:256], M1[:, 256:512], M1[:, 0:256]
        Kp, Krp = S[:, 0, GK:GK + 2 * TK], S[:, 1, GK:GK + 2 * TK]
        Vp = [S[0:TK, 2, GK:GK + 128], S[0:TK, 3, GK:GK + 128]]

        consts_in = sem("consts_in")
        ctx_in = sem("ctx_in")
        vm_set = sem("vm_set")
        masks_set = sem("masks_set")
        counts_ready = sem("counts_ready")
        mv_ready = sem("mv_ready")
        rstd_ready = sem("rstd_ready")
        xn_ready = sem("xn_ready")
        xT_ready = sem("xT_ready")
        xT_copied = sem("xT_copied")
        q_ready = sem("q_ready")
        qexp_ready = sem("qexp_ready")
        kv_ready = sem("kv_ready")
        kv_copied = sem("kv_copied")
        kexp_ready = sem("kexp_ready")
        vm_ready = sem("vm_ready")
        s_ready = sem("s_ready")
        sub_done = sem("sub_done")
        exp_done = sem("exp_done")
        pt_ready = sem("pt_ready")
        pt_copied = sem("pt_copied")
        pv_done = sem("pv_done")
        norm_done = sem("norm_done")
        anT_ready = sem("anT_ready")
        aT_copied = sem("aT_copied")
        y_ready = sem("y_ready")
        bo_added = sem("bo_added")
        res_done = sem("res_done")
        dve_step = sem("dve_step")
        pool_step = sem("pool_step")

        n_const = 16 * (4 + (0 if rope else 4))

        def turns(eng, body):
            body(0, first=True)
            with eng.Fori(1, NP - 1) as i:
                body(i)
            body(NP - 1, last=True)

        def wait(eng, s, value):
            if not isinstance(value, int) or value > 0:
                eng.wait_ge(s, value)

        block = ctx.enter_context(nc.Block())

        @block.sync
        def _(sp):
            def load_ctx(j):
                wait(sp, kv_ready, j)
                sp.dma_start(ctxT[:, :], st["ctxT_dram"][:, bass.ds(j * (2 * TK), 2 * TK)]).then_inc(ctx_in, 16)

            sp.dma_start(W[:, :, :], w["W"]).then_inc(consts_in, 16)
            sp.dma_start(cols[:, :], w["cols"]).then_inc(consts_in, 16)
            sp.dma_start(bo[:, :], w["bo"].partition_broadcast(128)).then_inc(consts_in, 16)
            sp.dma_start(bv[:, :], w["bv"].partition_broadcast(128)).then_inc(consts_in, 16)
            load_ctx(0)
            if not rope:
                sp.dma_start(am8[:, :], w["am"]).then_inc(consts_in, 16)
                sp.dma_start(amT8[:, :], w["amT"]).then_inc(consts_in, 16)
                sp.dma_start(pad8[:, :], w["pad"].partition_broadcast(128)).then_inc(consts_in, 16)
                sp.dma_start(padT8[:, :], w["padT"]).then_inc(consts_in, 16)
            load_ctx(1)
            with sp.Fori(2, NP) as j:
                load_ctx(j)

        @block.gpsimd
        def _(pool):
            steps = Steps(pool_step)
            nc.gpsimd.memset(vm[:, :, :], 0.0).then_inc(pool_step, 1)
            pool.wait_ge(pool_step, 1)
            for s in range(2):
                last = nc.gpsimd.memset(vm[:, s, D:D + H * (VW + 1)].rearrange("k (h c) -> k h c", h=H)[:, :, 0:1], 1.0)
            last.then_inc(vm_set, 1)
            pool.wait_ge(vm_set, 1)
            pool.wait_ge(consts_in, n_const)
            pool.wait_ge(st["consts_in"], st["n_consts"])
            base = 1
            if rope:
                for s in range(2):
                    last = nc.gpsimd.tensor_copy(bias_qk[:, s, :], cst[:, C_BAND:C_BAND + TK])
                last.then_inc(masks_set, 1)
            per_turn = 4 if rope else 3

            def front(j, first=False):
                steps.at(base + per_turn * j)
                pool.wait_ge(mv_ready, j + 1)
                steps.then(pool, nc.gpsimd.tensor_tensor(vare[:, :], mv[:, :, 1], cst[:, C_EPS:C_EPS + 2], ALU.add))
                nc.gpsimd.tensor_tensor(rstd[:, :], vare[:, :], cst[:, C_HALF:C_HALF + 2], ALU.pow).then_inc(rstd_ready, 1)
                pool.wait_ge(kv_copied, j + 1)
                k2 = kT[:, :].rearrange("p (s k) -> p s k", s=2)
                if rope:
                    kr2 = krT[:, :].rearrange("p (s k) -> p s k", s=2)
                    tab = [cst[:, c:c + TK].unsqueeze(1).broadcast_to([128, 2, TK]) for c in (C_COS, C_SIN)]
                    steps.then(pool, nc.gpsimd.tensor_tensor(kcos[:, :, :], k2, tab[0], ALU.mult))
                    steps.then(pool, nc.gpsimd.tensor_tensor(ksin[:, :, :], kr2, tab[1], ALU.mult))
                    steps.then(pool, nc.gpsimd.tensor_tensor(kro[:, :, :], kcos[:, :, :], ksin[:, :, :], ALU.add))
                    k2 = kro[:, :, :]
                for s in range(2):
                    n = j * 2 + s
                    wait(pool, s_ready, n - 1 if not first else 0)
                    if not rope:
                        pool.wait_ge(masks_set, 1)
                        steps.then(pool, nc.gpsimd.tensor_tensor(
                            bias_qk[:, s, :], negA[:, :], negP[:, bass.ds(n * TK, TK)], ALU.add))
                    nc.gpsimd.tensor_tensor(
                        kexp[:, s, :, :], k2[:, s, :].unsqueeze(1).broadcast_to([128, J, TK]),
                        cst[:, C_HM:C_HM + J].unsqueeze(2).broadcast_to([128, J, TK]), ALU.mult).then_inc(kexp_ready, 1)
                pool.wait_ge(xn_ready, 2 * j + 2)
                for s in range(2):
                    n = j * 2 + s
                    wait(pool, pv_done, n - 1 if not first else 0)
                    own = vm[:, s, 0:H * (VW + DH)].rearrange("k (h c) -> k h c", h=H)[:, :, 0:DH]
                    nc.gpsimd.tensor_tensor(own, vs[:, s, :].rearrange("k (h d) -> k h d", d=DH),
                                            bv[0:TK, :].rearrange("k (h d) -> k h d", d=DH), ALU.add).then_inc(vm_ready, 1)
                for s in range(2):
                    n = j * 2 + s
                    xb = x[:, bass.ds(n, 1), :].rearrange("p a d -> p (a d)")
                    nc.gpsimd.tensor_tensor(xb, xb, bo[:, :], ALU.add).then_inc(bo_added, 1)

            front(0, first=True)
            with pool.Fori(1, NP) as j:
                front(j)

        @block.scalar
        def _(act):
            act.wait_ge(consts_in, n_const)

            def x_copy(j):
                act.wait_ge(xT_ready, j + 1)
                nc.scalar.activation(xnT[:, :], xTp, ACT.Copy).then_inc(xT_copied, 1)

            def kv_copy(j, first=False):
                act.wait_ge(kv_ready, j + 1)
                wait(act, vm_ready, 2 * j if not first else 0)
                nc.scalar.activation(kT[:, :], Kp, ACT.Identity, bias=bias["k"])
                if rope:
                    nc.scalar.activation(krT[:, :], Krp, ACT.Identity, bias=bias["kr"])
                for s in range(2):
                    last = nc.scalar.activation(vs[:, s, :], Vp[s], ACT.Copy)
                last.then_inc(kv_copied, 1)

            def pt_copy(n, r):
                act.wait_ge(pt_ready, n * G + (r + 1))
                nc.scalar.activation(pT[:, r, :, :], ptp[r % 2][:, :, :], ACT.Copy).then_inc(pt_copied, 1)

            def exps(n, s):
                act.wait_ge(sub_done, n + 1)
                p = pr[:, s, :, :].rearrange("p h k -> p (h k)")
                nc.scalar.activation(p, p, ACT.Exp, scale=SCALE).then_inc(exp_done, 1)

            def at_copy(n):
                act.wait_ge(anT_ready, n + 1)
                nc.scalar.activation(aT[:, :], anTp, ACT.Copy).then_inc(aT_copied, 1)

            x_copy(0)
            kv_copy(0, first=True)

            def turn(i, first=False, last=False):
                a, b = 2 * i, 2 * i + 1
                if not first:
                    at_copy(a - 2)
                    for r in range(3):
                        pt_copy(b - 2, r)
                exps(a, 0)
                if not first:
                    pt_copy(b - 2, 3)
                    at_copy(b - 2)
                if not last:
                    x_copy(i + 1)
                pt_copy(a, 0)
                pt_copy(a, 1)
                if not last:
                    kv_copy(i + 1)
                exps(b, 1)
                pt_copy(a, 2)
                pt_copy(a, 3)

            turns(act, turn)
            at_copy(B - 2)
            for r in range(G):
                pt_copy(B - 1, r)
            at_copy(B - 1)

        @block.vector
        def _(dve):
            steps = Steps(dve_step)
            dve.wait_ge(consts_in, n_const)
            dve.wait_ge(st["consts_in"], st["n_consts"])
            pre = 0
            if not rope:
                nc.vector.tensor_scalar(negA[:, :], am8[:, :], MASKED, None, ALU.mult)
                nc.vector.tensor_scalar(negP[:, :], pad8[:, :], MASKED, None, ALU.mult).then_inc(masks_set, 1)
                nc.vector.tensor_scalar(keepA[:, :], amT8[:, :], -1.0, 1.0, ALU.mult, ALU.add)
                nc.vector.tensor_scalar(keepP[:, :], padT8[:, :], -1.0, 1.0, ALU.mult, ALU.add).then_inc(masks_set, 1)
                dve.wait_ge(counts_ready, 1)
                steps.at(0)
                steps.then(dve, nc.vector.tensor_scalar(some[:, :], Y[:, 0:B], 1.0, None, ALU.min))
                steps.then(dve, nc.vector.reciprocal(isome[:, :], some[:, :]))
                steps.then(dve, nc.vector.tensor_tensor(nz[:, :], some[:, :], isome[:, :], ALU.mult))
                pre = steps.n
            per_ln, per_soft, per_q, per_norm = 1, 1, (3 if rope else 0), 1
            per_turn = per_ln + 2 * per_soft + per_q + 2 * per_norm

            def row(n):
                return x[:, bass.ds(n, 1), :].rearrange("p a d -> p (a d)")

            def norm_stats(j):
                for s in range(2):
                    last = nc.vector.bn_stats(stats[:, s, :], row(j * 2 + s))
                last.then_inc(dve_step, 1)
                steps.n += 1

            def norm_mean(j):
                for s in range(2):
                    last = nc.vector.bn_aggr(mv[:, s, :], stats[:, s, :])
                last.then_inc(mv_ready, 1)

            def norm_x(j):
                dve.wait_ge(rstd_ready, j + 1)
                for s in range(2):
                    nc.vector.tensor_scalar(xn[:, s, :], row(j * 2 + s), mv[:, s, 0:1], rstd[:, s:s + 1],
                                            ALU.subtract, ALU.mult).then_inc(xn_ready, 1)

            def q_expand(j, first=False):
                dve.wait_ge(q_ready, j + 1)
                wait(dve, s_ready, 2 * j if not first else 0)
                gm = cst[:, C_GM:C_GM + G].unsqueeze(2).broadcast_to([128, G, T])
                q2 = Qp.rearrange("p (s q) -> p s q", s=2)
                if rope:
                    tab = [cst[:, c:c + T].unsqueeze(1).broadcast_to([128, 2, T]) for c in (C_COS, C_SIN)]
                    steps.then(dve, nc.vector.scalar_tensor_tensor(
                        qcos[:, :, :], q2, bias["q"], tab[0], ALU.add, ALU.mult))
                    steps.then(dve, nc.vector.scalar_tensor_tensor(
                        qsin[:, :, :], Qrp.rearrange("p (s q) -> p s q", s=2), bias["qr"], tab[1], ALU.add, ALU.mult))
                    steps.then(dve, nc.vector.tensor_tensor(qro[:, :, :], qcos[:, :, :], qsin[:, :, :], ALU.add))
                for s in range(2):
                    if rope:
                        last = nc.vector.tensor_tensor(
                            qexp[:, s, :, :], qro[:, s, :].unsqueeze(1).broadcast_to([128, G, T]), gm, ALU.mult)
                    else:
                        last = nc.vector.scalar_tensor_tensor(
                            qexp[:, s, :, :], q2[:, s, :].unsqueeze(1).broadcast_to([128, G, T]), bias["q"], gm,
                            ALU.add, ALU.mult)
                last.then_inc(qexp_ready, 1)

            def softmax_shift(n, s, first=False):
                dve.wait_ge(s_ready, n + 1)
                sc = S[:, :, 0:GK].rearrange("p g (j k) -> p g j k", k=TK)
                steps.then(dve, nc.vector.tensor_reduce(
                    mx[:, :].rearrange("p (g j) -> p g j", g=G), sc, AX.X, ALU.max))
                wait(dve, pv_done, n - 1 if not first else 0)
                nc.vector.tensor_tensor(
                    pr[:, s, :, :].rearrange("p (g j) k -> p g j k", g=G), sc,
                    mx[:, :].rearrange("p (g j) -> p g j", g=G).unsqueeze(3).broadcast_to([128, G, J, TK]),
                    ALU.subtract).then_inc(sub_done, 1)

            def normalise(n, s):
                dve.wait_ge(pv_done, n + 1)
                steps.then(dve, nc.vector.reciprocal(rden[:, :], O[:, D:VW]))
                nc.vector.scalar_tensor_tensor(
                    an[:, s, :].rearrange("p (h d) -> p h d", d=DH), O[:, 0:D].rearrange("p (h d) -> p h d", d=DH),
                    1.0 if rope else nz[:, bass.ds(n, 1)], rden[:, :].unsqueeze(2).broadcast_to([128, H, DH]),
                    ALU.mult, ALU.mult).then_inc(norm_done, 1)

            def residual(n):
                dve.wait_ge(y_ready, n + 1)
                dve.wait_ge(bo_added, n + 1)
                xb = x[:, bass.ds(n, 1), :].rearrange("p a d -> p (a d)")
                nc.vector.tensor_tensor(xb, xb, Y, ALU.add).then_inc(res_done, 1)

            steps.at(pre)
            if layer == 0:
                dve.wait_ge(st["x_in"], 16)
            norm_stats(0)
            dve.wait_ge(dve_step, pre + 1)
            norm_mean(0)
            norm_x(0)
            if layer == 0:
                dve.wait_ge(st["x_in"], 32)
            q_expand(0, first=True)
            start = pre + steps.n

            def turn(i, first=False, last=False):
                a, b = 2 * i, 2 * i + 1
                steps.at(start if first else start + per_turn * i - per_norm)
                if not last:
                    norm_stats(i + 1)
                softmax_shift(a, 0, first)
                if not last:
                    norm_mean(i + 1)
                if not first:
                    normalise(b - 2, 1)
                    residual(a - 2)
                if not last:
                    norm_x(i + 1)
                softmax_shift(b, 1, first)
                if not last:
                    q_expand(i + 1)
                normalise(a, 0)
                if not first:
                    residual(b - 2)

            turns(dve, turn)
            normalise(B - 1, 1)
            residual(B - 2)
            residual(B - 1)

        @block.tensor
        def _(pe):
            pe.wait_ge(consts_in, n_const)
            pe.wait_ge(st["consts_in"], st["n_consts"])
            if not rope:
                pe.wait_ge(masks_set, 2)
                nc.tensor.matmul(Y[:, 0:B], keepA[:, :], keepP[:, :], start=True, stop=True).then_inc(counts_ready, 1)
            else:
                pe.wait_ge(masks_set, 1)
            pe.wait_ge(st["ident_ready"], 1)

            def front_x(j, first=False, second=False):
                pe.wait_ge(xn_ready, 2 * j + 2)
                wait(pe, res_done, 2 * j - 3 if not first and not second else 0)
                for s in range(2):
                    last = nc.tensor.transpose(xTp[:, s * T:(s + 1) * T], xn[:, s, :], ident)
                last.then_inc(xT_ready, 1)

            def front_qkv(j, first=False):
                pe.wait_ge(xT_copied, j + 1)
                nc_q = nc.tensor.matmul(Qp, wt["q"], xnT[:, :], start=True, stop=True)
                if rope:
                    nc_q = nc.tensor.matmul(Qrp, wt["qr"], xnT[:, :], start=True, stop=True)
                nc_q.then_inc(q_ready, 1)
                pe.wait_ge(ctx_in, 16 * j + 16)
                wait(pe, sub_done, 2 * j)
                nc.tensor.matmul(Kp, wt["k"], ctxT[:, :], start=True, stop=True)
                if rope:
                    nc.tensor.matmul(Krp, wt["kr"], ctxT[:, :], start=True, stop=True)
                for s in range(2):
                    last = nc.tensor.matmul(Vp[s], ctxT[:, s * TK:(s + 1) * TK], wt["v"], start=True, stop=True)
                last.then_inc(kv_ready, 1)

            def scores(n, s, i, first=False):
                pe.wait_ge(qexp_ready, i + 1)
                pe.wait_ge(kexp_ready, n + 1)
                wait(pe, sub_done, n if not (first and s == 0) else 0)
                for g in range(G):
                    out = S[:, g, 0:GK]
                    nc.tensor.matmul(out, qexp[:, s, g, :], kexp[:, s, :, :], start=True, stop=False)
                    last = nc.tensor.matmul(out, identb[:, :], bias_qk[:, s, :].unsqueeze(1).broadcast_to([128, J, TK]),
                                            start=False, stop=True)
                last.then_inc(s_ready, 1)

            def transpose_group(n, s, r, first=False):
                wait(pe, pt_copied, n * G + (r - 1) if not (first and r < 2) else 0)
                for j in range(J):
                    last = nc.tensor.transpose(ptp[r % 2][:, j, :], pr[:, s, r * J + j, :], ident)
                last.then_inc(pt_ready, 1)

            def value_group(n, s, r):
                if r == 0:
                    wait(pe, aT_copied, n - 1)
                pe.wait_ge(pt_copied, n * G + (r + 1))
                for j in range(J):
                    h = r * J + j
                    last = nc.tensor.matmul(O, pT[:, r, j, :], vm[:, s, h * VW:(h + 1) * VW], start=(h == 0), stop=(h == H - 1))
                if r == G - 1:
                    last.then_inc(pv_done, 1)

            def values(n, s, first=False, between=None):
                pe.wait_ge(exp_done, n + 1)
                transpose_group(n, s, 0, first)
                transpose_group(n, s, 1, first)
                pe.wait_ge(vm_ready, n + 1)
                value_group(n, s, 0)
                transpose_group(n, s, 2)
                value_group(n, s, 1)
                if between:
                    between()
                transpose_group(n, s, 3)
                value_group(n, s, 2)
                value_group(n, s, 3)

            def transpose_out(n, s):
                pe.wait_ge(norm_done, n + 1)
                nc.tensor.transpose(anTp, an[:, s, :], ident).then_inc(anT_ready, 1)

            def project_out(n, s=0, q_pair=0):
                pe.wait_ge(aT_copied, n + 1)
                wait(pe, res_done, n)
                if s:
                    wait(pe, qexp_ready, q_pair)
                nc.tensor.matmul(Y, aT[:, :], wt["o"], start=True, stop=True).then_inc(y_ready, 1)

            front_x(0, first=True)
            front_qkv(0, first=True)

            def turn(i, first=False, last=False):
                a, b = 2 * i, 2 * i + 1
                scores(a, 0, i, first)
                if not first:
                    transpose_out(a - 2, 0)
                    values(b - 2, 1)
                    project_out(a - 2)
                scores(b, 1, i, first)
                if not first:
                    transpose_out(b - 2, 1)
                if not last:
                    front_x(i + 1, second=first)
                values(a, 0, first, between=None if last else (lambda: front_qkv(i + 1)))
                if not first:
                    project_out(b - 2, 1, i + 1 if last else i + 2)

            turns(pe, turn)
            transpose_out(B - 2, 0)
            values(B - 1, 1)
            project_out(B - 2)
            transpose_out(B - 1, 1)
            project_out(B - 1)


def experts(nc, st, layer, w):
    two = layer == 1
    F = F1 if two else F0
    FC = 2 if two else 4
    UW = 2 * F if two else F
    NSH = B if two else 0
    NS = NSH + SLOTS
    with ExitStack() as ctx:
        def sb(name, shape, dt=F32):
            return ctx.enter_context(nc.sbuf_tensor(f"{name}_e{layer}", shape, dt))

        def sem(name):
            return ctx.enter_context(nc.semaphore(f"{name}_e{layer}"))

        x, cst = st["x"], st["cst"]
        ident = cst[:, C_ID:C_ID + 128]
        NE = E + (1 if two else 0)
        Wg = sb("Wg", [128, E])
        W1 = sb("W1", [128, NE, UW])
        W2 = sb("W2", [128, NE, FC, D])
        B1 = sb("B1", [128, NE, UW]) if two else None
        B2 = sb("B2", [128, NE, D]) if two else None
        gb = sb("gb", [128, E]) if two else None
        ones = sb("ones", [128, 128])
        stats = sb("stats", [128, 2, 6])
        mv = sb("mv", [128, 2, 2])
        vare = sb("vare", [128, 2])
        rstd = sb("rstd", [128, 2])
        xn = sb("xn", [128, 2, D])
        xnT = sb("xnT", [128, 2, T])
        xn_all = sb("xn_all", [128, B, D])
        lg = sb("lg", [128, B, E])
        key = sb("key", [128, B, E])
        tmp = sb("tmp", [128, B, E])
        prob = sb("prob", [128, B, E]) if two else lg
        oh = sb("oh", [128, 2, B, E])
        m = sb("m", [128, 3, B])
        wsel = sb("wsel", [128, 2, B])
        incl = sb("incl", [128, E, B])
        pos = sb("pos", [128, E, B])
        cu = sb("cu", [128, 2, E], U32)
        tl = sb("tl", [128, 3, E])
        start = sb("start", [128, E])
        posf = sb("posf", [128, 2, B])
        posi = sb("posi", [128, 2, B], U32)
        cmp = sb("cmp", [128, SLOTS, E])
        emf = sb("emf", [128, SLOTS])
        emap = sb("emap", [128, NS], mybir.dt.int32)
        xs = sb("xs", [128, 2, D])
        xsT = sb("xsT", [128, 2, 128])
        hb = sb("hb", [128, 2, UW])
        hm = sb("hm", [128, 2, F]) if two else None
        h = sb("h", [128, 2, FC * 128])
        hT = sb("hT", [128, 2, FC, 128])
        ys = sb("ys", [128, 2, D])
        yg = sb("yg", [128, B, 2, D])
        z = sb("z", [128, B, D]) if two else None

        xTp = ctx.enter_context(nc.psum_tensor(f"xTp_e{layer}", [128, 4, 128], F32))
        lgp = ctx.enter_context(nc.psum_tensor(f"lgp_e{layer}", [128, 512], F32))
        up = [ctx.enter_context(nc.psum_tensor(f"up{i}_e{layer}", [128, 512], F32)) for i in range(2)]
        hTp = [ctx.enter_context(nc.psum_tensor(f"hTp{i}_e{layer}", [128, 4, 128], F32)) for i in range(2)]
        yp = [ctx.enter_context(nc.psum_tensor(f"yp{i}_e{layer}", [128, 512], F32)) for i in range(2)]

        w_in = sem("w_in")
        n_w = 16 * (6 if two else 3)
        ones_set = sem("ones_set")
        h_set = sem("h_set")
        mv_ready, rstd_ready, xn_ready = sem("mv_ready"), sem("rstd_ready"), sem("xn_ready")
        xn_kept = sem("xn_kept")
        xn_stored = sem("xn_stored")
        xT_ready, xT_copied = sem("xT_ready"), sem("xT_copied")
        lg_ready, lg_copied = sem("lg_ready"), sem("lg_copied")
        shifted, exp_ready = sem("shifted"), sem("exp_ready")
        oh_ready = sem("oh_ready")
        rank_ready = sem("rank_ready")
        pos_ready = sem("pos_ready")
        emap_ready = sem("emap_ready")
        scattered = sem("scattered")
        xs_in = [sem("xs_in_a"), sem("xs_in_b")]
        xsT_ready, xsT_copied = sem("xsT_ready"), sem("xsT_copied")
        up_ready, hb_ready, up_read = sem("up_ready"), sem("hb_ready"), sem("up_read")
        h_ready = sem("h_ready")
        hT_ready, hT_copied = sem("hT_ready"), sem("hT_copied")
        yp_ready, ys_ready = sem("yp_ready"), sem("ys_ready")
        ys_out = [sem("ys_out_a"), sem("ys_out_b")]
        z_in = sem("z_in")
        gathered = [sem(f"gathered{c}") for c in range(4)]
        pool_step, dve_step = sem("pool_step"), sem("dve_step")

        Xs, Ys = w["Xs"], w["Ys"]

        def wait(eng, s, value):
            if not isinstance(value, int) or value > 0:
                eng.wait_ge(s, value)

        def row(t, n):
            return t[:, bass.ds(n, 1), :].rearrange("p a d -> p (a d)")

        def pairs(eng, body):
            body(0, first=True)
            with eng.Fori(1, NP) as j:
                body(j)

        def slot_turns(eng, body):
            body(0, first=True)
            with eng.Fori(1, NS // 2) as i:
                body(i)
            body(NS // 2, last=True)

        block = ctx.enter_context(nc.Block())

        @block.sync
        def _(sp):
            sp.dma_start(Wg[:, :], w["Wg"]).then_inc(w_in, 16)
            sp.dma_start(W1[:, :, :], w["W1"]).then_inc(w_in, 16)
            sp.dma_start(W2[:, :, :, :], w["W2"]).then_inc(w_in, 16)
            if two:
                sp.dma_start(B1[:, :, :], w["B1"].partition_broadcast(128)).then_inc(w_in, 16)
                sp.dma_start(B2[:, :, :], w["B2"].partition_broadcast(128)).then_inc(w_in, 16)
                sp.dma_start(gb[:, :], w["gb"].partition_broadcast(128)).then_inc(w_in, 16)

                def store_xn(j, first=False):
                    sp.wait_ge(xn_ready, 2 * j + 2)
                    sp.dma_start(Xs[bass.ds(j * 256, 256), :].rearrange("(s p) d -> p s d", p=128),
                                 xn[:, :, :]).then_inc(xn_stored, 16)

                pairs(sp, store_xn)

            def load(n, s):
                wait(sp, xsT_ready, n - 1)
                sp.dma_start(xs[:, s, :], Xs[bass.ds(n * 128, 128), :]).then_inc(xs_in[s], 16)

            def store(n, s):
                sp.wait_ge(ys_ready, n + 1)
                sp.dma_start(Ys[bass.ds(n * 128, 128), :], ys[:, s, :]).then_inc(ys_out[s], 16)

            def turn(i, fill=True, drain=True):
                for s in range(2):
                    if fill:
                        load(2 * i + 2 + s, s)
                    if drain:
                        store(2 * i - 2 + s, s)

            if two:
                sp.wait_ge(xn_stored, 16 * NP)
            else:
                sp.wait_ge(scattered, 16 * 2 * B)
            load(0, 0)
            load(1, 1)
            turn(0, drain=False)
            if two:
                with sp.Fori(1, NSH // 2 - 1) as i:
                    turn(i)
                sp.wait_ge(scattered, 16 * 2 * B)
            with sp.Fori(max(NSH // 2 - 1, 1), NS // 2 - 1) as i:
                turn(i)
            for i in (NS // 2 - 1, NS // 2):
                turn(i, fill=False)
            if two:
                for s in range(2):
                    sp.wait_ge(ys_out[s], 16 * NS // 2)
                sp.dma_start(z[:, :, :], Ys[0:B * T, :].rearrange("(b p) d -> p b d", p=128)).then_inc(z_in, 16)

        @block.gpsimd
        def _(pool):
            steps = Steps(pool_step)
            nc.gpsimd.memset(ones[:, :], 1.0).then_inc(ones_set, 1)
            if two:
                nc.gpsimd.memset(h[:, :, :], 0.0).then_inc(h_set, 1)
                nc.gpsimd.memset(emap[:, 0:NSH], E).then_inc(h_set, 1)

            def norm(j, first=False):
                steps.at(j * 1)
                pool.wait_ge(mv_ready, j + 1)
                steps.then(pool, nc.gpsimd.tensor_tensor(vare[:, :], mv[:, :, 1], cst[:, C_EPS:C_EPS + 2], ALU.add))
                nc.gpsimd.tensor_tensor(rstd[:, :], vare[:, :], cst[:, C_HALF:C_HALF + 2], ALU.pow).then_inc(rstd_ready, 1)

            pairs(pool, norm)
            pool.wait_ge(xn_kept, NP)
            pool.wait_ge(pos_ready, 1)
            pool.wait_ge(st["zeroed"], st["n_zeroed"])
            for t in range(B):
                for k in range(2):
                    nc.gpsimd.indirect_dma_start(
                        Xs[:, :], bass.IndirectOffsetOnAxis(posi[:, k, t:t + 1], 0),
                        xn_all[:, t, :], None).then_inc(scattered, 16)
            for s in range(2):
                pool.wait_ge(ys_out[s], 16 * NS // 2)
            for t in range(B):
                for k in range(2):
                    nc.gpsimd.indirect_dma_start(
                        yg[:, t, k, :], None, Ys[:, :],
                        bass.IndirectOffsetOnAxis(posi[:, k, t:t + 1], 0)).then_inc(gathered[t // (B // 4)], 16)

        @block.scalar
        def _(act):
            def keep(j, first=False):
                act.wait_ge(xT_ready, j + 1)
                nc.scalar.activation(xnT[:, :, :], xTp[:, 0:2, :], ACT.Copy).then_inc(xT_copied, 1)
                nc.scalar.activation(xn_all[:, bass.ds(j * 2, 2), :], xn[:, :, :], ACT.Copy).then_inc(xn_kept, 1)

            pairs(act, keep)
            act.wait_ge(shifted, 1)
            if two:
                nc.scalar.activation(prob[:, :, :], tmp[:, :, :], ACT.Exp).then_inc(exp_ready, 1)
            else:
                nc.scalar.activation(m[:, 2, :], m[:, 2, :], ACT.Exp).then_inc(exp_ready, 1)
            if two:
                act.wait_ge(h_set, 2)

            def x_copy(n, s):
                act.wait_ge(xsT_ready, n + 1)
                nc.scalar.activation(xsT[:, s, :], xTp[:, 0, :], ACT.Copy).then_inc(xsT_copied, 1)

            def silu(n, s):
                if two:
                    act.wait_ge(hb_ready, n + 1)
                    nc.scalar.activation(h[:, s, 0:F], hm[:, s, :], ACT.Silu).then_inc(h_ready, 1)
                else:
                    act.wait_ge(up_ready, n + 1)
                    nc.scalar.activation(h[:, s, :], up[s][:, :], ACT.Silu).then_inc(h_ready, 1)

            def h_copy(n, s):
                act.wait_ge(hT_ready, n + 1)
                nc.scalar.activation(hT[:, s, :, :], hTp[s][:, 0:FC, :], ACT.Copy).then_inc(hT_copied, 1)

            def turn(i, first=False, last=False):
                for s in range(2):
                    n = 2 * i + s
                    if not last:
                        x_copy(n, s)
                        silu(n, s)
                    if two and not (first and s == 0) and not (last and s == 1):
                        h_copy(n - 1, 1 - s)

            slot_turns(act, turn)

        @block.vector
        def _(dve):
            steps = Steps(dve_step)

            def router(j, first=False):
                steps.at(j * 2)
                for s in range(2):
                    last = nc.vector.bn_stats(stats[:, s, :], row(x, j * 2 + s))
                last.then_inc(dve_step, 1)
                steps.n += 1
                if not first:
                    dve.wait_ge(dve_step, j * 2 + 1)
                    dve.wait_ge(lg_ready, j)
                    nc.vector.tensor_copy(lg[:, bass.ds(j * 2 - 2, 2), :], lgp[:, 0:2 * E].rearrange("p (s e) -> p s e", s=2))\
                        .then_inc(lg_copied, 1)
                else:
                    dve.wait_ge(dve_step, 1)
                for s in range(2):
                    last = nc.vector.bn_aggr(mv[:, s, :], stats[:, s, :])
                last.then_inc(mv_ready, 1)
                wait(dve, xn_kept, j)
                if two:
                    wait(dve, xn_stored, 16 * j)
                dve.wait_ge(rstd_ready, j + 1)
                for s in range(2):
                    nc.vector.tensor_scalar(xn[:, s, :], row(x, j * 2 + s), mv[:, s, 0:1], rstd[:, s:s + 1],
                                            ALU.subtract, ALU.mult).then_inc(xn_ready, 1)
                dve.sem_inc(dve_step, 1)

            pairs(dve, router)
            dve.wait_ge(lg_ready, NP)
            steps.at(2 * NP)
            nc.vector.tensor_copy(lg[:, B - 2:B, :], lgp[:, 0:2 * E].rearrange("p (s e) -> p s e", s=2)).then_inc(lg_copied, 1)
            dve.wait_ge(lg_copied, NP)

            def do(ins):
                steps.then(dve, ins)

            def over_e(a):
                return a.unsqueeze(2).broadcast_to([128, B, E])

            V = nc.vector
            back = cst[:, C_BACK:C_BACK + E].unsqueeze(1).broadcast_to([128, B, E])
            if two:
                dve.wait_ge(w_in, n_w)
                do(V.tensor_reduce(m[:, 0, :], lg[:, :, :], AX.X, ALU.max))
                V.tensor_tensor(tmp[:, :, :], lg[:, :, :], over_e(m[:, 0, :]), ALU.subtract).then_inc(shifted, 1)
                dve.wait_ge(exp_ready, 1)
                do(V.tensor_reduce(m[:, 1, :], prob[:, :, :], AX.X, ALU.add))
                do(V.reciprocal(m[:, 2, :], m[:, 1, :]))
                do(V.tensor_tensor(prob[:, :, :], prob[:, :, :], over_e(m[:, 2, :]), ALU.mult))
                do(V.tensor_tensor(key[:, :, :], prob[:, :, :], gb[:, :].unsqueeze(1).broadcast_to([128, B, E]), ALU.add))
                do(V.tensor_scalar(key[:, :, :], key[:, :, :], -1e38, None, ALU.max))
            else:
                do(V.tensor_scalar(key[:, :, :], lg[:, :, :], -1e38, None, ALU.max))
            for k in range(2):
                do(V.tensor_reduce(m[:, k, :], key[:, :, :], AX.X, ALU.max))
                do(V.tensor_tensor(tmp[:, :, :], key[:, :, :], over_e(m[:, k, :]), ALU.is_equal))
                do(V.tensor_tensor(tmp[:, :, :], tmp[:, :, :], back, ALU.mult))
                do(V.tensor_reduce(m[:, 2, :], tmp[:, :, :], AX.X, ALU.max))
                do(V.tensor_tensor(oh[:, k, :, :], over_e(m[:, 2, :]), back, ALU.is_equal))
                if k == 0:
                    do(V.scalar_tensor_tensor(key[:, :, :], oh[:, 0, :, :], -2e38, key[:, :, :], ALU.mult, ALU.add))
            V.tensor_tensor(tmp[:, :, :], oh[:, 0, :, :], oh[:, 1, :, :], ALU.add).then_inc(oh_ready, 1)
            if not two:
                do(V.tensor_tensor(m[:, 2, :], m[:, 1, :], m[:, 0, :], ALU.subtract))
                V.tensor_copy(m[:, 1, :], m[:, 2, :]).then_inc(shifted, 1)
                dve.wait_ge(exp_ready, 1)
                do(V.tensor_scalar(m[:, 0, :], m[:, 2, :], 1.0, None, ALU.add))
                do(V.reciprocal(wsel[:, 0, :], m[:, 0, :]))
                do(V.tensor_tensor(wsel[:, 1, :], m[:, 2, :], wsel[:, 0, :], ALU.mult))
            dve.wait_ge(rank_ready, 1)
            before, count = lgp[:, 0:E * B].rearrange("p (e t) -> p e t", e=E), lgp[:, E * B:2 * E * B]
            do(V.tensor_tensor_scan(incl[:, :, :].rearrange("p e t -> p (e t)"), cst[:, C_SAME:C_SAME + E * B], count, 0.0,
                                    ALU.mult, ALU.add))
            do(V.tensor_scalar(cu[:, 0, :], incl[:, :, B - 1], 127.0, None, ALU.add))
            do(V.tensor_scalar(cu[:, 1, :], cu[:, 0, :], 7, None, ALU.logical_shift_right))
            do(V.tensor_copy(tl[:, 0, :], cu[:, 1, :]))
            do(V.tensor_tensor_scan(tl[:, 1, :], ones[:, 0:E], tl[:, 0, :], 0.0, ALU.mult, ALU.add))
            do(V.tensor_tensor(tl[:, 2, :], tl[:, 1, :], tl[:, 0, :], ALU.subtract))
            do(V.tensor_scalar(start[:, :], tl[:, 2, :], 128.0, float(NSH * 128), ALU.mult, ALU.add))
            do(V.tensor_tensor(pos[:, :, :], incl[:, :, :], start[:, :].unsqueeze(2).broadcast_to([128, E, B]), ALU.add))
            do(V.tensor_tensor(pos[:, :, :], pos[:, :, :], count.rearrange("p (e t) -> p e t", e=E), ALU.subtract))
            do(V.tensor_tensor(pos[:, :, :], pos[:, :, :], before, ALU.add))
            for k in range(2):
                do(V.tensor_tensor(tmp[:, :, :], oh[:, k, :, :], pos[:, :, :].rearrange("p e t -> p t e"), ALU.mult))
                do(V.tensor_reduce(posf[:, k, :], tmp[:, :, :], AX.X, ALU.add))
            V.tensor_copy(posi[:, :, :], posf[:, :, :]).then_inc(pos_ready, 1)
            if two:
                for k in range(2):
                    do(V.tensor_tensor(tmp[:, :, :], oh[:, k, :, :], prob[:, :, :], ALU.mult))
                    do(V.tensor_reduce(wsel[:, k, :], tmp[:, :, :], AX.X, ALU.add))
            do(V.tensor_tensor(cmp[:, :, :], cst[:, C_SLOT:C_SLOT + SLOTS].unsqueeze(2).broadcast_to([128, SLOTS, E]),
                               tl[:, 1, :].unsqueeze(1).broadcast_to([128, SLOTS, E]), ALU.is_ge))
            do(V.tensor_reduce(emf[:, :], cmp[:, :, :], AX.X, ALU.add))
            V.tensor_scalar(emap[:, NSH:NS], emf[:, :], float(E - 1), None, ALU.min).then_inc(emap_ready, 1)
            dve.wait_ge(emap_ready, 1)
            if two:
                dve.wait_ge(h_set, 2)
            per_slot = 1 if two else 0
            s0 = steps.base + steps.n

            def hidden(n, s):
                steps.at(s0 + n * per_slot)
                e = dve.value_load(emap[0:1, bass.ds(n, 1)], min_val=0, max_val=NE - 1)
                dve.wait_ge(up_ready, n + 1)
                steps.then(dve, V.tensor_tensor(hb[:, s, :], up[s][:, 0:UW], row(B1, e), ALU.add))
                V.tensor_tensor(hm[:, s, :], hb[:, s, 0:F], hb[:, s, F:UW], ALU.mult).then_inc(hb_ready, 1)

            def h_copy(n, s):
                dve.wait_ge(hT_ready, n + 1)
                V.tensor_copy(hT[:, s, :, :], hTp[s][:, 0:FC, :]).then_inc(hT_copied, 1)

            def y_copy(n, s, i):
                dve.wait_ge(yp_ready, n + 1)
                wait(dve, ys_out[s], 16 * i)
                if two:
                    e = dve.value_load(emap[0:1, bass.ds(n, 1)], min_val=0, max_val=NE - 1)
                    V.tensor_tensor(ys[:, s, :], yp[s][:, 0:D], row(B2, e), ALU.add).then_inc(ys_ready, 1)
                else:
                    V.tensor_copy(ys[:, s, :], yp[s][:, 0:D]).then_inc(ys_ready, 1)

            def turn(i, first=False, last=False):
                for s in range(2):
                    n = 2 * i + s
                    if two:
                        if not last:
                            hidden(n, s)
                    elif not (first and s == 0) and not (last and s == 1):
                        h_copy(n - 1, 1 - s)
                    if not first:
                        y_copy(n - 2, s, i - 1)

            slot_turns(dve, turn)
            steps.at(s0 + NS * per_slot)
            if two:
                dve.wait_ge(z_in, 16)
                for c in range(4):
                    sl = slice(c * B // 4, (c + 1) * B // 4)
                    do(V.tensor_tensor(x[:, sl, :], x[:, sl, :], z[:, sl, :], ALU.add))
            c0 = steps.base + steps.n
            for c in range(4):
                dve.wait_ge(gathered[c], 16 * 2 * B // 4)
                with dve.Fori(c * (B // 4), (c + 1) * (B // 4)) as t:
                    steps.at(c0 + t)
                    g = yg[:, bass.ds(t, 1), :, :].rearrange("p a k d -> p (a k) d")
                    steps.then(dve, V.scalar_tensor_tensor(row(x, t), g[:, 0, :], wsel[:, 0, bass.ds(t, 1)], row(x, t),
                                                           ALU.mult, ALU.add))
                    V.scalar_tensor_tensor(row(x, t), g[:, 1, :], wsel[:, 1, bass.ds(t, 1)], row(x, t), ALU.mult, ALU.add)

        @block.tensor
        def _(pe):
            pe.wait_ge(w_in, n_w)
            pe.wait_ge(ones_set, 1)

            def router(j, first=False):
                pe.wait_ge(xn_ready, 2 * j + 2)
                for s in range(2):
                    last = nc.tensor.transpose(xTp[:, s, :], xn[:, s, :], ident)
                last.then_inc(xT_ready, 1)
                pe.wait_ge(xT_copied, j + 1)
                wait(pe, lg_copied, j)
                for s in range(2):
                    last = nc.tensor.matmul(lgp[:, s * E:(s + 1) * E], xnT[:, s, :], Wg[:, :], start=True, stop=True)
                last.then_inc(lg_ready, 1)

            pairs(pe, router)
            pe.wait_ge(oh_ready, 1)
            chosen = tmp[:, :, :].rearrange("p t e -> p e t")
            nc.tensor.matmul(lgp[:, 0:E * B], cst[:, C_BEFORE:C_BEFORE + 128], chosen, start=True, stop=True)
            nc.tensor.matmul(lgp[:, E * B:2 * E * B], ones[:, :], chosen, start=True, stop=True).then_inc(rank_ready, 1)
            if two:
                pe.wait_ge(h_set, 2)
            pe.wait_ge(emap_ready, 1)

            def take(n, s, i):
                pe.wait_ge(xs_in[s], 16 * i + 16)
                wait(pe, xsT_copied, n)
                nc.tensor.transpose(xTp[:, 0, :], xs[:, s, :], ident).then_inc(xsT_ready, 1)

            def widen(n, s):
                e = pe.value_load(emap[0:1, bass.ds(n, 1)], min_val=0, max_val=NE - 1)
                pe.wait_ge(xsT_copied, n + 1)
                wait(pe, hb_ready if two else h_ready, n - 1)
                nc.tensor.matmul(up[s][:, 0:UW], xsT[:, s, :], row(W1, e), start=True, stop=True).then_inc(up_ready, 1)

            def turn_hidden(n, s):
                pe.wait_ge(h_ready, n + 1)
                wait(pe, hT_copied, n - 1)
                for c in range(FC):
                    last = nc.tensor.transpose(hTp[s][:, c, :], h[:, s, c * 128:(c + 1) * 128], ident)
                last.then_inc(hT_ready, 1)

            def narrow(n, s):
                e = pe.value_load(emap[0:1, bass.ds(n, 1)], min_val=0, max_val=NE - 1)
                pe.wait_ge(hT_copied, n + 1)
                wait(pe, ys_ready, n - 1)
                w2 = W2[:, bass.ds(e, 1), :, :].rearrange("p a c d -> p (a c) d")
                for c in range(FC):
                    last = nc.tensor.matmul(yp[s][:, 0:D], hT[:, s, c, :], w2[:, c, :], start=(c == 0), stop=(c == FC - 1))
                last.then_inc(yp_ready, 1)

            take(0, 0, 0)

            def turn(i, first=False, last=False):
                for s in range(2):
                    n = 2 * i + s
                    if not last:
                        widen(n, s)
                    if not (first and s == 0) and not (last and s == 1):
                        turn_hidden(n - 1, 1 - s)
                    if not last and not (isinstance(i, int) and n + 1 >= NS):
                        take(n + 1, 1 - s, i + s)
                    if not first:
                        narrow(n - 2, s)

            turn(0, first=True)
            turn(1)
            with pe.Fori(2, NS // 2 - 1) as i:
                turn(i)
            turn(NS // 2 - 1)
            turn(NS // 2, last=True)


def build(nc, dram, phases=4):
    with ExitStack() as ctx:
        x = ctx.enter_context(nc.sbuf_tensor("x_res", [128, B, D], F32))
        cst = ctx.enter_context(nc.sbuf_tensor("cst", [128, C_END], F32))
        identb = ctx.enter_context(nc.sbuf_tensor("identb", [128, 128], BF16))
        st = {"x": x, "cst": cst, "identb": identb, "ctxT_dram": dram["ctxT"], "n_consts": 16}
        for name in ("consts_in", "x_in", "ident_ready", "zeroed", "x_out"):
            st[name] = ctx.enter_context(nc.semaphore(f"{name}_all"))
        zero = ctx.enter_context(nc.sbuf_tensor("zero", [128, SLOTS // 8 * D], F32))
        rows = [nc.dram_tensor(f"{a}_rows{l}", ((l * B + SLOTS) * 128, D), F32, kind="Internal").ap()
                for l in range(2) for a in ("in", "out")]
        st["n_zeroed"] = 16 * 2 * 8
        zero_set = ctx.enter_context(nc.semaphore("zero_set"))
        xd = dram["x"].rearrange("b t d -> t b d")
        with nc.Block() as block:
            @block.sync
            def _(sp):
                sp.dma_start(cst[:, :], dram["cst"]).then_inc(st["consts_in"], 16)
                sp.dma_start(x[:, 0:2, :], xd[:, 0:2, :]).then_inc(st["x_in"], 16)
                sp.dma_start(x[:, 2:B, :], xd[:, 2:B, :]).then_inc(st["x_in"], 16)

                sp.wait_ge(zero_set, 1)
                for layer in range(2):
                    flat = rows[2 * layer][layer * B * T:, :].rearrange("(p r) d -> p (r d)", p=128)
                    for c in range(8):
                        n = SLOTS // 8 * D
                        sp.dma_start(flat[:, c * n:(c + 1) * n], zero[:, :]).then_inc(st["zeroed"], 16)

            @block.gpsimd
            def _(pool):
                nc.gpsimd.memset(zero[:, :], 0.0).then_inc(zero_set, 1)

            @block.vector
            def _(dve):
                dve.wait_ge(st["consts_in"], 16)
                nc.vector.tensor_copy(identb[:, :], cst[:, C_ID:C_ID + 128]).then_inc(st["ident_ready"], 1)

        if phases >= 1:
            attention(nc, st, 0, {k: dram[f"a0_{k}"] for k in ("W", "cols", "bo", "bv", "am", "amT", "pad", "padT")})
        if phases >= 2:
            experts(nc, st, 0, {"Wg": dram["e0_Wg"], "W1": dram["e0_W1"], "W2": dram["e0_W2"], "Xs": rows[0], "Ys": rows[1]})
        if phases >= 3:
            attention(nc, st, 1, {k: dram[f"a1_{k}"] for k in ("W", "cols", "bo", "bv")})
        if phases >= 4:
            experts(nc, st, 1, {**{k: dram[f"e1_{k}"] for k in ("Wg", "W1", "W2", "B1", "B2", "gb")},
                                "Xs": rows[2], "Ys": rows[3]})
        with nc.Block() as block:
            @block.sync
            def _(sp):
                sp.dma_start(dram["out"].rearrange("b t d -> t b d"), x[:, :, :]).then_inc(st["x_out"], 16)
                sp.wait_ge(st["x_out"], 16)


def layout(v):
    a = {k: np.asarray(t) for k, t in v.items()}
    swap = np.arange(D).reshape(H, 2, DH // 2)[:, ::-1].reshape(D)
    out = {"x": a["x"], "cst": shape_constants()}
    out["ctxT"] = a["ctx_1024"].transpose(2, 0, 1).reshape(D, B * TK)
    q = "L0_xattn_"
    out["a0_W"] = np.stack([a[q + n].T for n in ("Wq", "Wk", "Wv", "Wo")], 1)
    out["a0_cols"] = np.stack([a[q + n] for n in ("bq", "bk", "bv", "bo")], 1)
    out["a0_bo"], out["a0_bv"] = a[q + "bo"], a[q + "bv"]
    mask, pad = a["mask_SxS2_bk1"], a["mask_BxS2_bf0"]
    out["a0_am"], out["a0_amT"], out["a0_pad"], out["a0_padT"] = mask, mask.T, pad.reshape(-1), pad.T
    q = "L1_xattn_"
    out["a1_W"] = np.stack([a[q + n + "_w"].T for n in "qkvo"] + [a[q + n + "_w"][swap].T for n in "qk"], 1)
    out["a1_cols"] = np.stack([a[q + n + "_b"] for n in "qkvo"] + [a[q + n + "_b"][swap] for n in "qk"], 1)
    out["a1_bo"], out["a1_bv"] = a[q + "o_b"], a[q + "v_b"]
    out["e0_Wg"] = a["L0_ffn_Wg"].T
    out["e0_W1"] = a["L0_ffn_W1"].transpose(1, 0, 2)
    out["e0_W2"] = a["L0_ffn_W2"].reshape(E0, F0 // 128, 128, D).transpose(2, 0, 1, 3)
    f = {k: np.concatenate([a["L1_ffn_" + k], a["L1_ffn_s" + k][None]]) for k in ("w1", "w3", "b1", "b3", "w2", "b2")}
    w2 = np.zeros((E1 + 1, 256, D), np.float32)
    w2[:, :F1] = f["w2"]
    out["e1_Wg"] = a["L1_ffn_gate_w"].T
    out["e1_W1"] = np.concatenate([f["w1"], f["w3"]], 2).transpose(1, 0, 2)
    out["e1_W2"] = w2.reshape(E1 + 1, 2, 128, D).transpose(2, 0, 1, 3)
    out["e1_B1"] = np.concatenate([f["b1"], f["b3"]], 1)
    out["e1_B2"] = f["b2"]
    out["e1_gb"] = a["L1_ffn_gate_b"]
    return {k: np.ascontiguousarray(t) for k, t in out.items()}


def kernel(**inputs):
    import concourse.bacc as bacc
    from concourse.bass_utils import run_bass_kernel_spmd

    nc = bacc.Bacc("TRN2", target_bir_lowering=False, num_devices=1)
    arrays = layout(inputs)
    dram = {k: nc.dram_tensor(f"in_{k}", t.shape, mybir.dt.from_np(t.dtype), kind="ExternalInput").ap()
            for k, t in arrays.items()}
    dram["out"] = nc.dram_tensor("out_x", (B, T, D), F32, kind="ExternalOutput").ap()
    build(nc, dram)
    r = run_bass_kernel_spmd(nc, [{f"in_{k}": t for k, t in arrays.items()}], core_ids=[0])
    return r.results[0]["out_x"]
```

```python
from contextlib import ExitStack

import numpy as np

import concourse.bass as bass
from concourse import mybir

F32 = mybir.dt.float32
BF16 = mybir.dt.bfloat16
U8 = mybir.dt.uint8
U32 = mybir.dt.uint32
ALU = mybir.AluOpType
ACT = mybir.ActivationFunctionType
AX = mybir.AxisListType

B, T, D = 32, 128, 128
TK = 77
H, DH = 16, 8
G, J = 4, 4
SCALE = DH ** -0.5
WINDOW = 64
EPS = 1e-5
NP = B // 2
GK = J * TK
VW = D + H
VM = 2448
MASKED = -1e30
E0, F0 = 8, 512
E1, F1 = 8, 176
E = E0
N = B * T
NB1 = (E1 + 1) * 2 * F1
NB = NB1 + (E1 + 1) * D
NBP = 120
SLOTS = 2 * N // 128 + E
PAST = SLOTS - 2 * N // 128
REGION = N + 128
SHARED = E * REGION + PAST * 128
RW = 132

C_ID, C_HM, C_GM, C_BAND, C_COS, C_SIN = 0, 128, 132, 136, 216, 344
C_HALF, C_EPS, C_BEFORE, C_BACK, C_SLOT, C_FIRST, C_E = 472, 476, 480, 608, 616, 688, 696
C_END = 704


def shape_constants():
    c = np.zeros((128, C_END), np.float32)
    p = np.arange(128)
    c[:, C_ID:C_ID + 128] = np.eye(128)
    c[p, C_HM + (p % 32) // DH] = 1.0
    c[p, C_GM + p // 32] = 1.0
    q, k = np.arange(T)[:, None], np.arange(TK)[None, :]
    c[:, C_BAND:C_BAND + TK] = np.where((k < q - WINDOW) | (k > q), MASKED, 0.0)
    half = DH // 2
    freqs = (np.float32(1.0) / np.float32(10000.0) ** (np.arange(half, dtype=np.float32) / np.float32(half)))
    ang = np.arange(T, dtype=np.float32)[None, :] * freqs.astype(np.float32)[p % half][:, None]
    c[:, C_COS:C_COS + T] = np.cos(ang)
    c[:, C_SIN:C_SIN + T] = np.sin(ang) * np.where(p % DH < half, -1.0, 1.0)[:, None]
    c[:, C_HALF:C_HALF + 4] = -0.5
    c[:, C_EPS:C_EPS + 4] = EPS
    c[:, C_BEFORE:C_BEFORE + 128] = p[:, None] < p[None, :]
    c[:, C_BACK:C_BACK + E] = E - np.arange(E)
    c[:, C_SLOT:C_SLOT + SLOTS] = np.arange(SLOTS)
    c[:, C_FIRST:C_FIRST + E] = np.arange(E) * REGION
    c[:, C_E:C_E + E] = np.arange(E)
    return c


class Steps:

    def __init__(self, sem):
        self.sem, self.base, self.n = sem, 0, 0

    def turn(self, done=None):
        if done is None:
            self.base, self.n = self.base + self.n, 0
        else:
            self.entry, self.per_turn = self.base + self.n, self.n
            self.base, self.n = self.entry + done * self.per_turn, 0

    def leave(self, count):
        assert self.n == self.per_turn
        self.base, self.n = self.entry + count * self.per_turn, 0

    def mark(self, ins):
        self.n += 1
        ins.then_inc(self.sem, 1)

    def wait(self, eng):
        eng.wait_ge(self.sem, self.base + self.n)

    def then(self, eng, ins):
        self.mark(ins)
        self.wait(eng)


def attention(nc, st, layer, w):
    rope = layer == 1
    copies = 3 if rope else 2
    with ExitStack() as ctx:
        def sb(name, shape, dt=F32):
            return ctx.enter_context(nc.sbuf_tensor(f"{name}_{layer}", shape, dt))

        def pb(name, shape, dt=F32):
            return ctx.enter_context(nc.psum_tensor(f"{name}_{layer}", shape, dt))

        def sem(name):
            return ctx.enter_context(nc.semaphore(f"{name}_{layer}"))

        x, cst, identb = st["x"], st["cst"], st["identb"]
        ident = cst[:, C_ID:C_ID + 128]
        names = ["q", "k", "v", "o"] + (["qr", "kr"] if rope else [])
        W = sb("W", [128, len(names), 128])
        cols = sb("cols", [128, len(names)])
        wt = {n: W[:, i, :] for i, n in enumerate(names)}
        bias = {n: cols[:, i:i + 1] for i, n in enumerate(names)}
        bo = sb("bo", [128, 128])
        bv = sb("bv", [128, 128])
        ctxT = sb("ctxT", [128, 2 * TK])
        stats = sb("stats", [128, 4, 6])
        mv = sb("mv", [128, 4, 2])
        rstd = sb("rstd", [128, 4])
        vare = sb("vare", [128, 4])
        xn = sb("xn", [128, 2, 128])
        xr = sb("xr", [128, 2, D])
        out_rows = sb("out_rows", [128, 2, copies, RW])
        xrT = sb("xrT", [128, 2, T])
        onesb = sb("onesb", [128, 128], BF16)
        beforeb = sb("beforeb", [128, 128], BF16)
        key = sb("key", [128, 2, E])
        pick = sb("pick", [128, 2, E])
        best = sb("best", [128, 2])
        mark = sb("mark", [128, 2])
        oh = sb("oh", [128, 2, 2, E])
        both = sb("both", [128, 2, E], BF16)
        rank = sb("rank", [128, 4, E])
        pos = sb("pos", [128, 2, E])
        carry = sb("carry", [128, 2, E])
        posk = sb("posk", [128, 2, 2, E])
        goes = sb("goes", [128, 2, copies], U32)
        posf = sb("posf", [128, 2, 2])
        posi = sb("posi", [128, 2, 2], U32)
        if rope:
            yc = sb("yc", [128, 2, 2, D])
            lg = sb("lg", [128, 2, E])
            shift = sb("shift", [128, 2, E])
            prob = sb("prob", [128, 2, E])
            total = sb("total", [128, 2])
            rtotal = sb("rtotal", [128, 2])
            gb = sb("gb", [128, E])
        else:
            top = sb("top", [128, 2, B])
        xnT = sb("xnT", [128, 2 * T])
        qexp = sb("qexp", [128, 2, G, T])
        kT = sb("kT", [128, 2 * TK])
        krT = sb("krT", [128, 2 * TK]) if rope else None
        kro = sb("kro", [128, 2, TK]) if rope else None
        kcos = sb("kcos", [128, 2, TK]) if rope else None
        ksin = sb("ksin", [128, 2, TK]) if rope else None
        qro = sb("qro", [128, 2, T]) if rope else None
        qcos = sb("qcos", [128, 2, T]) if rope else None
        qsin = sb("qsin", [128, 2, T]) if rope else None
        kexp = sb("kexp", [128, 2, J, TK])
        vs = sb("vs", [TK, 2, 128])
        vm = sb("vm", [TK, 2, VM])
        bias_qk = sb("bias_qk", [128, 2, TK], BF16)
        pr = sb("pr", [128, 2, H, TK])
        mx = sb("mx", [128, H])
        pT = sb("pT", [TK, G, J, T])
        rden = sb("rden", [128, H])
        an = sb("an", [128, 2, 128])
        aT = sb("aT", [128, 128])
        if not rope:
            am8 = sb("am8", [128, TK], U8)
            negA = sb("negA", [128, TK])
            amT8 = sb("amT8", [TK, 128], U8)
            keepA = sb("keepA", [TK, 128])
            pad8 = sb("pad8", [128, B * TK], U8)
            negP = sb("negP", [128, B * TK])
            padT8 = sb("padT8", [TK, B], U8)
            keepP = sb("keepP", [TK, B])
            some = sb("some", [128, B])
            isome = sb("isome", [128, B])
            nz = sb("nz", [128, B])

        S = pb("S", [128, G, 512])
        ptp = [pb(f"ptp{i}", [TK, J, T]) for i in range(2)]
        M0 = pb("M0", [128, 512])
        M1 = pb("M1", [128, 512])
        O, anTp, rankp = M0[:, 0:VW], M0[:, VW:VW + 128], M0[:, 384:384 + 4 * E]
        Y, lgp, xrTp = M1[:, 0:128], M1[:, 128:128 + 2 * E], M1[:, 0:256]
        xTp, Qp, Qrp = M1[:, 0:256], M1[:, 256:512], M1[:, 0:256]
        Kp, Krp = S[:, 0, GK:GK + 2 * TK], S[:, 1, GK:GK + 2 * TK]
        Vp = [S[0:TK, 2, GK:GK + 128], S[0:TK, 3, GK:GK + 128]]

        consts_in = sem("consts_in")
        ctx_in = sem("ctx_in")
        vm_set = sem("vm_set")
        masks_set = sem("masks_set")
        counts_ready = sem("counts_ready")
        mv_ready = sem("mv_ready")
        rstd_ready = sem("rstd_ready")
        xn_ready = sem("xn_ready")
        xT_ready = sem("xT_ready")
        xT_copied = sem("xT_copied")
        q_ready = sem("q_ready")
        qexp_ready = sem("qexp_ready")
        kv_ready = sem("kv_ready")
        kv_copied = sem("kv_copied")
        kexp_ready = sem("kexp_ready")
        vm_ready = sem("vm_ready")
        s_ready = sem("s_ready")
        sub_done = sem("sub_done")
        exp_done = sem("exp_done")
        pt_ready = sem("pt_ready")
        pt_copied = sem("pt_copied")
        pv_done = sem("pv_done")
        norm_done = sem("norm_done")
        anT_ready = sem("anT_ready")
        aT_copied = sem("aT_copied")
        y_ready = sem("y_ready")
        bo_added = sem("bo_added")
        res_done = sem("res_done")
        dve_step = sem("dve_step")
        pool_step = sem("pool_step")
        mv_set = sem("mv_set")
        idx_set = sem("idx_set")
        xr_ready = sem("xr_ready")
        spread_done = sem("spread_done")
        xrT_ready = sem("xrT_ready")
        xrT_copied = sem("xrT_copied")
        lg_ready = sem("lg_ready")
        lg_read = sem("lg_read")
        shift_ready = sem("shift_ready")
        prob_ready = sem("prob_ready")
        both_ready = sem("both_ready")
        rank_ready = sem("rank_ready")
        rank_copied = sem("rank_copied")
        pos_ready = sem("pos_ready")
        scattered = sem("scattered")
        filled = sem("filled")
        if rope:
            shared_out = sem("shared_out")
            results_in = sem("results_in")
            results_used = sem("results_used")
        maps_done = sem("maps_done")

        n_const = 16 * (5 if rope else 4 + 4)
        rows = w["rows"]

        FULL = 3

        def turns(body, eng, steps=None):
            for i in range(FULL + 1):
                if steps:
                    steps.turn()
                body(i)
            with eng.Fori(FULL + 1, NP - 2) as i:
                if steps:
                    steps.turn(i - (FULL + 1))
                body(i)
            if steps:
                steps.leave(NP - 2 - (FULL + 1))
            for i in range(NP - 2, NP + 3):
                if steps:
                    steps.turn()
                body(i)

        def live(p):
            return not isinstance(p, int) or 0 <= p < NP

        def wait(eng, s, value):
            if not isinstance(value, int) or value > 0:
                eng.wait_ge(s, value)

        block = ctx.enter_context(nc.Block())

        @block.sync
        def _(sp):
            def load_ctx(j):
                wait(sp, kv_ready, j)
                sp.dma_start(ctxT[:, :], st["ctxT_dram"][:, bass.ds(j * (2 * TK), 2 * TK)]).then_inc(ctx_in, 16)

            def load_results(j):
                wait(sp, results_used, j)
                for k in range(2):
                    sp.dma_start(yc[:, k, :, :], w["results"][k * N:(k + 1) * N, :].rearrange("(b p) d -> p b d", p=128)
                                 [:, bass.ds(2 * j, 2), :]).then_inc(results_in, 16)

            def store_shared(p):
                sp.wait_ge(spread_done, p + 1)
                sp.wait_ge(idx_set, p + 1)
                sp.dma_start(rows[bass.ds(p * 256 + SHARED, 256), :].rearrange("(s p) d -> p s d", p=128),
                             out_rows[:, :, 2, :]).then_inc(shared_out, 16)

            sp.dma_start(W[:, :, :], w["W"]).then_inc(consts_in, 16)
            sp.dma_start(cols[:, :], w["cols"]).then_inc(consts_in, 16)
            sp.dma_start(bo[:, :], w["bo"].partition_broadcast(128)).then_inc(consts_in, 16)
            sp.dma_start(bv[:, :], w["bv"].partition_broadcast(128)).then_inc(consts_in, 16)
            load_ctx(0)
            if rope:
                sp.dma_start(gb[:, :], w["gb"].partition_broadcast(128)).then_inc(consts_in, 16)
                load_results(0)
                load_results(1)
            else:
                sp.dma_start(am8[:, :], w["am"]).then_inc(consts_in, 16)
                sp.dma_start(amT8[:, :], w["amT"]).then_inc(consts_in, 16)
                sp.dma_start(pad8[:, :], w["pad"].partition_broadcast(128)).then_inc(consts_in, 16)
                sp.dma_start(padT8[:, :], w["padT"]).then_inc(consts_in, 16)
                for b0, b1 in ((2, 8), (8, B)):
                    sp.dma_start(st["x"][:, b0:b1, :], st["x_dram"][:, b0:b1, :]).then_inc(st["x_in"], 16)
            load_ctx(1)
            for dst, src in w["prefetch"]:
                sp.dma_start(dst, src).then_inc(st["weights_in"], 16)
            if not rope:
                sp.wait_ge(st["bias_split"], 1)
                sp.dma_start(st["parts_dram"].rearrange("k (p n) -> p k n", p=NBP), st["bias_parts"][:, :, :])\
                    .then_inc(st["bias_out"], 16)
                sp.wait_ge(st["bias_out"], 16)
                sp.dma_start(st["parts"][:, :], st["parts_dram"]).then_inc(st["bias_in"], 16)

            def turn(i):
                if live(i) and live(i + 2):
                    if rope:
                        load_results(i + 2)
                    load_ctx(i + 2)
                if rope and live(i - 3):
                    store_shared(i - 3)

            turns(turn, sp)
            if rope:
                sp.wait_ge(shared_out, 16 * NP)
            sp.wait_ge(st["maps_ready"], layer + 1)
            for e in range(E):
                count = 128 * (1 if e < E - 1 else 1 + PAST)
                first = sp.value_load(st["fill"][0:1, e:e + 1], min_val=0, max_val=(e + 1) * REGION - 128)
                sp.dma_start(rows[bass.ds(first, count), :], st["filling"][e * 128:e * 128 + count, :]).then_inc(filled, 16)
            sp.wait_ge(scattered, 64 * NP)
            sp.wait_ge(filled, 16 * E)

        @block.gpsimd
        def _(pool):
            steps = Steps(pool_step)
            steps.then(pool, nc.gpsimd.memset(vm[:, :, :], 0.0))
            for s in range(2):
                last = nc.gpsimd.memset(vm[:, s, D:D + H * (VW + 1)].rearrange("k (h c) -> k h c", h=H)[:, :, 0:1], 1.0)
            last.then_inc(vm_set, 1)
            pool.wait_ge(vm_set, 1)
            nc.gpsimd.memset(mv[:, :, :], 1.0).then_inc(mv_set, 1)
            pool.wait_ge(mv_set, 1)
            nc.gpsimd.memset(out_rows[:, :, :, :], 0.0).then_inc(mv_set, 1)
            nc.gpsimd.memset(onesb[:, :], 1.0).then_inc(mv_set, 1)
            pool.wait_ge(consts_in, n_const)
            pool.wait_ge(st["consts_in"], st["n_consts"])
            if rope:
                for s in range(2):
                    last = nc.gpsimd.tensor_copy(bias_qk[:, s, :], cst[:, C_BAND:C_BAND + TK])
                last.then_inc(masks_set, 1)

            def norms(i):
                pool.wait_ge(mv_ready, i + 2)
                steps.then(pool, nc.gpsimd.tensor_tensor(vare[:, :], mv[:, :, 1], cst[:, C_EPS:C_EPS + 4], ALU.add))
                nc.gpsimd.tensor_tensor(rstd[:, :], vare[:, :], cst[:, C_HALF:C_HALF + 4], ALU.pow).then_inc(rstd_ready, 1)

            def scatter(p):
                pool.wait_ge(idx_set, p + 1)
                pool.wait_ge(spread_done, p + 1)
                pool.wait_ge(pos_ready, p + 1)
                steps.mark(nc.gpsimd.tensor_tensor(
                    goes[:, :, :], goes[:, :, :],
                    st["onward"][:, 0:2 * copies].rearrange("p (s c) -> p s c", s=2), ALU.add))
                for s in range(2):
                    for k in range(2):
                        nc.gpsimd.indirect_dma_start(rows[:, :], bass.IndirectOffsetOnAxis(posi[:, k, s:s + 1], 0),
                                                     out_rows[:, s, k, :], None).then_inc(scattered, 16)

            def keys(j):
                pool.wait_ge(kv_copied, j + 1)
                k2 = kT[:, :].rearrange("p (s k) -> p s k", s=2)
                if rope:
                    kr2 = krT[:, :].rearrange("p (s k) -> p s k", s=2)
                    tab = [cst[:, c:c + TK].unsqueeze(1).broadcast_to([128, 2, TK]) for c in (C_COS, C_SIN)]
                    steps.mark(nc.gpsimd.tensor_tensor(kcos[:, :, :], k2, tab[0], ALU.mult))
                    steps.then(pool, nc.gpsimd.tensor_tensor(ksin[:, :, :], kr2, tab[1], ALU.mult))
                    steps.then(pool, nc.gpsimd.tensor_tensor(kro[:, :, :], kcos[:, :, :], ksin[:, :, :], ALU.add))
                    k2 = kro[:, :, :]
                for s in range(2):
                    n = j * 2 + s
                    wait(pool, s_ready, n - 1)
                    if not rope:
                        pool.wait_ge(masks_set, 1)
                        steps.mark(nc.gpsimd.tensor_tensor(
                            bias_qk[:, s, :], negA[:, :], negP[:, bass.ds(n * TK, TK)], ALU.add))
                    nc.gpsimd.tensor_tensor(
                        kexp[:, s, :, :], k2[:, s, :].unsqueeze(1).broadcast_to([128, J, TK]),
                        cst[:, C_HM:C_HM + J].unsqueeze(2).broadcast_to([128, J, TK]), ALU.mult).then_inc(kexp_ready, 1)

            def index(p):
                wait(pool, scattered, 64 * p)
                if rope:
                    wait(pool, shared_out, 16 * p)
                steps.wait(pool)
                nc.gpsimd.tensor_tensor(out_rows[:, :, :, D:D + 1].bitcast(U32), goes[:, :, :].unsqueeze(3),
                                        st["zero"][:, 0:2 * copies].rearrange("p (s c) -> p s c", s=2).unsqueeze(3),
                                        ALU.add).then_inc(idx_set, 1)

            def padded_values(j, s):
                n = j * 2 + s
                pool.wait_ge(kv_copied, j + 1)
                wait(pool, pv_done, n - 1)
                own = vm[:, s, 0:H * (VW + DH)].rearrange("k (h c) -> k h c", h=H)[:, :, 0:DH]
                nc.gpsimd.tensor_tensor(own, vs[:, s, :].rearrange("k (h d) -> k h d", d=DH),
                                        bv[0:TK, :].rearrange("k (h d) -> k h d", d=DH), ALU.add).then_inc(vm_ready, 1)

            def output_bias(j):
                pool.wait_ge(xn_ready, 2 * j + 2)
                for s in range(2):
                    xb = x[:, bass.ds(j * 2 + s, 1), :].rearrange("p a d -> p (a d)")
                    nc.gpsimd.tensor_tensor(xb, xb, bo[:, :], ALU.add).then_inc(bo_added, 1)

            steps.then(pool, nc.gpsimd.tensor_copy(goes[:, :, :], st["dest"][:, :, 0:copies]))
            norms(-1)
            keys(0)
            output_bias(0)

            def turn(i):
                if live(i + 1) or live(i - 2):
                    norms(i)
                if live(i):
                    padded_values(i, 0)
                    padded_values(i, 1)
                if live(i - 3):
                    index(i - 3)
                if live(i + 1):
                    output_bias(i + 1)
                    keys(i + 1)
                if live(i - 3):
                    scatter(i - 3)

            turns(turn, pool, steps)

        @block.scalar
        def _(act):
            act.wait_ge(consts_in, n_const)

            def x_copy(j):
                act.wait_ge(xT_ready, j + 1)
                nc.scalar.activation(xnT[:, :], xTp, ACT.Copy).then_inc(xT_copied, 1)

            def kv_copy(j):
                act.wait_ge(kv_ready, j + 1)
                wait(act, vm_ready, 2 * j)
                nc.scalar.activation(kT[:, :], Kp, ACT.Identity, bias=bias["k"])
                if rope:
                    nc.scalar.activation(krT[:, :], Krp, ACT.Identity, bias=bias["kr"])
                for s in range(2):
                    last = nc.scalar.activation(vs[:, s, :], Vp[s], ACT.Copy)
                last.then_inc(kv_copied, 1)

            def pt_copy(n, r):
                act.wait_ge(pt_ready, n * G + (r + 1))
                nc.scalar.activation(pT[:, r, :, :], ptp[r % 2][:, :, :], ACT.Copy).then_inc(pt_copied, 1)

            def exps(n, s):
                act.wait_ge(sub_done, n + 1)
                p = pr[:, s, :, :].rearrange("p h k -> p (h k)")
                nc.scalar.activation(p, p, ACT.Exp, scale=SCALE).then_inc(exp_done, 1)

            def at_copy(n):
                act.wait_ge(anT_ready, n + 1)
                nc.scalar.activation(aT[:, :], anTp, ACT.Copy).then_inc(aT_copied, 1)

            def rank_copy(p):
                act.wait_ge(rank_ready, p + 1)
                nc.scalar.activation(rank[:, :, :], rankp.rearrange("p (a e) -> p a e", e=E), ACT.Copy).then_inc(rank_copied, 1)

            def xr_copy(p):
                act.wait_ge(xrT_ready, p + 1)
                nc.scalar.activation(xrT[:, :, :], xrTp.rearrange("p (s t) -> p s t", s=2), ACT.Copy).then_inc(xrT_copied, 1)

            def spread(p):
                act.wait_ge(xr_ready, p + 1)
                wait(act, scattered, 64 * p)
                if rope:
                    wait(act, shared_out, 16 * p)
                nc.scalar.activation(out_rows[:, :, :, 0:D], xr[:, :, :].unsqueeze(2).broadcast_to([128, 2, copies, D]),
                                     ACT.Copy).then_inc(spread_done, 1)

            def router_exp(p):
                act.wait_ge(shift_ready, p + 1)
                nc.scalar.activation(prob[:, :, :], shift[:, :, :], ACT.Exp).then_inc(prob_ready, 1)

            x_copy(0)
            kv_copy(0)

            def turn(i):
                a, b = 2 * i, 2 * i + 1
                if live(i - 1):
                    at_copy(a - 2)
                if rope and live(i - 3):
                    router_exp(i - 3)
                if live(i - 1):
                    for r in range(G):
                        pt_copy(b - 2, r)
                if live(i):
                    exps(a, 0)
                if live(i - 3):
                    spread(i - 3)
                if live(i - 1):
                    at_copy(b - 2)
                if live(i - 3):
                    rank_copy(i - 3)
                if live(i + 1):
                    x_copy(i + 1)
                if live(i):
                    for r in range(3):
                        pt_copy(a, r)
                if live(i - 2):
                    xr_copy(i - 2)
                if live(i + 1):
                    kv_copy(i + 1)
                if live(i):
                    pt_copy(a, 3)
                    exps(b, 1)

            turns(turn, act)
            if not rope:
                act.wait_ge(shift_ready, 1)
                nc.scalar.activation(top[:, 1, :], top[:, 0, :], ACT.Exp).then_inc(prob_ready, 1)

        @block.vector
        def _(dve):
            steps = Steps(dve_step)
            dve.wait_ge(consts_in, n_const)
            dve.wait_ge(st["consts_in"], st["n_consts"])
            if not rope:
                nc.vector.tensor_scalar(negA[:, :], am8[:, :], MASKED, None, ALU.mult)
                nc.vector.tensor_scalar(negP[:, :], pad8[:, :], MASKED, None, ALU.mult).then_inc(masks_set, 1)
                nc.vector.tensor_scalar(keepA[:, :], amT8[:, :], -1.0, 1.0, ALU.mult, ALU.add)
                nc.vector.tensor_scalar(keepP[:, :], padT8[:, :], -1.0, 1.0, ALU.mult, ALU.add).then_inc(masks_set, 1)
                dve.wait_ge(counts_ready, 1)
                steps.then(dve, nc.vector.tensor_scalar(some[:, :], Y[:, 0:B], 1.0, None, ALU.min))
                steps.then(dve, nc.vector.reciprocal(isome[:, :], some[:, :]))
                steps.then(dve, nc.vector.tensor_tensor(nz[:, :], some[:, :], isome[:, :], ALU.mult))

            def row(n):
                return x[:, bass.ds(n, 1), :].rearrange("p a d -> p (a d)")

            def take_results(j):
                dve.wait_ge(results_in, 32 * j + 32)
                for k in range(2):
                    for s in range(2):
                        n = j * 2 + s
                        last = nc.vector.scalar_tensor_tensor(row(n), yc[:, k, s, :], st["wsel"][0][:, k, bass.ds(n, 1)], row(n),
                                                              ALU.mult, ALU.add)
                        if k == 0:
                            steps.mark(last)
                    if k == 0:
                        steps.wait(dve)
                steps.then(dve, last)
                dve.sem_inc(results_used, 1)

            def norm_stats(p, at):
                for s in range(2):
                    last = nc.vector.bn_stats(stats[:, at + s, :], row(p * 2 + s))
                steps.mark(last)

            def norm_mean(at):
                for s in range(2):
                    last = nc.vector.bn_aggr(mv[:, at + s, :], stats[:, at + s, :])
                return last

            def norm_x(j):
                dve.wait_ge(rstd_ready, j + 1)
                for s in range(2):
                    nc.vector.tensor_scalar(xn[:, s, :], row(j * 2 + s), mv[:, s, 0:1], rstd[:, s:s + 1],
                                            ALU.subtract, ALU.mult).then_inc(xn_ready, 1)

            def router_x(p):
                dve.wait_ge(rstd_ready, p + 4)
                wait(dve, spread_done, p)
                wait(dve, xrT_ready, p)
                for s in range(2):
                    last = nc.vector.tensor_scalar(xr[:, s, :], row(p * 2 + s), mv[:, 2 + s, 0:1], rstd[:, 2 + s:3 + s],
                                                   ALU.subtract, ALU.mult)
                last.then_inc(xr_ready, 1)

            V = nc.vector
            back = cst[:, C_BACK:C_BACK + E]

            def over_e(a):
                return a.unsqueeze(2).broadcast_to([128, 2, E])

            def over_s(a):
                return a.unsqueeze(1).broadcast_to([128, 2, E])

            def do(ins):
                steps.then(dve, ins)

            def take_logits(p):
                dve.wait_ge(lg_ready, p + 1)
                logits = lgp.rearrange("p (s e) -> p s e", s=2)
                if rope:
                    V.tensor_copy(lg[:, :, :], logits).then_inc(lg_read, 1)
                    dve.wait_ge(lg_read, p + 1)
                    do(V.tensor_reduce(best[:, :], lg[:, :, :], AX.X, ALU.max))
                    V.tensor_tensor(shift[:, :, :], lg[:, :, :], over_e(best[:, :]), ALU.subtract).then_inc(shift_ready, 1)
                else:
                    V.tensor_scalar(key[:, :, :], logits, -1e38, None, ALU.max).then_inc(lg_read, 1)

            def choose(p):
                if rope:
                    dve.wait_ge(prob_ready, p + 1)
                    do(V.tensor_reduce(total[:, :], prob[:, :, :], AX.X, ALU.add))
                    do(V.reciprocal(rtotal[:, :], total[:, :]))
                    do(V.tensor_tensor(prob[:, :, :], prob[:, :, :], over_e(rtotal[:, :]), ALU.mult))
                    do(V.tensor_tensor(key[:, :, :], prob[:, :, :], over_s(gb[:, :]), ALU.add))
                    do(V.tensor_scalar(key[:, :, :], key[:, :, :], -1e38, None, ALU.max))
                else:
                    dve.wait_ge(lg_read, p + 1)
                for k in range(2):
                    do(V.tensor_reduce(best[:, :], key[:, :, :], AX.X, ALU.max))
                    if not rope:
                        steps.mark(V.tensor_copy(top[:, k, bass.ds(2 * p, 2)], best[:, :]))
                    for s in range(2):
                        last = V.scalar_tensor_tensor(pick[:, s, :], key[:, s, :], best[:, s:s + 1], back,
                                                      ALU.is_equal, ALU.mult)
                    do(last)
                    do(V.tensor_reduce(mark[:, :], pick[:, :, :], AX.X, ALU.max))
                    do(V.tensor_tensor(oh[:, k, :, :], over_s(back), over_e(mark[:, :]), ALU.is_equal))
                    if k == 0:
                        do(V.scalar_tensor_tensor(key[:, :, :], oh[:, 0, :, :], -2e38, key[:, :, :], ALU.mult, ALU.add))
                V.tensor_tensor(both[:, :, :], oh[:, 0, :, :], oh[:, 1, :, :], ALU.add).then_inc(both_ready, 1)
                if rope:
                    do(V.tensor_tensor(posk[:, :, :, :], oh[:, :, :, :], prob[:, :, :].unsqueeze(1).broadcast_to([128, 2, 2, E]),
                                       ALU.mult))
                    do(V.tensor_reduce(st["wsel"][1][:, :, bass.ds(2 * p, 2)], posk[:, :, :, :], AX.X, ALU.add))

            def place(p):
                dve.wait_ge(rank_copied, p + 1)
                steps.mark(V.tensor_tensor(pos[:, :, :], rank[:, 0:2, :], over_s(carry[:, 0, :]), ALU.add))
                do(V.tensor_tensor(carry[:, 1, :], carry[:, 0, :], rank[:, 2, :], ALU.add))
                steps.mark(V.tensor_tensor(carry[:, 0, :], carry[:, 1, :], rank[:, 3, :], ALU.add))
                do(V.tensor_tensor(posk[:, :, :, :], oh[:, :, :, :], pos[:, :, :].unsqueeze(1).broadcast_to([128, 2, 2, E]),
                                   ALU.mult))
                do(V.tensor_reduce(posf[:, :, :], posk[:, :, :, :], AX.X, ALU.add))
                V.tensor_copy(posi[:, :, :], posf[:, :, :]).then_inc(pos_ready, 1)

            def q_expand(j):
                dve.wait_ge(q_ready, j + 1)
                wait(dve, s_ready, 2 * j)
                gm = cst[:, C_GM:C_GM + G].unsqueeze(2).broadcast_to([128, G, T])
                q2 = Qp.rearrange("p (s q) -> p s q", s=2)
                if rope:
                    tab = [cst[:, c:c + T].unsqueeze(1).broadcast_to([128, 2, T]) for c in (C_COS, C_SIN)]
                    steps.then(dve, nc.vector.scalar_tensor_tensor(
                        qcos[:, :, :], q2, bias["q"], tab[0], ALU.add, ALU.mult))
                    steps.then(dve, nc.vector.scalar_tensor_tensor(
                        qsin[:, :, :], Qrp.rearrange("p (s q) -> p s q", s=2), bias["qr"], tab[1], ALU.add, ALU.mult))
                    steps.then(dve, nc.vector.tensor_tensor(qro[:, :, :], qcos[:, :, :], qsin[:, :, :], ALU.add))
                for s in range(2):
                    if rope:
                        last = nc.vector.tensor_tensor(
                            qexp[:, s, :, :], qro[:, s, :].unsqueeze(1).broadcast_to([128, G, T]), gm, ALU.mult)
                    else:
                        last = nc.vector.scalar_tensor_tensor(
                            qexp[:, s, :, :], q2[:, s, :].unsqueeze(1).broadcast_to([128, G, T]), bias["q"], gm,
                            ALU.add, ALU.mult)
                last.then_inc(qexp_ready, 1)

            def softmax_shift(n, s):
                dve.wait_ge(s_ready, n + 1)
                sc = S[:, :, 0:GK].rearrange("p g (j k) -> p g j k", k=TK)
                steps.then(dve, nc.vector.tensor_reduce(
                    mx[:, :].rearrange("p (g j) -> p g j", g=G), sc, AX.X, ALU.max))
                wait(dve, pv_done, n - 1)
                nc.vector.tensor_tensor(
                    pr[:, s, :, :].rearrange("p (g j) k -> p g j k", g=G), sc,
                    mx[:, :].rearrange("p (g j) -> p g j", g=G).unsqueeze(3).broadcast_to([128, G, J, TK]),
                    ALU.subtract).then_inc(sub_done, 1)

            def normalise(n, s):
                dve.wait_ge(pv_done, n + 1)
                steps.then(dve, nc.vector.reciprocal(rden[:, :], O[:, D:VW]))
                nc.vector.scalar_tensor_tensor(
                    an[:, s, :].rearrange("p (h d) -> p h d", d=DH), O[:, 0:D].rearrange("p (h d) -> p h d", d=DH),
                    1.0 if rope else nz[:, bass.ds(n, 1)], rden[:, :].unsqueeze(2).broadcast_to([128, H, DH]),
                    ALU.mult, ALU.mult).then_inc(norm_done, 1)

            def residual(n):
                dve.wait_ge(y_ready, n + 1)
                dve.wait_ge(bo_added, n + 1)
                xb = x[:, bass.ds(n, 1), :].rearrange("p a d -> p (a d)")
                nc.vector.tensor_tensor(xb, xb, Y, ALU.add).then_inc(res_done, 1)

            if not rope:
                bias1, part, rest = st["bias"], st["bias_parts"], st["bias_rest"]
                do(V.tensor_copy(part[:, 0, :], bias1[:, :]))
                do(V.tensor_tensor(rest[:, 0, :], bias1[:, :], part[:, 0, :], ALU.subtract))
                do(V.tensor_copy(part[:, 1, :], rest[:, 0, :]))
                do(V.tensor_tensor(rest[:, 1, :], rest[:, 0, :], part[:, 1, :], ALU.subtract))
                V.tensor_copy(part[:, 2, :], rest[:, 1, :]).then_inc(st["bias_split"], 1)
            steps.mark(V.tensor_copy(beforeb[:, :], cst[:, C_BEFORE:C_BEFORE + 128]))
            steps.mark(V.tensor_copy(carry[:, 0, :], cst[:, C_FIRST:C_FIRST + E]))
            dve.wait_ge(mv_set, 3)
            if rope:
                take_results(0)
            else:
                dve.wait_ge(st["x_in"], 16)
            norm_stats(0, 0)
            steps.wait(dve)
            norm_mean(0).then_inc(mv_ready, 1)
            norm_x(0)
            if not rope:
                dve.wait_ge(st["x_in"], 48)
            q_expand(0)

            def turn(i):
                a, b = 2 * i, 2 * i + 1
                if live(i + 1):
                    if rope:
                        take_results(i + 1)
                    norm_stats(i + 1, 0)
                if live(i - 2):
                    dve.wait_ge(res_done, 2 * i - 2)
                    norm_stats(i - 2, 2)
                if live(i):
                    softmax_shift(a, 0)
                else:
                    steps.wait(dve)
                last = None
                if live(i + 1):
                    last = norm_mean(0)
                if live(i - 2):
                    last = norm_mean(2)
                if last:
                    last.then_inc(mv_ready, 1)
                if live(i - 3):
                    choose(i - 3)
                if live(i + 1):
                    norm_x(i + 1)
                if live(i - 1):
                    residual(a - 2)
                    normalise(b - 2, 1)
                if live(i):
                    softmax_shift(b, 1)
                if live(i - 1):
                    residual(b - 2)
                if live(i - 2):
                    router_x(i - 2)
                if live(i + 1):
                    q_expand(i + 1)
                if live(i - 3):
                    place(i - 3)
                if live(i):
                    normalise(a, 0)
                if live(i - 2):
                    take_logits(i - 2)

            turns(turn, dve, steps)
            wsel = st["wsel"][layer]
            steps.turn()
            steps.wait(dve)
            if not rope:
                do(V.tensor_tensor(top[:, 0, :], top[:, 1, :], top[:, 0, :], ALU.subtract))
                dve.sem_inc(shift_ready, 1)
                dve.wait_ge(prob_ready, 1)
                do(V.tensor_scalar(top[:, 0, :], top[:, 1, :], 1.0, None, ALU.add))
                do(V.reciprocal(wsel[:, 0, :], top[:, 0, :]))
                do(V.tensor_tensor(wsel[:, 1, :], top[:, 1, :], wsel[:, 0, :], ALU.mult))
            fill, tmap, cu, big = st["fill"], st["tiles"], st["tiles_u"], st["big"]
            first = cst[:, C_FIRST:C_FIRST + E]
            do(V.tensor_copy(fill[:, :], carry[:, 0, :]))
            do(V.tensor_tensor(tmap[:, 0, :], carry[:, 0, :], first, ALU.subtract))
            do(V.tensor_scalar(cu[:, 0, :], tmap[:, 0, :], 127.0, None, ALU.add))
            do(V.tensor_scalar(cu[:, 1, :], cu[:, 0, :], 7, None, ALU.logical_shift_right))
            do(V.tensor_copy(tmap[:, 1, :], cu[:, 1, :]))
            do(V.tensor_tensor_scan(tmap[:, 2, :], st["one"][:, :], tmap[:, 1, :], 0.0, ALU.mult, ALU.add))
            do(V.tensor_tensor(tmap[:, 3, :], tmap[:, 2, :], tmap[:, 1, :], ALU.subtract))
            dve.sem_inc(st["maps_ready"], 1)

            def by_slot(a):
                return a.unsqueeze(2).broadcast_to([128, SLOTS, E])

            def by_expert(a):
                return a.unsqueeze(1).broadcast_to([128, SLOTS, E])

            slot = cst[:, C_SLOT:C_SLOT + SLOTS]
            slot_e, slot_row = st["slot_f"][:, 0, :], st["slot_f"][:, 1, :]
            sh = B if rope else 0
            do(V.tensor_tensor(big[:, 0, :, :], by_slot(slot), by_expert(tmap[:, 2, :]), ALU.is_ge))
            do(V.tensor_reduce(slot_e, big[:, 0, :, :], AX.X, ALU.add))
            do(V.tensor_scalar(slot_e, slot_e, float(E - 1), None, ALU.min))
            steps.mark(V.tensor_copy(st["emap"][:, sh:sh + SLOTS], slot_e))
            do(V.tensor_tensor(big[:, 0, :, :], by_slot(slot), by_expert(tmap[:, 3, :]), ALU.subtract))
            do(V.tensor_scalar(big[:, 1, :, :], big[:, 0, :, :], 128.0, None, ALU.mult))
            do(V.tensor_tensor(big[:, 1, :, :], big[:, 1, :, :], by_expert(first), ALU.add))
            do(V.tensor_tensor(big[:, 0, :, :], by_slot(slot_e), by_expert(cst[:, C_E:C_E + E]), ALU.is_equal))
            do(V.tensor_tensor(big[:, 1, :, :], big[:, 0, :, :], big[:, 1, :, :], ALU.mult))
            do(V.tensor_reduce(slot_row, big[:, 1, :, :], AX.X, ALU.add))
            V.tensor_copy(st["rowmap"][:, sh:sh + SLOTS], slot_row).then_inc(maps_done, 1)
            dve.wait_ge(maps_done, 1)

        @block.tensor
        def _(pe):
            pe.wait_ge(consts_in, n_const)
            pe.wait_ge(st["consts_in"], st["n_consts"])
            if not rope:
                pe.wait_ge(masks_set, 2)
                nc.tensor.matmul(Y[:, 0:B], keepA[:, :], keepP[:, :], start=True, stop=True).then_inc(counts_ready, 1)
            else:
                pe.wait_ge(masks_set, 1)
            pe.wait_ge(st["ident_ready"], 1)

            def front_x(j):
                pe.wait_ge(xn_ready, 2 * j + 2)
                wait(pe, res_done, 2 * j - 3)
                for s in range(2):
                    last = nc.tensor.transpose(xTp[:, s * T:(s + 1) * T], xn[:, s, :], ident)
                last.then_inc(xT_ready, 1)

            def front_qkv(j, p):
                if live(j):
                    pe.wait_ge(xT_copied, j + 1)
                if live(p):
                    pe.wait_ge(xr_ready, p + 1)
                    wait(pe, lg_read, p)
                    pe.wait_ge(res_done, 2 * j - 2 if live(j - 2) else B)
                    for s in range(2):
                        last = nc.tensor.transpose(xrTp[:, s * T:(s + 1) * T], xr[:, s, :], ident)
                    last.then_inc(xrT_ready, 1)
                if live(j):
                    pe.wait_ge(ctx_in, 16 * j + 16)
                    wait(pe, sub_done, 2 * j)
                    nc.tensor.matmul(Kp, wt["k"], ctxT[:, :], start=True, stop=True)
                    if rope:
                        nc.tensor.matmul(Krp, wt["kr"], ctxT[:, :], start=True, stop=True)
                    for s in range(2):
                        last = nc.tensor.matmul(Vp[s], ctxT[:, s * TK:(s + 1) * TK], wt["v"], start=True, stop=True)
                    last.then_inc(kv_ready, 1)
                if live(p):
                    pe.wait_ge(xrT_copied, p + 1)
                elif live(j - 2):
                    pe.wait_ge(res_done, 2 * j - 2)
                if live(j):
                    last = nc.tensor.matmul(Qp, wt["q"], xnT[:, :], start=True, stop=True)
                    if rope:
                        last = nc.tensor.matmul(Qrp, wt["qr"], xnT[:, :], start=True, stop=True)
                    last.then_inc(q_ready, 1)

            def router_logits(p, q_pair):
                pe.wait_ge(xrT_copied, p + 1)
                wait(pe, qexp_ready, q_pair)
                for s in range(2):
                    last = nc.tensor.matmul(lgp[:, s * E:(s + 1) * E], xrT[:, s, :], st["Wg"][layer][:, :], start=True, stop=True)
                last.then_inc(lg_ready, 1)

            def ranks(p, i):
                pe.wait_ge(both_ready, p + 1)
                pe.wait_ge(norm_done, 2 * i if live(i - 1) else B)
                pe.wait_ge(aT_copied, 2 * i - 1 if live(i - 1) else B)
                wait(pe, rank_copied, p)
                nc.tensor.matmul(rankp[:, 0:2 * E], beforeb[:, :], both[:, :, :], start=True, stop=False)
                nc.tensor.matmul(rankp[:, E:2 * E], onesb[:, :], both[:, 0, :], start=False, stop=True)
                nc.tensor.matmul(rankp[:, 2 * E:4 * E], onesb[:, :], both[:, :, :], start=True, stop=True).then_inc(rank_ready, 1)

            def scores(n, s, i):
                pe.wait_ge(qexp_ready, i + 1)
                pe.wait_ge(kexp_ready, n + 1)
                wait(pe, sub_done, n)
                for g in range(G):
                    out = S[:, g, 0:GK]
                    nc.tensor.matmul(out, qexp[:, s, g, :], kexp[:, s, :, :], start=True, stop=False)
                    last = nc.tensor.matmul(out, identb[:, :], bias_qk[:, s, :].unsqueeze(1).broadcast_to([128, J, TK]),
                                            start=False, stop=True)
                last.then_inc(s_ready, 1)

            def transpose_group(n, s, r):
                wait(pe, pt_copied, n * G + (r - 1))
                for j in range(J):
                    last = nc.tensor.transpose(ptp[r % 2][:, j, :], pr[:, s, r * J + j, :], ident)
                last.then_inc(pt_ready, 1)

            def value_group(n, s, r, i):
                if r == 0:
                    wait(pe, aT_copied, n)
                    if not s and live(i - 3):
                        pe.wait_ge(rank_copied, i - 2)
                pe.wait_ge(pt_copied, n * G + (r + 1))
                for j in range(J):
                    h = r * J + j
                    last = nc.tensor.matmul(O, pT[:, r, j, :], vm[:, s, h * VW:(h + 1) * VW], start=(h == 0), stop=(h == H - 1))
                if r == G - 1:
                    last.then_inc(pv_done, 1)

            def values(n, s, i, between=None, first=None):
                pe.wait_ge(exp_done, n + 1)
                transpose_group(n, s, 0)
                transpose_group(n, s, 1)
                if first:
                    first()
                pe.wait_ge(vm_ready, n + 1)
                value_group(n, s, 0, i)
                transpose_group(n, s, 2)
                value_group(n, s, 1, i)
                if between:
                    between()
                transpose_group(n, s, 3)
                value_group(n, s, 2, i)
                value_group(n, s, 3, i)

            def transpose_out(n, s):
                pe.wait_ge(norm_done, n + 1)
                nc.tensor.transpose(anTp, an[:, s, :], ident).then_inc(anT_ready, 1)

            def project_out(n, s, i):
                pe.wait_ge(aT_copied, n + 1)
                wait(pe, res_done, n)
                if s and live(i + 1):
                    pe.wait_ge(xT_copied, i + 2)
                elif not s and live(i - 3):
                    pe.wait_ge(lg_read, i - 2)
                elif not s:
                    wait(pe, qexp_ready, min(i + 1, NP))
                nc.tensor.matmul(Y, aT[:, :], wt["o"], start=True, stop=True).then_inc(y_ready, 1)

            pe.wait_ge(mv_set, 3)
            front_x(0)
            front_qkv(0, -1)

            def turn(i):
                a, b = 2 * i, 2 * i + 1
                if live(i):
                    scores(a, 0, i)
                if live(i - 1):
                    transpose_out(a - 2, 0)
                    values(b - 2, 1, i, first=lambda: project_out(a - 2, 0, i))
                if live(i):
                    scores(b, 1, i)
                if live(i - 3):
                    ranks(i - 3, i)
                if live(i - 1):
                    transpose_out(b - 2, 1)
                if live(i + 1):
                    front_x(i + 1)
                last_project = (lambda: project_out(b - 2, 1, i)) if live(i - 1) else None
                if live(i):
                    values(a, 0, i, between=lambda: front_qkv(i + 1, i - 2), first=last_project)
                else:
                    if last_project:
                        last_project()
                    if live(i - 2):
                        front_qkv(i + 1, i - 2)
                if live(i - 2):
                    router_logits(i - 2, i + 2 if live(i + 1) else 0)

            turns(turn, pe)


def experts(nc, st, layer, w):
    two = layer == 1
    U = 4
    F = F1 if two else F0
    FC = 2 if two else 4
    UW = 2 * F if two else F
    NSH = B if two else 0
    NS = NSH + SLOTS
    NT = NS // U
    NE = E + (1 if two else 0)
    CH = 8
    with ExitStack() as ctx:
        def sb(name, shape, dt=F32):
            return ctx.enter_context(nc.sbuf_tensor(f"{name}_e{layer}", shape, dt))

        def pb(name):
            return ctx.enter_context(nc.psum_tensor(f"{name}_e{layer}", [128, 4, 128], F32))

        def sem(name):
            return ctx.enter_context(nc.semaphore(f"{name}_e{layer}"))

        three, x, cst, emap, rowmap = st["three"], st["x"], st["cst"], st["emap"], st["rowmap"]
        ident = cst[:, C_ID:C_ID + 128]
        W1, W2 = w["W1"], w["W2"]
        xs = sb("xs", [128, U, RW])
        xi = sb("xi", [128, U], U32)
        xsT = sb("xsT", [128, 2, 128])
        hb = sb("hb", [128, 2, F])
        hm = sb("hm", [128, 2, F])
        h = sb("h", [128, 2, FC * 128])
        hT = sb("hT", [128, 2, FC, 128])
        ys = sb("ys", [128, U, D])
        if two:
            yg = sb("yg", [128, 2, B, D])

        xTp = pb("xTp")
        up = [pb(f"up{i}")[:, :, :].rearrange("p a c -> p (a c)") for i in range(2)]
        hTp = [pb(f"hTp{i}") for i in range(2)]
        yp = [pb(f"yp{i}")[:, 0, :] for i in range(2)]

        xs_in = [sem(f"xs_in{s}") for s in range(U)]
        xi_copied = sem("xi_copied")
        xsT_ready, xsT_copied = sem("xsT_ready"), sem("xsT_copied")
        up_ready, hb_ready, h_ready = sem("up_ready"), sem("hb_ready"), sem("h_ready")
        hT_ready, hT_copied = sem("hT_ready"), sem("hT_copied")
        yp_ready, ys_ready = sem("yp_ready"), sem("ys_ready")
        ys_out = [sem(f"ys_out{s}") for s in range(U)]
        if two:
            h_set = sem("h_set")
            results_in = [sem(f"results_in{c}") for c in range(CH)]
            x_done = sem("x_done")
        dve_step = sem("dve_step")

        rows, results = w["rows"], w["results"]

        def wait(eng, s, value):
            if not isinstance(value, int) or value > 0:
                eng.wait_ge(s, value)

        def row(t, n):
            return t[:, bass.ds(n, 1), :].rearrange("p a d -> p (a d)")

        EDGE = NSH // U

        def turns(body, eng, steps=None):
            def loop(start, end, routed):
                with eng.Fori(start, end) as i:
                    if steps:
                        steps.turn(i - start)
                    body(i, routed)
                if steps:
                    steps.leave(end - start)

            def peeled(i):
                if steps:
                    steps.turn()
                body(i, None)

            peeled(0)
            peeled(1)
            if two:
                loop(2, EDGE - 1, False)
                peeled(EDGE - 1)
                peeled(EDGE)
                peeled(EDGE + 1)
                loop(EDGE + 2, NT - 1, True)
            else:
                loop(2, NT - 1, True)
            peeled(NT - 1)
            peeled(NT)

        def live(n):
            return not isinstance(n, int) or 0 <= n < NS

        def is_routed(n, routed):
            return n >= NSH if routed is None else routed

        def expert(eng, n, routed):
            if not is_routed(n, routed):
                return E
            return nc.s_assert_within(eng.value_load(emap[0:1, bass.ds(n, 1)]), 0, E - 1,
                                      skip_runtime_bounds_check_because="VectorE bounds the map's entries by E - 1")

        def reuse(i):
            return 16 * (i - EDGE)

        block = ctx.enter_context(nc.Block())

        @block.sync
        def _(sp):
            def load(n, s, routed):
                if n is not s:
                    wait(sp, xsT_ready, n - (U - 1))
                    if is_routed(n - U if isinstance(n, int) else n, routed):
                        wait(sp, xi_copied, n - (U - 1))
                if is_routed(n, routed):
                    r = nc.s_assert_within(sp.value_load(rowmap[0:1, bass.ds(n, 1)]), 0, SHARED - 128,
                                           skip_runtime_bounds_check_because="the map's rows are those of its experts' tiles")
                else:
                    r = n * 128 + SHARED
                sp.dma_start(xs[:, s, :], rows[bass.ds(r, 128), :]).then_inc(xs_in[s], 16)

            for s in range(U):
                load(s, s, None)

            def turn(i, routed):
                for s in range(U):
                    if live(U * i + s + U):
                        load(U * i + U + s, s, routed)

            turns(turn, sp)
            for s in range(U):
                sp.wait_ge(ys_out[s], 16 * SLOTS // U)
            if two:
                per = B // CH
                for c in range(CH):
                    for k in range(2):
                        sp.dma_start(yg[:, k, c * per:(c + 1) * per, :],
                                     results[k * N:(k + 1) * N, :].rearrange("(b p) d -> p b d", p=128)
                                     [:, c * per:(c + 1) * per, :]).then_inc(results_in[c], 16)

        @block.gpsimd
        def _(pool):
            if two:
                nc.gpsimd.memset(h[:, :, :], 0.0).then_inc(h_set, 1)
                pool.sem_inc(xi_copied, NSH)

            def send(s):
                nc.gpsimd.indirect_dma_start(results[:, :], bass.IndirectOffsetOnAxis(xi[:, s:s + 1], 0), ys[:, s, :], None)\
                    .then_inc(ys_out[s], 16)

            def note(n, s, i, results_of):
                wait(pool, ys_out[s], reuse(i))
                pool.wait_ge(xs_in[s], 16 * i + 16)
                if results_of is not None:
                    pool.wait_ge(ys_ready, results_of + 1)
                    pool.wait_ge(xi_copied, results_of + 1)
                nc.gpsimd.tensor_tensor(xi[:, s:s + 1], xs[:, s, D:D + 1].bitcast(U32), st["zero"][:, 0:1], ALU.add).then_inc(xi_copied, 1)

            def turn(i, routed):
                for s in range(U):
                    n = U * i + s
                    sends = live(n - 3) and is_routed(n - 3, routed)
                    if live(n - 1) and is_routed(n - 1, routed):
                        note(n - 1, (s - 1) % U, i - (s < 1), n - 3 if sends else None)
                    elif sends:
                        pool.wait_ge(ys_ready, n - 2)
                        pool.wait_ge(xi_copied, n - 2)
                    if sends:
                        send((s - 3) % U)

            turns(turn, pool)

        @block.scalar
        def _(act):
            act.wait_ge(st["weights_in"], st["n_weights"])
            if two:
                act.wait_ge(h_set, 1)

            def x_copy(n, s):
                act.wait_ge(xsT_ready, n + 1)
                nc.scalar.activation(xsT[:, s % 2, :], xTp[:, 0, :], ACT.Copy).then_inc(xsT_copied, 1)

            def silu(n, s):
                if two:
                    act.wait_ge(hb_ready, n + 1)
                    nc.scalar.activation(h[:, s % 2, 0:F], hm[:, s % 2, :], ACT.Silu).then_inc(h_ready, 1)
                else:
                    act.wait_ge(up_ready, n + 1)
                    nc.scalar.activation(h[:, s % 2, :], up[s % 2][:, :], ACT.Silu).then_inc(h_ready, 1)

            def h_copy(n, s):
                act.wait_ge(hT_ready, n + 1)
                nc.scalar.activation(hT[:, s % 2, :, :], hTp[s % 2][:, 0:FC, :], ACT.Copy).then_inc(hT_copied, 1)

            x_copy(0, 0)

            def turn(i, routed):
                for s in range(U):
                    n = U * i + s
                    if live(n + 1):
                        x_copy(n + 1, s + 1)
                    if two and live(n - 1):
                        h_copy(n - 1, s + 1)
                    if live(n):
                        silu(n, s)

            turns(turn, act)
            if two:
                per = B // CH
                for c in range(CH):
                    act.wait_ge(x_done, c + 1)
                    act.dma_start(st["out_dram"][:, c * per:(c + 1) * per, :], x[:, c * per:(c + 1) * per, :])\
                        .then_inc(st["x_out"], 16)
                act.wait_ge(st["x_out"], 16 * CH)

        @block.vector
        def _(dve):
            steps = Steps(dve_step)
            V = nc.vector

            def hidden(n, s):
                dve.wait_ge(up_ready, n + 1)
                steps.then(dve, V.tensor_copy(hb[:, s % 2, :], up[s % 2][:, 0:F]))
                V.tensor_tensor(hm[:, s % 2, :], hb[:, s % 2, :], up[s % 2][:, F:UW], ALU.mult).then_inc(hb_ready, 1)

            def h_copy(n, s):
                dve.wait_ge(hT_ready, n + 1)
                V.tensor_copy(hT[:, s % 2, :, :], hTp[s % 2][:, 0:FC, :]).then_inc(hT_copied, 1)

            def y_copy(n, s, i, routed):
                if routed:
                    wait(dve, ys_out[s], reuse(i))
                dve.wait_ge(yp_ready, n + 1)
                if routed:
                    V.tensor_copy(ys[:, s, :], yp[s % 2]).then_inc(ys_ready, 1)
                else:
                    V.tensor_tensor(row(x, n), row(x, n), yp[s % 2], ALU.add).then_inc(ys_ready, 1)

            def turn(i, routed):
                for s in range(U):
                    n = U * i + s
                    if two:
                        if live(n):
                            hidden(n, s)
                    elif live(n - 1):
                        h_copy(n - 1, s + 1)
                    if live(n - 2):
                        y_copy(n - 2, (s - 2) % U, i - (s < 2), is_routed(n - 2, routed))

            turns(turn, dve, steps)
            if two:
                wsel, per = st["wsel"][1], B // CH
                steps.turn()
                for c in range(CH):
                    dve.wait_ge(results_in[c], 32)
                    for k in range(2):
                        for t in range(c * per, (c + 1) * per):
                            last = V.scalar_tensor_tensor(x[:, t, :], yg[:, k, t, :], wsel[:, k, t:t + 1], x[:, t, :],
                                                          ALU.mult, ALU.add)
                        if k == 0:
                            steps.then(dve, last)
                    last.then_inc(x_done, 1)

        @block.tensor
        def _(pe):
            pe.wait_ge(st["weights_in"], st["n_weights"])
            pe.wait_ge(st["bias_in"], 16)

            def take(n, s, i):
                pe.wait_ge(xs_in[s], 16 * i + 16)
                nc.tensor.transpose(xTp[:, 0, :], xs[:, s, 0:D], ident).then_inc(xsT_ready, 1)

            def widen(n, s, e):
                pe.wait_ge(xsT_copied, n + 1)
                last = nc.tensor.matmul(up[s % 2][:, 0:UW], xsT[:, s % 2, :], row(W1, e), start=True, stop=not two)
                if two:
                    last = nc.tensor.matmul(up[s % 2][:, 0:UW], three[:, :], row(w["B1"], e), start=False, stop=True)
                last.then_inc(up_ready, 1)

            def turn_hidden(n, s):
                pe.wait_ge(h_ready, n + 1)
                for c in range(FC):
                    last = nc.tensor.transpose(hTp[s % 2][:, c, :], h[:, s % 2, c * 128:(c + 1) * 128], ident)
                last.then_inc(hT_ready, 1)

            def narrow(n, s, e):
                pe.wait_ge(hT_copied, n + 1)
                wait(pe, ys_ready, n - 1)
                w2 = W2[:, bass.ds(e, 1), :, :].rearrange("p a c d -> p (a c) d")
                for c in range(FC):
                    last = nc.tensor.matmul(yp[s % 2], hT[:, s % 2, c, :], w2[:, c, :], start=(c == 0),
                                            stop=(c == FC - 1 and not two))
                if two:
                    last = nc.tensor.matmul(yp[s % 2], three[:, :], row(w["B2"], e), start=False, stop=True)
                last.then_inc(yp_ready, 1)

            take(0, 0, 0)

            def turn(i, routed):
                of = {}
                for s in range(U):
                    n = U * i + s
                    if live(n):
                        of[s] = expert(pe, n, routed)
                        widen(n, s, of[s])
                    if live(n + 1):
                        take(n + 1, (s + 1) % U, i + (s == U - 1))
                    if live(n - 1):
                        turn_hidden(n - 1, s + 1)
                    if live(n - 2):
                        narrow(n - 2, s, of[s - 2] if s - 2 in of else expert(pe, n - 2, routed))

            turns(turn, pe)


def build(nc, dram, phases=4):
    with ExitStack() as ctx:
        def sb(name, shape, dt=F32):
            return ctx.enter_context(nc.sbuf_tensor(name, shape, dt))

        I32 = mybir.dt.int32
        st = {"x": sb("x_res", [128, B, D]), "cst": sb("cst", [128, C_END]), "identb": sb("identb", [128, 128], BF16),
              "wsel": [sb(f"wsel{l}", [128, 2, B]) for l in range(2)], "Wg": [sb(f"Wg{l}", [128, E]) for l in range(2)],
              "dest": sb("dest", [128, 2, 4], U32), "fill": sb("fill", [128, E], I32),
              "tiles": sb("tiles", [128, 4, E]), "tiles_u": sb("tiles_u", [128, 2, E], U32), "one": sb("one", [128, E]), "zero": sb("zero", [128, E], U32),
              "onward": sb("onward", [128, E], U32),
              "big": sb("big", [128, 2, SLOTS, E]), "slot_f": sb("slot_f", [128, 2, SLOTS]),
              "emap": sb("emap", [128, B + SLOTS], I32), "rowmap": sb("rowmap", [128, B + SLOTS], I32)}
        st["filling"] = dram["filling"]
        st["ctxT_dram"], st["n_consts"], st["n_weights"] = dram["ctxT"], 16 * 5 + 4, 16 * 4
        parts = sb("parts", [3, NB], BF16)
        st["parts"], st["parts_dram"] = parts, nc.dram_tensor("bias_parts", (3, NB), BF16, kind="Internal").ap()
        st["bias"], st["bias_parts"], st["bias_rest"] = (sb("bias", [NBP, NB // NBP]), sb("bias_p", [NBP, 3, NB // NBP], BF16),
                                                         sb("bias_r", [NBP, 2, NB // NBP]))
        st["three"] = sb("three", [3, 128], BF16)
        w0 = {"W1": sb("W1_0", [128, E, F0]), "W2": sb("W2_0", [128, E, F0 // 128, D])}
        w1 = {"W1": sb("W1_1", [128, E + 1, 2 * F1]), "W2": sb("W2_1", [128, E + 1, 2, D]),
              "B1": parts[:, 0:NB1].rearrange("k (e f) -> k e f", e=E + 1),
              "B2": parts[:, NB1:NB].rearrange("k (e d) -> k e d", e=E + 1)}
        prefetch = [(t[:], dram[f"e0_{k}"]) for k, t in w0.items()]
        prefetch += [(w1[k][:], dram[f"e1_{k}"]) for k in ("W1", "W2")]
        for name in ("consts_in", "x_in", "ident_ready", "weights_in", "maps_ready", "x_out", "bias_split", "bias_out", "bias_in"):
            st[name] = ctx.enter_context(nc.semaphore(f"{name}_all"))
        rows = [nc.dram_tensor(f"rows{l}", (SHARED + l * N, RW), F32, kind="Internal").ap() for l in range(2)]
        results = [nc.dram_tensor(f"results{l}", (2 * N + (E + PAST) * 128, D), F32, kind="Internal").ap() for l in range(2)]
        st["x_dram"] = dram["x"].rearrange("b t d -> t b d")
        st["out_dram"] = dram["out"].rearrange("b t d -> t b d")
        with nc.Block() as block:
            @block.sync
            def _(sp):
                sp.dma_start(st["cst"][:, :], dram["cst"]).then_inc(st["consts_in"], 16)
                sp.dma_start(st["x"][:, 0:2, :], st["x_dram"][:, 0:2, :]).then_inc(st["x_in"], 16)
                for l in range(2):
                    sp.dma_start(st["Wg"][l][:, :], dram[f"e{l}_Wg"]).then_inc(st["consts_in"], 16)
                sp.dma_start(st["bias"][:, :], dram["e1_B"]).then_inc(st["consts_in"], 16)
                sp.dma_start(st["dest"][:, :, :], dram["dest"]).then_inc(st["consts_in"], 16)

            @block.gpsimd
            def _(pool):
                nc.gpsimd.memset(st["one"][:, :], 1.0).then_inc(st["consts_in"], 1)
                nc.gpsimd.memset(st["three"][:, :], 1.0).then_inc(st["consts_in"], 1)
                nc.gpsimd.memset(st["zero"][:, :], 0).then_inc(st["consts_in"], 1)
                nc.gpsimd.memset(st["onward"][:, :], 2 * T).then_inc(st["consts_in"], 1)

            @block.vector
            def _(dve):
                dve.wait_ge(st["consts_in"], st["n_consts"])
                nc.vector.tensor_copy(st["identb"][:, :], st["cst"][:, C_ID:C_ID + 128]).then_inc(st["ident_ready"], 1)

        names = ("W", "cols", "bo", "bv")
        if phases >= 1:
            attention(nc, st, 0, {**{k: dram[f"a0_{k}"] for k in names + ("am", "amT", "pad", "padT")},
                                  "rows": rows[0], "prefetch": prefetch})
        if phases >= 2:
            experts(nc, st, 0, {**w0, "rows": rows[0], "results": results[0]})
        if phases >= 3:
            attention(nc, st, 1, {**{k: dram[f"a1_{k}"] for k in names}, "gb": dram["e1_gb"], "rows": rows[1],
                                  "results": results[0], "prefetch": []})
        if phases >= 4:
            experts(nc, st, 1, {**w1, "rows": rows[1], "results": results[1]})
        else:
            with nc.Block() as block:
                @block.sync
                def _(sp):
                    sp.dma_start(st["out_dram"], st["x"][:, :, :]).then_inc(st["x_out"], 16)
                    sp.wait_ge(st["x_out"], 16)


def layout(v):
    a = {k: np.asarray(t) for k, t in v.items()}
    swap = np.arange(D).reshape(H, 2, DH // 2)[:, ::-1].reshape(D)
    out = {"x": a["x"], "cst": shape_constants()}
    out["dest"] = (np.arange(4)[None, None] * N + np.arange(2)[None, :, None] * T + np.arange(T)[:, None, None]).astype(np.uint32)
    out["filling"] = np.zeros(((E + PAST) * 128, RW), np.uint32)
    out["filling"][:, D] = 2 * N + np.arange((E + PAST) * 128)
    out["filling"] = out["filling"].view(np.float32)
    out["ctxT"] = a["ctx_1024"].transpose(2, 0, 1).reshape(D, B * TK)
    q = "L0_xattn_"
    out["a0_W"] = np.stack([a[q + n].T for n in ("Wq", "Wk", "Wv", "Wo")], 1)
    out["a0_cols"] = np.stack([a[q + n] for n in ("bq", "bk", "bv", "bo")], 1)
    out["a0_bo"], out["a0_bv"] = a[q + "bo"], a[q + "bv"]
    mask, pad = a["mask_SxS2_bk1"], a["mask_BxS2_bf0"]
    out["a0_am"], out["a0_amT"], out["a0_pad"], out["a0_padT"] = mask, mask.T, pad.reshape(-1), pad.T
    q = "L1_xattn_"
    out["a1_W"] = np.stack([a[q + n + "_w"].T for n in "qkvo"] + [a[q + n + "_w"][swap].T for n in "qk"], 1)
    out["a1_cols"] = np.stack([a[q + n + "_b"] for n in "qkvo"] + [a[q + n + "_b"][swap] for n in "qk"], 1)
    out["a1_bo"], out["a1_bv"] = a[q + "o_b"], a[q + "v_b"]
    out["e0_Wg"] = a["L0_ffn_Wg"].T
    out["e0_W1"] = a["L0_ffn_W1"].transpose(1, 0, 2)
    out["e0_W2"] = a["L0_ffn_W2"].reshape(E0, F0 // 128, 128, D).transpose(2, 0, 1, 3)
    f = {k: np.concatenate([a["L1_ffn_" + k], a["L1_ffn_s" + k][None]]) for k in ("w1", "w3", "b1", "b3", "w2", "b2")}
    w2 = np.zeros((E1 + 1, 256, D), np.float32)
    w2[:, :F1] = f["w2"]
    out["e1_Wg"] = a["L1_ffn_gate_w"].T
    out["e1_W1"] = np.concatenate([f["w1"], f["w3"]], 2).transpose(1, 0, 2)
    out["e1_W2"] = w2.reshape(E1 + 1, 2, 128, D).transpose(2, 0, 1, 3)
    out["e1_B"] = np.concatenate([np.concatenate([f["b1"], f["b3"]], 1).reshape(-1), f["b2"].reshape(-1)]).reshape(NBP, -1)
    out["e1_gb"] = a["L1_ffn_gate_b"]
    return {k: np.ascontiguousarray(t) for k, t in out.items()}


def kernel(**inputs):
    import concourse.bacc as bacc
    from concourse.bass_utils import run_bass_kernel_spmd

    nc = bacc.Bacc("TRN2", target_bir_lowering=False, num_devices=1)
    arrays = layout(inputs)
    dram = {k: nc.dram_tensor(f"in_{k}", t.shape, mybir.dt.from_np(t.dtype), kind="ExternalInput").ap()
            for k, t in arrays.items()}
    dram["out"] = nc.dram_tensor("out_x", (B, T, D), F32, kind="ExternalOutput").ap()
    build(nc, dram)
    r = run_bass_kernel_spmd(nc, [{f"in_{k}": t for k, t in arrays.items()}], core_ids=[0])
    return r.results[0]["out_x"]
```

```python
from contextlib import ExitStack

import numpy as np

import concourse.bass as bass
from concourse import mybir

F32 = mybir.dt.float32
BF16 = mybir.dt.bfloat16
U8 = mybir.dt.uint8
U32 = mybir.dt.uint32
ALU = mybir.AluOpType
ACT = mybir.ActivationFunctionType
AX = mybir.AxisListType

B, T, D = 32, 128, 128
TK = 77
H, DH = 16, 8
G, J = 4, 4
SCALE = DH ** -0.5
WINDOW = 64
EPS = 1e-5
NP = B // 2
GK = J * TK
VC = DH + 1
VW = H * VC
VN = 128
VM = H * (VW + VC)
MASKED = -1e30
E0, F0 = 8, 512
E1, F1 = 8, 176
E = E0
N = B * T
NB = (E1 + 1) * 2 * F1
NBP = 96
SLOTS = 2 * N // 128 + E
PAST = SLOTS - 2 * N // 128
REGION = N + 128
SHARED = E * REGION + PAST * 128
RW = 132

C_ID, C_HM, C_GM, C_BAND, C_COS, C_SIN = 0, 128, 132, 136, 216, 344
C_HALF, C_EPS, C_BEFORE, C_BACK, C_SLOT, C_FIRST = 472, 476, 480, 608, 616, 688
C_END = 704


def shape_constants():
    c = np.zeros((128, C_END), np.float32)
    p = np.arange(128)
    c[:, C_ID:C_ID + 128] = np.eye(128)
    c[p, C_HM + (p % 32) // DH] = 1.0
    c[p, C_GM + p // 32] = 1.0
    q, k = np.arange(T)[:, None], np.arange(TK)[None, :]
    c[:, C_BAND:C_BAND + TK] = np.where((k < q - WINDOW) | (k > q), MASKED, 0.0)
    half = DH // 2
    freqs = (np.float32(1.0) / np.float32(10000.0) ** (np.arange(half, dtype=np.float32) / np.float32(half)))
    ang = np.arange(T, dtype=np.float32)[None, :] * freqs.astype(np.float32)[p % half][:, None]
    c[:, C_COS:C_COS + T] = np.cos(ang)
    c[:, C_SIN:C_SIN + T] = np.sin(ang) * np.where(p % DH < half, -1.0, 1.0)[:, None]
    c[:, C_HALF:C_HALF + 4] = -0.5
    c[:, C_EPS:C_EPS + 4] = EPS
    c[:, C_BEFORE:C_BEFORE + 128] = p[:, None] < p[None, :]
    c[:, C_BACK:C_BACK + E] = E - np.arange(E)
    c[:, C_SLOT:C_SLOT + SLOTS] = np.arange(SLOTS)
    c[:, C_FIRST:C_FIRST + E] = np.arange(E) * REGION
    return c


class Steps:

    def __init__(self, sem):
        self.sem, self.base, self.n = sem, 0, 0

    def turn(self, done=None):
        if done is None:
            self.base, self.n = self.base + self.n, 0
        else:
            self.entry, self.per_turn = self.base + self.n, self.n
            self.base, self.n = self.entry + done * self.per_turn, 0

    def leave(self, count):
        assert self.n == self.per_turn
        self.base, self.n = self.entry + count * self.per_turn, 0

    def mark(self, ins):
        self.n += 1
        ins.then_inc(self.sem, 1)

    def wait(self, eng):
        eng.wait_ge(self.sem, self.base + self.n)

    def then(self, eng, ins):
        self.mark(ins)
        self.wait(eng)


def attention(nc, st, layer, w):
    rope = layer == 1
    copies = 3 if rope else 2
    with ExitStack() as ctx:
        def sb(name, shape, dt=F32):
            return ctx.enter_context(nc.sbuf_tensor(f"{name}_{layer}", shape, dt))

        def pb(name, shape, dt=F32):
            return ctx.enter_context(nc.psum_tensor(f"{name}_{layer}", shape, dt))

        def sem(name):
            return ctx.enter_context(nc.semaphore(f"{name}_{layer}"))

        x, cst, identb = st["x"], st["cst"], st["identb"]
        ident = cst[:, C_ID:C_ID + 128]
        names = ["q", "k", "v", "o"] + (["qr", "kr"] if rope else [])
        W = sb("W", [128, len(names), 128])
        cols = sb("cols", [128, len(names)])
        wt = {n: W[:, i, :] for i, n in enumerate(names)}
        bias = {n: cols[:, i:i + 1] for i, n in enumerate(names)}
        bo = sb("bo", [128, 128])
        bv = sb("bv", [128, 128])
        ctxT = sb("ctxT", [128, 2 * TK])
        stats = sb("stats", [128, 4, 6])
        mv = st["mv"]
        rstd = sb("rstd", [128, 4])
        vare = sb("vare", [128, 4])
        xn = sb("xn", [128, 2, 128])
        xr = sb("xr", [128, 2, D])
        out_rows = st["out_rows"][:, :, 0:copies, :]
        onesb, beforeb = st["onesb"], st["beforeb"]
        key = sb("key", [128, 2, E])
        pick = sb("pick", [128, 2, E])
        best = sb("best", [128, 2])
        mark = sb("mark", [128, 2])
        oh = sb("oh", [128, 2, 2, E])
        both = sb("both", [128, 2, E], BF16)
        rank = sb("rank", [128, 4, E])
        pos = sb("pos", [128, 2, E])
        carry = sb("carry", [128, 2, E])
        posk = sb("posk", [128, 2, 2, E])
        goes = sb("goes", [128, 2, copies], U32)
        posf = sb("posf", [128, 2, 2])
        posi = sb("posi", [128, 2, 2], U32)
        if rope:
            yc = sb("yc", [128, 2, 2, D])
            yw = sb("yw", [128, 2, 2, D])
            lg = sb("lg", [128, 2, E])
            shift = sb("shift", [128, 2, E])
            prob = sb("prob", [128, 2, E])
            total = sb("total", [128, 2])
            rtotal = sb("rtotal", [128, 2])
            gb = sb("gb", [128, E])
        else:
            top = sb("top", [128, 2, B])
        xT = sb("xT", [128, 4 * T])
        qexp = sb("qexp", [128, 2, G, T])
        kT = sb("kT", [128, 2 * TK])
        krT = sb("krT", [128, 2 * TK]) if rope else None
        kro = sb("kro", [128, 2, TK]) if rope else None
        kcos = sb("kcos", [128, 2, TK]) if rope else None
        ksin = sb("ksin", [128, 2, TK]) if rope else None
        qro = sb("qro", [128, 2, T]) if rope else None
        qcos = sb("qcos", [128, 2, T]) if rope else None
        qsin = sb("qsin", [128, 2, T]) if rope else None
        kexp = sb("kexp", [128, 2, J, TK])
        vs = sb("vs", [TK, 2, 128])
        vm = st["vm"]
        bias_qk = sb("bias_qk", [128, 2, TK], BF16)
        pr = sb("pr", [128, 2, H, TK])
        mx = sb("mx", [128, H])
        pT = sb("pT", [TK, G, J, T])
        rden = sb("rden", [128, H])
        an = sb("an", [128, 2, 128])
        aT = sb("aT", [128, 128])
        if not rope:
            am8 = sb("am8", [128, TK], U8)
            negA = sb("negA", [128, TK])
            amT8 = sb("amT8", [TK, 128], U8)
            keepA = sb("keepA", [TK, 128])
            pad8 = sb("pad8", [128, B * TK], U8)
            negP = sb("negP", [128, B * TK])
            padT8 = sb("padT8", [TK, B], U8)
            keepP = sb("keepP", [TK, B])
            some = sb("some", [128, B])
            isome = sb("isome", [128, B])
            nz = sb("nz", [128, B])

        S = pb("S", [128, G, 512])
        ptp = [pb(f"ptp{i}", [TK, J, T]) for i in range(2)]
        M0 = pb("M0", [128, 512])
        M1 = pb("M1", [128, 512])
        O, anTp, rankp = M0[:, 0:VW], M0[:, VW:VW + 128], M0[:, 384:384 + 4 * E]
        Y, lgp = M1[:, 0:128], M1[:, 128:128 + 2 * E]
        Qp, Qrp = M1[:, 256:512], M1[:, 0:256]
        Kp, Krp = S[:, 0, GK:GK + 2 * TK], S[:, 1, GK:GK + 2 * TK]
        Vp = [S[0:TK, 2, GK:GK + 128], S[0:TK, 3, GK:GK + 128]]

        consts_in = sem("consts_in")
        ctx_in = sem("ctx_in")
        vm_set = sem("vm_set")
        masks_set = sem("masks_set")
        counts_ready = sem("counts_ready")
        mv_ready = sem("mv_ready")
        rstd_ready = sem("rstd_ready")
        xn_ready = sem("xn_ready")
        xT_ready = sem("xT_ready")
        xT_copied = sem("xT_copied")
        q_ready = sem("q_ready")
        qexp_ready = sem("qexp_ready")
        kv_ready = sem("kv_ready")
        k_copied = sem("k_copied")
        v_copied = sem("v_copied")
        kexp_ready = sem("kexp_ready")
        vm_ready = sem("vm_ready")
        s_ready = sem("s_ready")
        sub_done = sem("sub_done")
        exp_done = sem("exp_done")
        pt_ready = sem("pt_ready")
        pt_copied = sem("pt_copied")
        pv_done = sem("pv_done")
        norm_done = sem("norm_done")
        anT_ready = sem("anT_ready")
        aT_copied = sem("aT_copied")
        y_ready = sem("y_ready")
        bo_added = sem("bo_added")
        res_done = sem("res_done")
        dve_step = sem("dve_step")
        pool_step = sem("pool_step")
        mv_set = sem("mv_set")
        idx_set = sem("idx_set")
        xr_ready = sem("xr_ready")
        spread_done = sem("spread_done")
        lg_ready = sem("lg_ready")
        lg_read = sem("lg_read")
        shift_ready = sem("shift_ready")
        prob_ready = sem("prob_ready")
        both_ready = sem("both_ready")
        rank_ready = sem("rank_ready")
        rank_copied = sem("rank_copied")
        pos_ready = sem("pos_ready")
        scattered = sem("scattered")
        filled = sem("filled")
        if rope:
            shared_out = sem("shared_out")
            results_in = sem("results_in")
            weighted = sem("weighted")
            x_taken = sem("x_taken")
        maps_done = sem("maps_done")

        n_const = 16 * (5 if rope else 4 + 4)
        rows = w["rows"]

        FULL = 3

        def turns(body, eng, steps=None):
            for i in range(FULL + 1):
                if steps:
                    steps.turn()
                body(i)
            with eng.Fori(FULL + 1, NP - 2) as i:
                if steps:
                    steps.turn(i - (FULL + 1))
                body(i)
            if steps:
                steps.leave(NP - 2 - (FULL + 1))
            for i in range(NP - 2, NP + 3):
                if steps:
                    steps.turn()
                body(i)

        def live(p):
            return not isinstance(p, int) or 0 <= p < NP

        def wait(eng, s, value):
            if not isinstance(value, int) or value > 0:
                eng.wait_ge(s, value)

        def fill_up(eng, experts):
            eng.wait_ge(st["maps_ready"], layer + 1)
            for e in experts:
                count = 128 * (1 if e < E - 1 else 1 + PAST)
                first = nc.s_assert_within(eng.value_load(st["fill"][0:1, e:e + 1]), 0, (e + 1) * REGION - 128,
                                           skip_runtime_bounds_check_because="a region has room for all the tokens")
                eng.dma_start(rows[bass.ds(first, count), :], st["filling"][e * 128:e * 128 + count, :]).then_inc(filled, 16)

        block = ctx.enter_context(nc.Block())

        @block.sync
        def _(sp):
            def load_ctx(j):
                wait(sp, kv_ready, j)
                sp.dma_start(ctxT[:, :], st["ctxT_dram"][:, bass.ds(j * (2 * TK), 2 * TK)]).then_inc(ctx_in, 16)

            def load_results(j):
                wait(sp, weighted, j)
                for k in range(2):
                    sp.dma_start(yc[:, k, :, :], w["results"][k * N:(k + 1) * N, :].rearrange("(b p) d -> p b d", p=128)
                                 [:, bass.ds(2 * j, 2), :]).then_inc(results_in, 16)

            def store_shared(p):
                sp.wait_ge(spread_done, p + 1)
                sp.wait_ge(idx_set, p + 1)
                sp.dma_start(rows[bass.ds(p * 256 + SHARED, 256), :].rearrange("(s p) d -> p s d", p=128),
                             out_rows[:, :, 2, :]).then_inc(shared_out, 16)

            if rope:
                load_results(0)
            sp.dma_start(W[:, :, :], w["W"]).then_inc(consts_in, 16)
            sp.dma_start(cols[:, :], w["cols"]).then_inc(consts_in, 16)
            sp.dma_start(bo[:, :], w["bo"].partition_broadcast(128)).then_inc(consts_in, 16)
            sp.dma_start(bv[:, :], w["bv"].partition_broadcast(128)).then_inc(consts_in, 16)
            load_ctx(0)
            if rope:
                sp.dma_start(gb[:, :], w["gb"].partition_broadcast(128)).then_inc(consts_in, 16)
                load_results(1)
            else:
                sp.dma_start(am8[:, :], w["am"]).then_inc(consts_in, 16)
                sp.dma_start(amT8[:, :], w["amT"]).then_inc(consts_in, 16)
                sp.dma_start(pad8[:, :], w["pad"].partition_broadcast(128)).then_inc(consts_in, 16)
                sp.dma_start(padT8[:, :], w["padT"]).then_inc(consts_in, 16)
                for b0, b1 in ((2, 8), (8, B)):
                    sp.dma_start(st["x"][:, b0:b1, :], st["x_dram"][:, b0:b1, :]).then_inc(st["x_in"], 16)
            load_ctx(1)
            for dst, src in w["prefetch"]:
                sp.dma_start(dst, src).then_inc(st["weights_in"], 16)
            if not rope:
                sp.wait_ge(st["bias_split"], 1)
                sp.dma_start(st["parts_dram"].rearrange("k (p n) -> p k n", p=NBP), st["bias_parts"][:, :, :])\
                    .then_inc(st["bias_out"], 16)
                sp.wait_ge(st["bias_out"], 16)
                sp.dma_start(st["parts"][:, :], st["parts_dram"]).then_inc(st["bias_in"], 16)

            def turn(i):
                if live(i) and live(i + 2):
                    if rope:
                        load_results(i + 2)
                    load_ctx(i + 2)
                if rope and live(i - 3):
                    store_shared(i - 3)

            turns(turn, sp)
            if rope:
                sp.wait_ge(shared_out, 16 * NP)
            fill_up(sp, range(E - 1, E // 2 - 1, -1))
            sp.wait_ge(scattered, 64 * NP)
            sp.wait_ge(filled, 16 * E)

        @block.gpsimd
        def _(pool):
            steps = Steps(pool_step)
            if not rope:
                nc.gpsimd.memset(mv[:, :, :], 1.0).then_inc(mv_set, 1)
                steps.then(pool, nc.gpsimd.memset(vm[:, :, :], 0.0))
                for s in range(2):
                    last = nc.gpsimd.memset(vm[:, s, 0:H * (VW + VC)].rearrange("k (h c) -> k h c", h=H)[:, :, DH:VC], 1.0)
                last.then_inc(vm_set, 1)
                nc.gpsimd.memset(st["out_rows"][:, :, :, :], 0.0).then_inc(mv_set, 1)
                nc.gpsimd.memset(onesb[:, :], 1.0).then_inc(mv_set, 1)
                pool.wait_ge(vm_set, 1)
                pool.wait_ge(mv_set, 3)
            pool.wait_ge(consts_in, n_const)
            pool.wait_ge(st["consts_in"], st["n_consts"])
            if rope:
                for s in range(2):
                    last = nc.gpsimd.tensor_copy(bias_qk[:, s, :], cst[:, C_BAND:C_BAND + TK])
                last.then_inc(masks_set, 1)

            def norms(i):
                pool.wait_ge(mv_ready, i + 2)
                steps.then(pool, nc.gpsimd.tensor_tensor(vare[:, :], mv[:, :, 1], cst[:, C_EPS:C_EPS + 4], ALU.add))
                nc.gpsimd.tensor_tensor(rstd[:, :], vare[:, :], cst[:, C_HALF:C_HALF + 4], ALU.pow).then_inc(rstd_ready, 1)

            def scatter(p):
                pool.wait_ge(idx_set, p + 1)
                pool.wait_ge(spread_done, p + 1)
                pool.wait_ge(pos_ready, p + 1)
                steps.mark(nc.gpsimd.tensor_tensor(
                    goes[:, :, :], goes[:, :, :],
                    st["onward"][:, 0:2 * copies].rearrange("p (s c) -> p s c", s=2), ALU.add))
                for s in range(2):
                    for k in range(2):
                        nc.gpsimd.indirect_dma_start(rows[:, :], bass.IndirectOffsetOnAxis(posi[:, k, s:s + 1], 0),
                                                     out_rows[:, s, k, :], None).then_inc(scattered, 16)

            def keys(j):
                pool.wait_ge(k_copied, j + 1)
                k2 = kT[:, :].rearrange("p (s k) -> p s k", s=2)
                if rope:
                    kr2 = krT[:, :].rearrange("p (s k) -> p s k", s=2)
                    tab = [cst[:, c:c + TK].unsqueeze(1).broadcast_to([128, 2, TK]) for c in (C_COS, C_SIN)]
                    steps.mark(nc.gpsimd.tensor_tensor(kcos[:, :, :], k2, tab[0], ALU.mult))
                    steps.then(pool, nc.gpsimd.tensor_tensor(ksin[:, :, :], kr2, tab[1], ALU.mult))
                    steps.then(pool, nc.gpsimd.tensor_tensor(kro[:, :, :], kcos[:, :, :], ksin[:, :, :], ALU.add))
                    k2 = kro[:, :, :]
                for s in range(2):
                    n = j * 2 + s
                    wait(pool, s_ready, n - 1)
                    if not rope:
                        pool.wait_ge(masks_set, 1)
                        steps.mark(nc.gpsimd.tensor_tensor(
                            bias_qk[:, s, :], negA[:, :], negP[:, bass.ds(n * TK, TK)], ALU.add))
                    nc.gpsimd.tensor_tensor(
                        kexp[:, s, :, :], k2[:, s, :].unsqueeze(1).broadcast_to([128, J, TK]),
                        cst[:, C_HM:C_HM + J].unsqueeze(2).broadcast_to([128, J, TK]), ALU.mult).then_inc(kexp_ready, 1)

            def index(p):
                wait(pool, scattered, 64 * p)
                if rope:
                    wait(pool, shared_out, 16 * p)
                steps.wait(pool)
                nc.gpsimd.tensor_tensor(out_rows[:, :, :, D:D + 1].bitcast(U32), goes[:, :, :].unsqueeze(3),
                                        st["zero"][:, 0:2 * copies].rearrange("p (s c) -> p s c", s=2).unsqueeze(3),
                                        ALU.add).then_inc(idx_set, 1)

            def padded_values(j, s):
                n = j * 2 + s
                pool.wait_ge(v_copied, j + 1)
                wait(pool, pv_done, n - 1)
                own = vm[:, s, 0:H * (VW + VC)].rearrange("k (h c) -> k h c", h=H)[:, :, 0:DH]
                nc.gpsimd.tensor_tensor(own, vs[:, s, :].rearrange("k (h d) -> k h d", d=DH),
                                        bv[0:TK, :].rearrange("k (h d) -> k h d", d=DH), ALU.add).then_inc(vm_ready, 1)

            def output_bias(j):
                pool.wait_ge(xn_ready, 2 * j + 2)
                xb = x[:, bass.ds(j * 2, 2), :]
                nc.gpsimd.tensor_tensor(xb, xb, bo[:, :].unsqueeze(1).broadcast_to([128, 2, D]), ALU.add).then_inc(bo_added, 1)

            def take_results(j):
                pool.wait_ge(weighted, j + 1)
                steps.then(pool, nc.gpsimd.tensor_tensor(yw[:, 0, :, :], yw[:, 0, :, :], yw[:, 1, :, :], ALU.add))
                xb = x[:, bass.ds(j * 2, 2), :]
                nc.gpsimd.tensor_tensor(xb, xb, yw[:, 0, :, :], ALU.add).then_inc(x_taken, 1)

            steps.then(pool, nc.gpsimd.tensor_copy(goes[:, :, :], st["dest"][:, :, 0:copies]))
            if rope:
                take_results(0)
            norms(-1)
            if rope:
                take_results(1)
            keys(0)
            output_bias(0)

            def turn(i):
                if live(i + 1) or live(i - 2):
                    norms(i)
                if live(i):
                    padded_values(i, 0)
                    padded_values(i, 1)
                if live(i - 3):
                    index(i - 3)
                if live(i + 1):
                    output_bias(i + 1)
                if rope and live(i) and live(i + 2):
                    take_results(i + 2)
                if live(i + 1):
                    keys(i + 1)
                if live(i - 3):
                    scatter(i - 3)

            turns(turn, pool, steps)

        @block.scalar
        def _(act):
            def x_copy(i):
                act.wait_ge(xT_ready, i + 2)
                first, end = 0 if live(i + 1) else 2 * T, 4 * T if live(i - 2) else 2 * T
                nc.scalar.activation(xT[:, first:end], M1[:, first:end], ACT.Copy).then_inc(xT_copied, 1)

            def kv_copy(j):
                act.wait_ge(kv_ready, j + 1)
                wait(act, vm_ready, 2 * j)
                last = nc.scalar.activation(kT[:, :], Kp, ACT.Identity, bias=bias["k"])
                if rope:
                    last = nc.scalar.activation(krT[:, :], Krp, ACT.Identity, bias=bias["kr"])
                last.then_inc(k_copied, 1)
                for s in range(2):
                    last = nc.scalar.activation(vs[:, s, :], Vp[s], ACT.Copy)
                last.then_inc(v_copied, 1)

            def pt_copy(n, r):
                act.wait_ge(pt_ready, n * G + (r + 1))
                nc.scalar.activation(pT[:, r, :, :], ptp[r % 2][:, :, :], ACT.Copy).then_inc(pt_copied, 1)

            def exps(n, s):
                act.wait_ge(sub_done, n + 1)
                p = pr[:, s, :, :].rearrange("p h k -> p (h k)")
                nc.scalar.activation(p, p, ACT.Exp, scale=SCALE).then_inc(exp_done, 1)

            def at_copy(n):
                act.wait_ge(anT_ready, n + 1)
                nc.scalar.activation(aT[:, :], anTp, ACT.Copy).then_inc(aT_copied, 1)

            def rank_copy(p):
                act.wait_ge(rank_ready, p + 1)
                nc.scalar.activation(rank[:, :, :], rankp.rearrange("p (a e) -> p a e", e=E), ACT.Copy).then_inc(rank_copied, 1)

            def spread(p):
                act.wait_ge(xr_ready, p + 1)
                wait(act, scattered, 64 * p)
                if rope:
                    wait(act, shared_out, 16 * p)
                nc.scalar.activation(out_rows[:, :, :, 0:D], xr[:, :, :].unsqueeze(2).broadcast_to([128, 2, copies, D]),
                                     ACT.Copy).then_inc(spread_done, 1)

            def weigh(j):
                act.wait_ge(results_in, 32 * j + 32)
                wait(act, x_taken, j)
                for k in range(2):
                    for s in range(2):
                        last = nc.scalar.activation(yw[:, k, s, :], yc[:, k, s, :], ACT.Copy,
                                                    scale=st["wsel"][0][:, k, bass.ds(2 * j + s, 1)])
                last.then_inc(weighted, 1)

            def router_exp(p):
                act.wait_ge(shift_ready, p + 1)
                nc.scalar.activation(prob[:, :, :], shift[:, :, :], ACT.Exp).then_inc(prob_ready, 1)

            if rope:
                weigh(0)
                weigh(1)
            act.wait_ge(consts_in, n_const)
            x_copy(-1)
            kv_copy(0)

            def turn(i):
                a, b = 2 * i, 2 * i + 1
                if live(i - 1):
                    at_copy(a - 2)
                if live(i - 1):
                    for r in range(G):
                        pt_copy(b - 2, r)
                if live(i):
                    exps(a, 0)
                if live(i - 3):
                    spread(i - 3)
                if rope and live(i) and live(i + 2):
                    weigh(i + 2)
                if live(i - 1):
                    at_copy(b - 2)
                if live(i - 3):
                    rank_copy(i - 3)
                if live(i + 1) or live(i - 2):
                    x_copy(i)
                if live(i):
                    for r in range(3):
                        pt_copy(a, r)
                if rope and live(i - 2):
                    router_exp(i - 2)
                if live(i + 1):
                    kv_copy(i + 1)
                if live(i):
                    pt_copy(a, 3)
                    exps(b, 1)

            turns(turn, act)
            if not rope:
                act.wait_ge(shift_ready, 1)
                nc.scalar.activation(top[:, 1, :], top[:, 0, :], ACT.Exp).then_inc(prob_ready, 1)
            fill_up(act, range(E // 2))

        @block.vector
        def _(dve):
            steps = Steps(dve_step)
            dve.wait_ge(consts_in, n_const)
            dve.wait_ge(st["consts_in"], st["n_consts"])
            if not rope:
                nc.vector.tensor_scalar(negA[:, :], am8[:, :], MASKED, None, ALU.mult)
                nc.vector.tensor_scalar(negP[:, :], pad8[:, :], MASKED, None, ALU.mult).then_inc(masks_set, 1)
                nc.vector.tensor_scalar(keepA[:, :], amT8[:, :], -1.0, 1.0, ALU.mult, ALU.add)
                nc.vector.tensor_scalar(keepP[:, :], padT8[:, :], -1.0, 1.0, ALU.mult, ALU.add).then_inc(masks_set, 1)
                dve.wait_ge(counts_ready, 1)
                steps.then(dve, nc.vector.tensor_scalar(some[:, :], Y[:, 0:B], 1.0, None, ALU.min))
                steps.then(dve, nc.vector.reciprocal(isome[:, :], some[:, :]))
                steps.then(dve, nc.vector.tensor_tensor(nz[:, :], some[:, :], isome[:, :], ALU.mult))

            def row(n):
                return x[:, bass.ds(n, 1), :].rearrange("p a d -> p (a d)")

            def norm_stats(p, at):
                for s in range(2):
                    last = nc.vector.bn_stats(stats[:, at + s, :], row(p * 2 + s))
                steps.mark(last)

            def norm_mean(at):
                for s in range(2):
                    last = nc.vector.bn_aggr(mv[:, at + s, :], stats[:, at + s, :])
                return last

            def norm_x(j):
                dve.wait_ge(rstd_ready, j + 1)
                for s in range(2):
                    nc.vector.tensor_scalar(xn[:, s, :], row(j * 2 + s), mv[:, s, 0:1], rstd[:, s:s + 1],
                                            ALU.subtract, ALU.mult).then_inc(xn_ready, 1)

            def router_x(p):
                dve.wait_ge(rstd_ready, p + 4)
                wait(dve, spread_done, p)
                wait(dve, xT_ready, p + 3)
                for s in range(2):
                    last = nc.vector.tensor_scalar(xr[:, s, :], row(p * 2 + s), mv[:, 2 + s, 0:1], rstd[:, 2 + s:3 + s],
                                                   ALU.subtract, ALU.mult)
                last.then_inc(xr_ready, 1)

            V = nc.vector
            back = cst[:, C_BACK:C_BACK + E]

            def over_e(a):
                return a.unsqueeze(2).broadcast_to([128, 2, E])

            def over_s(a):
                return a.unsqueeze(1).broadcast_to([128, 2, E])

            def do(ins):
                steps.then(dve, ins)

            def take_logits(p):
                dve.wait_ge(lg_ready, p + 1)
                logits = lgp.rearrange("p (s e) -> p s e", s=2)
                if rope:
                    V.tensor_copy(lg[:, :, :], logits).then_inc(lg_read, 1)
                    dve.wait_ge(lg_read, p + 1)
                    do(V.tensor_reduce(best[:, :], lg[:, :, :], AX.X, ALU.max))
                    V.tensor_tensor(shift[:, :, :], lg[:, :, :], over_e(best[:, :]), ALU.subtract).then_inc(shift_ready, 1)
                else:
                    V.tensor_scalar(key[:, :, :], logits, -1e38, None, ALU.max).then_inc(lg_read, 1)

            def softmax_logits(p):
                dve.wait_ge(prob_ready, p + 1)
                do(V.tensor_reduce(total[:, :], prob[:, :, :], AX.X, ALU.add))
                do(V.reciprocal(rtotal[:, :], total[:, :]))
                do(V.tensor_tensor(prob[:, :, :], prob[:, :, :], over_e(rtotal[:, :]), ALU.mult))
                do(V.tensor_tensor(key[:, :, :], prob[:, :, :], over_s(gb[:, :]), ALU.add))
                steps.mark(V.tensor_scalar(key[:, :, :], key[:, :, :], -1e38, None, ALU.max))

            def choose(p):
                if not rope:
                    dve.wait_ge(lg_read, p + 1)
                for k in range(2):
                    do(V.tensor_reduce(best[:, :], key[:, :, :], AX.X, ALU.max))
                    if not rope:
                        steps.mark(V.tensor_copy(top[:, k, bass.ds(2 * p, 2)], best[:, :]))
                    for s in range(2):
                        last = V.scalar_tensor_tensor(pick[:, s, :], key[:, s, :], best[:, s:s + 1], back,
                                                      ALU.is_equal, ALU.mult)
                    do(last)
                    do(V.tensor_reduce(mark[:, :], pick[:, :, :], AX.X, ALU.max))
                    do(V.tensor_tensor(oh[:, k, :, :], over_s(back), over_e(mark[:, :]), ALU.is_equal))
                    if k == 0:
                        do(V.scalar_tensor_tensor(key[:, :, :], oh[:, 0, :, :], -2e38, key[:, :, :], ALU.mult, ALU.add))
                V.tensor_tensor(both[:, :, :], oh[:, 0, :, :], oh[:, 1, :, :], ALU.add).then_inc(both_ready, 1)
                if rope:
                    do(V.tensor_tensor(posk[:, :, :, :], oh[:, :, :, :], prob[:, :, :].unsqueeze(1).broadcast_to([128, 2, 2, E]),
                                       ALU.mult))
                    do(V.tensor_reduce(st["wsel"][1][:, :, bass.ds(2 * p, 2)], posk[:, :, :, :], AX.X, ALU.add))

            def place(p):
                dve.wait_ge(rank_copied, p + 1)
                steps.mark(V.tensor_tensor(pos[:, :, :], rank[:, 0:2, :], over_s(carry[:, 0, :]), ALU.add))
                do(V.tensor_tensor(carry[:, 1, :], carry[:, 0, :], rank[:, 2, :], ALU.add))
                steps.mark(V.tensor_tensor(carry[:, 0, :], carry[:, 1, :], rank[:, 3, :], ALU.add))
                do(V.tensor_tensor(posk[:, :, :, :], oh[:, :, :, :], pos[:, :, :].unsqueeze(1).broadcast_to([128, 2, 2, E]),
                                   ALU.mult))
                do(V.tensor_reduce(posf[:, :, :], posk[:, :, :, :], AX.X, ALU.add))
                V.tensor_copy(posi[:, :, :], posf[:, :, :]).then_inc(pos_ready, 1)

            def q_expand(j):
                dve.wait_ge(q_ready, j + 1)
                wait(dve, s_ready, 2 * j)
                gm = cst[:, C_GM:C_GM + G].unsqueeze(2).broadcast_to([128, G, T])
                q2 = Qp.rearrange("p (s q) -> p s q", s=2)
                if rope:
                    tab = [cst[:, c:c + T].unsqueeze(1).broadcast_to([128, 2, T]) for c in (C_COS, C_SIN)]
                    steps.then(dve, nc.vector.scalar_tensor_tensor(
                        qcos[:, :, :], q2, bias["q"], tab[0], ALU.add, ALU.mult))
                    steps.then(dve, nc.vector.scalar_tensor_tensor(
                        qsin[:, :, :], Qrp.rearrange("p (s q) -> p s q", s=2), bias["qr"], tab[1], ALU.add, ALU.mult))
                    steps.then(dve, nc.vector.tensor_tensor(qro[:, :, :], qcos[:, :, :], qsin[:, :, :], ALU.add))
                for s in range(2):
                    if rope:
                        last = nc.vector.tensor_tensor(
                            qexp[:, s, :, :], qro[:, s, :].unsqueeze(1).broadcast_to([128, G, T]), gm, ALU.mult)
                    else:
                        last = nc.vector.scalar_tensor_tensor(
                            qexp[:, s, :, :], q2[:, s, :].unsqueeze(1).broadcast_to([128, G, T]), bias["q"], gm,
                            ALU.add, ALU.mult)
                last.then_inc(qexp_ready, 1)

            def softmax_shift(n, s):
                dve.wait_ge(s_ready, n + 1)
                sc = S[:, :, 0:GK].rearrange("p g (j k) -> p g j k", k=TK)
                steps.then(dve, nc.vector.tensor_reduce(
                    mx[:, :].rearrange("p (g j) -> p g j", g=G), sc, AX.X, ALU.max))
                wait(dve, pv_done, n - 1)
                nc.vector.tensor_tensor(
                    pr[:, s, :, :].rearrange("p (g j) k -> p g j k", g=G), sc,
                    mx[:, :].rearrange("p (g j) -> p g j", g=G).unsqueeze(3).broadcast_to([128, G, J, TK]),
                    ALU.subtract).then_inc(sub_done, 1)

            def normalise(n, s):
                heads = O.rearrange("p (h c) -> p h c", h=H)
                dve.wait_ge(pv_done, n + 1)
                steps.then(dve, nc.vector.reciprocal(rden[:, :], heads[:, :, DH]))
                nc.vector.scalar_tensor_tensor(
                    an[:, s, :].rearrange("p (h d) -> p h d", d=DH), heads[:, :, 0:DH],
                    1.0 if rope else nz[:, bass.ds(n, 1)], rden[:, :].unsqueeze(2).broadcast_to([128, H, DH]),
                    ALU.mult, ALU.mult).then_inc(norm_done, 1)

            def residual(n, pair):
                dve.wait_ge(y_ready, n + 1)
                dve.wait_ge(bo_added, pair + 1)
                xb = x[:, bass.ds(n, 1), :].rearrange("p a d -> p (a d)")
                nc.vector.tensor_tensor(xb, xb, Y, ALU.add).then_inc(res_done, 1)

            if not rope:
                bias1, part, rest = st["bias"], st["bias_parts"], st["bias_rest"]
                do(V.tensor_copy(part[:, 0, :], bias1[:, :]))
                do(V.tensor_tensor(rest[:, 0, :], bias1[:, :], part[:, 0, :], ALU.subtract))
                do(V.tensor_copy(part[:, 1, :], rest[:, 0, :]))
                do(V.tensor_tensor(rest[:, 1, :], rest[:, 0, :], part[:, 1, :], ALU.subtract))
                V.tensor_copy(part[:, 2, :], rest[:, 1, :]).then_inc(st["bias_split"], 1)
            if not rope:
                steps.mark(V.tensor_copy(beforeb[:, :], cst[:, C_BEFORE:C_BEFORE + 128]))
            steps.mark(V.tensor_copy(carry[:, 0, :], cst[:, C_FIRST:C_FIRST + E]))
            if not rope:
                dve.wait_ge(mv_set, 3)
            if rope:
                dve.wait_ge(x_taken, 1)
            else:
                dve.wait_ge(st["x_in"], 16)
            norm_stats(0, 0)
            steps.wait(dve)
            norm_mean(0).then_inc(mv_ready, 1)
            norm_x(0)
            if not rope:
                dve.wait_ge(st["x_in"], 48)
            q_expand(0)

            def turn(i):
                a, b = 2 * i, 2 * i + 1
                if live(i + 1):
                    if rope:
                        dve.wait_ge(x_taken, i + 2)
                    norm_stats(i + 1, 0)
                if live(i - 2):
                    dve.wait_ge(res_done, 2 * i - 2)
                    norm_stats(i - 2, 2)
                if live(i):
                    softmax_shift(a, 0)
                else:
                    steps.wait(dve)
                last = None
                if live(i + 1):
                    last = norm_mean(0)
                if live(i - 2):
                    last = norm_mean(2)
                if last:
                    last.then_inc(mv_ready, 1)
                if live(i - 3):
                    choose(i - 3)
                if live(i + 1):
                    norm_x(i + 1)
                if live(i - 2):
                    router_x(i - 2)
                if live(i - 1):
                    residual(a - 2, i - 1)
                    normalise(b - 2, 1)
                if live(i):
                    softmax_shift(b, 1)
                if live(i - 1):
                    residual(b - 2, i - 1)
                if live(i - 2):
                    take_logits(i - 2)
                if live(i - 3):
                    place(i - 3)
                if live(i + 1):
                    q_expand(i + 1)
                if live(i):
                    normalise(a, 0)
                if rope and live(i - 2):
                    softmax_logits(i - 2)

            turns(turn, dve, steps)
            wsel = st["wsel"][layer]
            steps.turn()
            steps.wait(dve)
            if not rope:
                do(V.tensor_tensor(top[:, 0, :], top[:, 1, :], top[:, 0, :], ALU.subtract))
                dve.sem_inc(shift_ready, 1)
                dve.wait_ge(prob_ready, 1)
                do(V.tensor_scalar(top[:, 0, :], top[:, 1, :], 1.0, None, ALU.add))
                do(V.reciprocal(wsel[:, 0, :], top[:, 0, :]))
                do(V.tensor_tensor(wsel[:, 1, :], top[:, 1, :], wsel[:, 0, :], ALU.mult))
            fill, tmap, cu, big = st["fill"], st["tiles"], st["tiles_u"], st["big"]
            first = cst[:, C_FIRST:C_FIRST + E]
            do(V.tensor_copy(fill[:, :], carry[:, 0, :]))
            do(V.tensor_tensor(tmap[:, 0, :], carry[:, 0, :], first, ALU.subtract))
            do(V.tensor_scalar(cu[:, 0, :], tmap[:, 0, :], 127.0, None, ALU.add))
            do(V.tensor_scalar(cu[:, 1, :], cu[:, 0, :], 7, None, ALU.logical_shift_right))
            do(V.tensor_copy(tmap[:, 1, :], cu[:, 1, :]))
            do(V.tensor_tensor_scan(tmap[:, 2, :], st["one"][:, :], tmap[:, 1, :], 0.0, ALU.mult, ALU.add))
            dve.sem_inc(st["maps_ready"], 1)
            do(V.tensor_scalar(tmap[:, 3, :], tmap[:, 1, :], -128.0, float(REGION), ALU.mult, ALU.add))

            def by_slot(a):
                return a.unsqueeze(2).broadcast_to([128, SLOTS, E - 1])

            def by_expert(a):
                return a.unsqueeze(1).broadcast_to([128, SLOTS, E - 1])

            slot = cst[:, C_SLOT:C_SLOT + SLOTS]
            slot_e, slot_row = st["slot_f"][:, 0, :], st["slot_f"][:, 1, :]
            do(V.tensor_tensor(big[:, 0, :, 0:E - 1], by_slot(slot), by_expert(tmap[:, 2, 0:E - 1]), ALU.is_ge))
            do(V.tensor_reduce(slot_e, big[:, 0, :, 0:E - 1], AX.X, ALU.add))
            steps.mark(V.tensor_copy(st["emap"][:, 0:SLOTS], slot_e))
            do(V.tensor_tensor(big[:, 1, :, 0:E - 1], big[:, 0, :, 0:E - 1], by_expert(tmap[:, 3, 0:E - 1]), ALU.mult))
            do(V.tensor_reduce(slot_row, big[:, 1, :, 0:E - 1], AX.X, ALU.add))
            do(V.scalar_tensor_tensor(slot_row, slot, 128.0, slot_row, ALU.mult, ALU.add))
            V.tensor_copy(st["rowmap"][:, 0:SLOTS], slot_row).then_inc(maps_done, 1)
            dve.wait_ge(maps_done, 1)

        @block.tensor
        def _(pe):
            pe.wait_ge(consts_in, n_const)
            pe.wait_ge(st["consts_in"], st["n_consts"])
            if not rope:
                pe.wait_ge(masks_set, 2)
                nc.tensor.matmul(Y[:, 0:B], keepA[:, :], keepP[:, :], start=True, stop=True).then_inc(counts_ready, 1)
            else:
                pe.wait_ge(masks_set, 1)
            pe.wait_ge(st["ident_ready"], 1)

            def front_x(i):
                j, p = i + 1, i - 2
                if live(j):
                    pe.wait_ge(xn_ready, 2 * j + 2)
                wait(pe, res_done, 2 * i - 1 if live(i - 1) else 0 if live(j) else B)
                if live(p):
                    pe.wait_ge(xr_ready, p + 1)
                    wait(pe, lg_read, p)
                rows_of = ([xn[:, 0, :], xn[:, 1, :]] if live(j) else [None] * 2) + ([xr[:, 0, :], xr[:, 1, :]] if live(p) else [])
                for at, rows_in in enumerate(rows_of):
                    if rows_in is not None:
                        last = nc.tensor.transpose(M1[:, at * T:(at + 1) * T], rows_in, ident)
                last.then_inc(xT_ready, 1)

            def front_qkv(j):
                pe.wait_ge(ctx_in, 16 * j + 16)
                wait(pe, sub_done, 2 * j)
                nc.tensor.matmul(Kp, wt["k"], ctxT[:, :], start=True, stop=True)
                if rope:
                    nc.tensor.matmul(Krp, wt["kr"], ctxT[:, :], start=True, stop=True)
                for s in range(2):
                    last = nc.tensor.matmul(Vp[s], ctxT[:, s * TK:(s + 1) * TK], wt["v"], start=True, stop=True)
                last.then_inc(kv_ready, 1)
                pe.wait_ge(xT_copied, j + 1)
                if live(j - 2):
                    pe.wait_ge(res_done, 2 * j - 2)
                if live(j - 3):
                    pe.wait_ge(lg_read, j - 2)
                last = nc.tensor.matmul(Qp, wt["q"], xT[:, 0:2 * T], start=True, stop=True)
                if rope:
                    last = nc.tensor.matmul(Qrp, wt["qr"], xT[:, 0:2 * T], start=True, stop=True)
                last.then_inc(q_ready, 1)

            def router_logits(p):
                pe.wait_ge(xT_copied, p + 4)
                for s in range(2):
                    last = nc.tensor.matmul(lgp[:, s * E:(s + 1) * E], xT[:, (2 + s) * T:(3 + s) * T], st["Wg"][layer][:, :],
                                            start=True, stop=True)
                last.then_inc(lg_ready, 1)

            def ranks(p, i):
                pe.wait_ge(both_ready, p + 1)
                pe.wait_ge(norm_done, 2 * i if live(i - 1) else B)
                pe.wait_ge(aT_copied, 2 * i - 1 if live(i - 1) else B)
                wait(pe, rank_copied, p)
                nc.tensor.matmul(rankp[:, 0:2 * E], beforeb[:, :], both[:, :, :], start=True, stop=False)
                nc.tensor.matmul(rankp[:, E:2 * E], onesb[:, :], both[:, 0, :], start=False, stop=True)
                nc.tensor.matmul(rankp[:, 2 * E:4 * E], onesb[:, :], both[:, :, :], start=True, stop=True).then_inc(rank_ready, 1)

            def scores(n, s, i):
                pe.wait_ge(qexp_ready, i + 1)
                pe.wait_ge(kexp_ready, n + 1)
                wait(pe, sub_done, n)
                if s == 0:
                    pe.wait_ge(v_copied, i + 1)
                for g in range(G):
                    out = S[:, g, 0:GK]
                    nc.tensor.matmul(out, qexp[:, s, g, :], kexp[:, s, :, :], start=True, stop=False)
                    last = nc.tensor.matmul(out, identb[:, :], bias_qk[:, s, :].unsqueeze(1).broadcast_to([128, J, TK]),
                                            start=False, stop=True)
                last.then_inc(s_ready, 1)

            def transpose_group(n, s, r):
                wait(pe, pt_copied, n * G + (r - 1))
                for j in range(J):
                    last = nc.tensor.transpose(ptp[r % 2][:, j, :], pr[:, s, r * J + j, :], ident)
                last.then_inc(pt_ready, 1)

            def value_group(n, s, r, i):
                if r == 0:
                    wait(pe, aT_copied, n)
                    if not s and live(i - 3):
                        pe.wait_ge(rank_copied, i - 2)
                pe.wait_ge(pt_copied, n * G + (r + 1))
                for j in range(J):
                    h = r * J + j
                    first, end = (0, VW) if h == 0 else (0, VN) if (h + 1) * VC <= VN else (VW - VN, VW)
                    last = nc.tensor.matmul(O[:, first:end], pT[:, r, j, :], vm[:, s, h * VW + first:h * VW + end],
                                            start=(h == 0), stop=(h == H - 1))
                if r == G - 1:
                    last.then_inc(pv_done, 1)

            def values(n, s, i, between=None, first=None):
                pe.wait_ge(exp_done, n + 1)
                transpose_group(n, s, 0)
                transpose_group(n, s, 1)
                if first:
                    first()
                pe.wait_ge(vm_ready, n + 1)
                value_group(n, s, 0, i)
                transpose_group(n, s, 2)
                if between:
                    between()
                value_group(n, s, 1, i)
                transpose_group(n, s, 3)
                value_group(n, s, 2, i)
                value_group(n, s, 3, i)

            def transpose_out(n, s):
                pe.wait_ge(norm_done, n + 1)
                nc.tensor.transpose(anTp, an[:, s, :], ident).then_inc(anT_ready, 1)

            def project_out(n, s, i):
                pe.wait_ge(aT_copied, n + 1)
                wait(pe, res_done, n)
                if s and (live(i + 1) or live(i - 2)):
                    pe.wait_ge(xT_copied, i + 2)
                elif not s:
                    wait(pe, qexp_ready, i + 1 if live(i) else NP)
                nc.tensor.matmul(Y, aT[:, :], wt["o"], start=True, stop=True).then_inc(y_ready, 1)

            if not rope:
                pe.wait_ge(mv_set, 3)
            front_x(-1)
            front_qkv(0)

            def turn(i):
                a, b = 2 * i, 2 * i + 1
                if live(i):
                    scores(a, 0, i)
                if live(i - 1):
                    transpose_out(a - 2, 0)
                    values(b - 2, 1, i, first=lambda: project_out(a - 2, 0, i))
                if live(i):
                    scores(b, 1, i)
                if live(i - 3):
                    ranks(i - 3, i)
                if live(i - 1):
                    transpose_out(b - 2, 1)
                if live(i + 1) or live(i - 2):
                    front_x(i)

                def last_products():
                    if live(i - 2):
                        router_logits(i - 2)
                    if live(i - 1):
                        project_out(b - 2, 1, i)

                if live(i):
                    values(a, 0, i, between=(lambda: front_qkv(i + 1)) if live(i + 1) else None, first=last_products)
                else:
                    last_products()

            turns(turn, pe)


def experts(nc, st, layer, w):
    two = layer == 1
    U = 8 if two else 4
    HU = U // 2
    F = F1 if two else F0
    FC = 2 if two else 4
    UW = 2 * F if two else F
    NSH = B if two else 0
    NS = NSH + SLOTS
    NT = NS // U
    CH = B // U
    with ExitStack() as ctx:
        def sb(name, shape, dt=F32):
            return ctx.enter_context(nc.sbuf_tensor(f"{name}_e{layer}", shape, dt))

        def pb(name):
            return ctx.enter_context(nc.psum_tensor(f"{name}_e{layer}", [128, 4, 128], F32))

        def sem(name):
            return ctx.enter_context(nc.semaphore(f"{name}_e{layer}"))

        three, x, cst, emap, rowmap = st["three"], st["x"], st["cst"], st["emap"], st["rowmap"]
        ident = cst[:, C_ID:C_ID + 128]
        W1, W2 = w["W1"], w["W2"]
        xs = sb("xs", [128, U, RW])
        xi = sb("xi", [128, U], U32)
        xsT = sb("xsT", [128, 2, 128])
        hb = sb("hb", [128, 2, F])
        hm = sb("hm", [128, 2, F])
        h = sb("h", [128, 2, FC * 128])
        hT = sb("hT", [128, 2, FC, 128])
        ys = sb("ys", [128, U, D])
        if two:
            yg = sb("yg", [128, 2, B, D])

        xTp = pb("xTp")
        up = [pb(f"up{i}")[:, :, :].rearrange("p a c -> p (a c)") for i in range(2)]
        hTp = [pb(f"hTp{i}") for i in range(2)]
        yp = [pb(f"yp{i}")[:, 0, :] for i in range(2)]

        xs_in = [sem(f"xs_in{s}") for s in range(U)]
        xi_copied = sem("xi_copied")
        xsT_ready, xsT_copied = sem("xsT_ready"), sem("xsT_copied")
        up_ready, hb_ready, h_ready = sem("up_ready"), sem("hb_ready"), sem("h_ready")
        hT_ready, hT_copied = sem("hT_ready"), sem("hT_copied")
        yp_ready, ys_ready = sem("yp_ready"), sem("ys_ready")
        ys_out = [sem(f"ys_out{s}") for s in range(U)]
        if two:
            h_set = sem("h_set")
            results_in = sem("results_in")
            weighted = sem("weighted")
            summed = sem("summed")
            x_done = sem("x_done")
        dve_step = sem("dve_step")

        rows, results = w["rows"], w["results"]

        def wait(eng, s, value):
            if not isinstance(value, int) or value > 0:
                eng.wait_ge(s, value)

        def row(t, n):
            return t[:, bass.ds(n, 1), :].rearrange("p a d -> p (a d)")

        EDGE = SLOTS // U

        def turns(body, eng, steps=None):
            def loop(start, end, routed):
                with eng.Fori(start, end) as i:
                    if steps:
                        steps.turn(i - start)
                    body(i, routed)
                if steps:
                    steps.leave(end - start)

            def peeled(i):
                if steps:
                    steps.turn()
                body(i, None)

            peeled(0)
            peeled(1)
            if two:
                loop(2, EDGE - 1, True)
                peeled(EDGE - 1)
                peeled(EDGE)
                peeled(EDGE + 1)
                loop(EDGE + 2, NT - 1, False)
            else:
                loop(2, NT - 1, True)
            peeled(NT - 1)
            peeled(NT)

        def live(n):
            return not isinstance(n, int) or 0 <= n < NS

        def chunk(i, routed):
            if not two or routed or (routed is None and not EDGE < i <= EDGE + CH):
                return None
            return i - (EDGE + 1)

        def ready_slots(c):
            return c * U + (SLOTS + U)

        def is_routed(n, routed):
            return n < SLOTS if routed is None else routed

        def expert(eng, n, routed):
            if not is_routed(n, routed):
                return E
            return nc.s_assert_within(eng.value_load(emap[0:1, bass.ds(n, 1)]), 0, E - 1,
                                      skip_runtime_bounds_check_because="VectorE bounds the map's entries by E - 1")

        def reuse(i):
            return 16 * i

        block = ctx.enter_context(nc.Block())

        @block.sync
        def _(sp):
            def load(n, s, routed):
                if n is not s:
                    wait(sp, xsT_ready, n - (U - 1))
                    if is_routed(n - U if isinstance(n, int) else n, routed):
                        wait(sp, xi_copied, n - (U - 1))
                if is_routed(n, routed):
                    r = nc.s_assert_within(sp.value_load(rowmap[0:1, bass.ds(n, 1)]), 0, SHARED - 128,
                                           skip_runtime_bounds_check_because="the map's rows are those of its experts' tiles")
                else:
                    r = n * 128 + (SHARED - SLOTS * 128)
                sp.dma_start(xs[:, s, :], rows[bass.ds(r, 128), :]).then_inc(xs_in[s], 16)

            for s in range(U):
                load(s, s, None)

            def load_results(c):
                if isinstance(c, int) and c == 0:
                    for s in range(U):
                        sp.wait_ge(ys_out[s], 16 * SLOTS // U)
                wait(sp, results_in, 32 * c)
                for k in range(2):
                    sp.dma_start(yg[:, k, bass.ds(c * U, U), :], results[k * N:(k + 1) * N, :].rearrange("(b p) d -> p b d", p=128)
                                 [:, bass.ds(c * U, U), :]).then_inc(results_in, 16)

            def store(c):
                sp.wait_ge(x_done, 2 * c + 2)
                sp.dma_start(st["out_dram"][:, bass.ds(c * U, U), :], x[:, bass.ds(c * U, U), :]).then_inc(st["x_out"], 16)

            def turn(i, routed):
                c = chunk(i, routed)
                if c is not None:
                    if isinstance(c, int) and c == 0:
                        load_results(0)
                    if not isinstance(c, int) or c + 1 < CH:
                        load_results(c + 1)
                for s in range(U):
                    if live(U * i + s + U):
                        load(U * i + U + s, s, routed)
                if c is not None and not (isinstance(c, int) and c == 0):
                    store(c - 1)

            turns(turn, sp)
            if two:
                store(CH - 1)
                sp.wait_ge(st["x_out"], 16 * CH)
            else:
                for s in range(U):
                    sp.wait_ge(ys_out[s], 16 * SLOTS // U)

        @block.gpsimd
        def _(pool):
            if two:
                nc.gpsimd.memset(h[:, :, :], 0.0).then_inc(h_set, 1)
                pool.wait_ge(h_set, 1)
                nc.gpsimd.memset(h[:, :, F:F + 1], 1.0).then_inc(h_set, 1)

            def send(s):
                nc.gpsimd.indirect_dma_start(results[:, :], bass.IndirectOffsetOnAxis(xi[:, s:s + 1], 0), ys[:, s, :], None)\
                    .then_inc(ys_out[s], 16)

            def note(n, s, i, results_of):
                wait(pool, ys_out[s], reuse(i))
                pool.wait_ge(xs_in[s], 16 * i + 16)
                if results_of is not None:
                    pool.wait_ge(ys_ready, results_of + 1)
                    pool.wait_ge(xi_copied, results_of + 1)
                nc.gpsimd.tensor_tensor(xi[:, s:s + 1], xs[:, s, D:D + 1].bitcast(U32), st["zero"][:, 0:1], ALU.add).then_inc(xi_copied, 1)

            def take_results(c, half):
                pool.wait_ge(weighted, 2 * c + (half + 1))
                y = [yg[:, k, bass.ds(c * U + half * HU, HU), :] for k in range(2)]
                nc.gpsimd.tensor_tensor(y[0], y[0], y[1], ALU.add).then_inc(summed, 1)
                pool.wait_ge(summed, 2 * c + (half + 1))
                pool.wait_ge(ys_ready, ready_slots(c))
                xb = x[:, bass.ds(c * U + half * HU, HU), :]
                nc.gpsimd.tensor_tensor(xb, xb, y[0], ALU.add).then_inc(x_done, 1)

            def turn(i, routed):
                for s in range(U):
                    n = U * i + s
                    sends = live(n - 3) and is_routed(n - 3, routed)
                    if live(n - 1) and is_routed(n - 1, routed):
                        note(n - 1, (s - 1) % U, i - (s < 1), n - 3 if sends else None)
                    elif sends:
                        pool.wait_ge(ys_ready, n - 2)
                        pool.wait_ge(xi_copied, n - 2)
                    if sends:
                        send((s - 3) % U)
                c = chunk(i, routed)
                if c is not None:
                    take_results(c, 0)
                    take_results(c, 1)

            turns(turn, pool)

        @block.scalar
        def _(act):
            act.wait_ge(st["weights_in"], st["n_weights"])
            if two:
                act.wait_ge(h_set, 2)

            def x_copy(n, s):
                act.wait_ge(xsT_ready, n + 1)
                nc.scalar.activation(xsT[:, s % 2, :], xTp[:, 0, :], ACT.Copy).then_inc(xsT_copied, 1)

            def silu(n, s):
                if two:
                    act.wait_ge(hb_ready, n + 1)
                    nc.scalar.activation(h[:, s % 2, 0:F], hm[:, s % 2, :], ACT.Silu).then_inc(h_ready, 1)
                else:
                    act.wait_ge(up_ready, n + 1)
                    nc.scalar.activation(h[:, s % 2, :], up[s % 2][:, :], ACT.Silu).then_inc(h_ready, 1)

            def h_copy(n, s):
                act.wait_ge(hT_ready, n + 1)
                nc.scalar.activation(hT[:, s % 2, :, :], hTp[s % 2][:, 0:FC, :], ACT.Copy).then_inc(hT_copied, 1)

            def weigh(c, t):
                if t == 0:
                    act.wait_ge(results_in, 32 * c + 32)
                for k in range(2):
                    y = yg[:, k, bass.ds(c * U + t, 1), :].rearrange("p a d -> p (a d)")
                    last = nc.scalar.activation(y, y, ACT.Copy, scale=st["wsel"][1][:, k, bass.ds(c * U + t, 1)])
                if t % HU == HU - 1:
                    last.then_inc(weighted, 1)

            x_copy(0, 0)

            def turn(i, routed):
                c = chunk(i, routed)
                for s in range(U):
                    n = U * i + s
                    if live(n + 1):
                        x_copy(n + 1, s + 1)
                    if two and live(n - 1):
                        h_copy(n - 1, s + 1)
                    if live(n):
                        silu(n, s)
                    if c is not None:
                        weigh(c, s)

            turns(turn, act)

        @block.vector
        def _(dve):
            steps = Steps(dve_step)
            V = nc.vector

            def hidden(n, s):
                dve.wait_ge(up_ready, n + 1)
                steps.then(dve, V.tensor_copy(hb[:, s % 2, :], up[s % 2][:, 0:F]))
                V.tensor_tensor(hm[:, s % 2, :], hb[:, s % 2, :], up[s % 2][:, F:UW], ALU.mult).then_inc(hb_ready, 1)

            def h_copy(n, s):
                dve.wait_ge(hT_ready, n + 1)
                V.tensor_copy(hT[:, s % 2, :, :], hTp[s % 2][:, 0:FC, :]).then_inc(hT_copied, 1)

            def y_copy(n, s, i, routed):
                if routed:
                    wait(dve, ys_out[s], reuse(i))
                dve.wait_ge(yp_ready, n + 1)
                if routed:
                    V.tensor_copy(ys[:, s, :], yp[s % 2]).then_inc(ys_ready, 1)
                else:
                    xb = row(x, n - SLOTS)
                    V.tensor_tensor(xb, xb, yp[s % 2], ALU.add).then_inc(ys_ready, 1)

            def turn(i, routed):
                for s in range(U):
                    n = U * i + s
                    if two:
                        if live(n):
                            hidden(n, s)
                    elif live(n - 1):
                        h_copy(n - 1, s + 1)
                    if live(n - 2):
                        y_copy(n - 2, (s - 2) % U, i - (s < 2), is_routed(n - 2, routed))

            turns(turn, dve, steps)

        @block.tensor
        def _(pe):
            pe.wait_ge(st["weights_in"], st["n_weights"])
            pe.wait_ge(st["bias_in"], 16)

            def take(n, s, i):
                pe.wait_ge(xs_in[s], 16 * i + 16)
                nc.tensor.transpose(xTp[:, 0, :], xs[:, s, 0:D], ident).then_inc(xsT_ready, 1)

            def widen(n, s, e):
                pe.wait_ge(xsT_copied, n + 1)
                last = nc.tensor.matmul(up[s % 2][:, 0:UW], xsT[:, s % 2, :], row(W1, e), start=True, stop=not two)
                if two:
                    last = nc.tensor.matmul(up[s % 2][:, 0:UW], three[:, :], row(w["B1"], e), start=False, stop=True)
                last.then_inc(up_ready, 1)

            def turn_hidden(n, s):
                pe.wait_ge(h_ready, n + 1)
                for c in range(FC):
                    last = nc.tensor.transpose(hTp[s % 2][:, c, :], h[:, s % 2, c * 128:(c + 1) * 128], ident)
                last.then_inc(hT_ready, 1)

            def narrow(n, s, e):
                pe.wait_ge(hT_copied, n + 1)
                if isinstance(n, int) and n == NS - 1:
                    pe.wait_ge(ys_ready, n - 1)
                w2 = W2[:, bass.ds(e, 1), :, :].rearrange("p a c d -> p (a c) d")
                for c in range(FC):
                    last = nc.tensor.matmul(yp[s % 2], hT[:, s % 2, c, :], w2[:, c, :], start=(c == 0),
                                            stop=(c == FC - 1))
                last.then_inc(yp_ready, 1)

            take(0, 0, 0)

            def turn(i, routed):
                of = {0: expert(pe, U * i, routed)} if live(U * i) else {}
                for s in range(U):
                    n = U * i + s
                    if live(n):
                        widen(n, s, of[s])
                    if live(n + 1):
                        take(n + 1, (s + 1) % U, i + (s == U - 1))
                    if live(n - 1):
                        turn_hidden(n - 1, s + 1)
                    if s < 2 and live(n - 2):
                        of[s - 2] = expert(pe, n - 2, routed)
                    if s + 1 < U and live(n + 1):
                        of[s + 1] = expert(pe, n + 1, routed)
                    if live(n - 2):
                        narrow(n - 2, s, of[s - 2])

            turns(turn, pe)


def build(nc, dram, phases=4):
    with ExitStack() as ctx:
        def sb(name, shape, dt=F32):
            return ctx.enter_context(nc.sbuf_tensor(name, shape, dt))

        I32 = mybir.dt.int32
        st = {"x": sb("x_res", [128, B, D]), "cst": sb("cst", [128, C_END]), "identb": sb("identb", [128, 128], BF16),
              "wsel": [sb(f"wsel{l}", [128, 2, B]) for l in range(2)], "Wg": [sb(f"Wg{l}", [128, E]) for l in range(2)],
              "dest": sb("dest", [128, 2, 4], U32), "fill": sb("fill", [128, E], I32),
              "out_rows": sb("out_rows", [128, 2, 3, RW]), "onesb": sb("onesb", [128, 128], BF16),
              "beforeb": sb("beforeb", [128, 128], BF16), "mv": sb("mv", [128, 4, 2]), "vm": sb("vm", [TK, 2, VM]),
              "tiles": sb("tiles", [128, 4, E]), "tiles_u": sb("tiles_u", [128, 2, E], U32), "one": sb("one", [128, E]), "zero": sb("zero", [128, E], U32),
              "onward": sb("onward", [128, E], U32),
              "big": sb("big", [128, 2, SLOTS, E]), "slot_f": sb("slot_f", [128, 2, SLOTS]),
              "emap": sb("emap", [128, SLOTS], I32), "rowmap": sb("rowmap", [128, SLOTS], I32)}
        st["filling"] = dram["filling"]
        st["ctxT_dram"], st["n_consts"], st["n_weights"] = dram["ctxT"], 16 * 5 + 4, 16 * 4
        parts = sb("parts", [3, NB], BF16)
        st["parts"], st["parts_dram"] = parts, nc.dram_tensor("bias_parts", (3, NB), BF16, kind="Internal").ap()
        st["bias"], st["bias_parts"], st["bias_rest"] = (sb("bias", [NBP, NB // NBP]), sb("bias_p", [NBP, 3, NB // NBP], BF16),
                                                         sb("bias_r", [NBP, 2, NB // NBP]))
        st["three"] = sb("three", [3, 128], BF16)
        w0 = {"W1": sb("W1_0", [128, E, F0]), "W2": sb("W2_0", [128, E, F0 // 128, D])}
        w1 = {"W1": sb("W1_1", [128, E + 1, 2 * F1]), "W2": sb("W2_1", [128, E + 1, 2, D]),
              "B1": parts[:, :].rearrange("k (e f) -> k e f", e=E + 1)}
        prefetch = [(t[:], dram[f"e0_{k}"]) for k, t in w0.items()]
        prefetch += [(w1[k][:], dram[f"e1_{k}"]) for k in ("W1", "W2")]
        for name in ("consts_in", "x_in", "ident_ready", "weights_in", "maps_ready", "x_out", "bias_split", "bias_out", "bias_in"):
            st[name] = ctx.enter_context(nc.semaphore(f"{name}_all"))
        rows = [nc.dram_tensor(f"rows{l}", (SHARED + l * N, RW), F32, kind="Internal").ap() for l in range(2)]
        results = [nc.dram_tensor(f"results{l}", (2 * N + (E + PAST) * 128, D), F32, kind="Internal").ap() for l in range(2)]
        st["x_dram"] = dram["x"].rearrange("b t d -> t b d")
        st["out_dram"] = dram["out"].rearrange("b t d -> t b d")
        with nc.Block() as block:
            @block.sync
            def _(sp):
                sp.dma_start(st["cst"][:, :], dram["cst"]).then_inc(st["consts_in"], 16)
                sp.dma_start(st["x"][:, 0:2, :], st["x_dram"][:, 0:2, :]).then_inc(st["x_in"], 16)
                for l in range(2):
                    sp.dma_start(st["Wg"][l][:, :], dram[f"e{l}_Wg"]).then_inc(st["consts_in"], 16)
                sp.dma_start(st["bias"][:, :], dram["e1_B"]).then_inc(st["consts_in"], 16)
                sp.dma_start(st["dest"][:, :, :], dram["dest"]).then_inc(st["consts_in"], 16)

            @block.gpsimd
            def _(pool):
                nc.gpsimd.memset(st["one"][:, :], 1.0).then_inc(st["consts_in"], 1)
                nc.gpsimd.memset(st["three"][:, :], 1.0).then_inc(st["consts_in"], 1)
                nc.gpsimd.memset(st["zero"][:, :], 0).then_inc(st["consts_in"], 1)
                nc.gpsimd.memset(st["onward"][:, :], 2 * T).then_inc(st["consts_in"], 1)

            @block.vector
            def _(dve):
                dve.wait_ge(st["consts_in"], st["n_consts"])
                nc.vector.tensor_copy(st["identb"][:, :], st["cst"][:, C_ID:C_ID + 128]).then_inc(st["ident_ready"], 1)

        names = ("W", "cols", "bo", "bv")
        if phases >= 1:
            attention(nc, st, 0, {**{k: dram[f"a0_{k}"] for k in names + ("am", "amT", "pad", "padT")},
                                  "rows": rows[0], "prefetch": prefetch})
        if phases >= 2:
            experts(nc, st, 0, {**w0, "rows": rows[0], "results": results[0]})
        if phases >= 3:
            attention(nc, st, 1, {**{k: dram[f"a1_{k}"] for k in names}, "gb": dram["e1_gb"], "rows": rows[1],
                                  "results": results[0], "prefetch": []})
        if phases >= 4:
            experts(nc, st, 1, {**w1, "rows": rows[1], "results": results[1]})
        else:
            with nc.Block() as block:
                @block.sync
                def _(sp):
                    sp.dma_start(st["out_dram"], st["x"][:, :, :]).then_inc(st["x_out"], 16)
                    sp.wait_ge(st["x_out"], 16)


def layout(v):
    a = {k: np.asarray(t) for k, t in v.items()}
    swap = np.arange(D).reshape(H, 2, DH // 2)[:, ::-1].reshape(D)
    out = {"x": a["x"], "cst": shape_constants()}
    out["dest"] = (np.arange(4)[None, None] * N + np.arange(2)[None, :, None] * T + np.arange(T)[:, None, None]).astype(np.uint32)
    out["filling"] = np.zeros(((E + PAST) * 128, RW), np.uint32)
    out["filling"][:, D] = 2 * N + np.arange((E + PAST) * 128)
    out["filling"] = out["filling"].view(np.float32)
    out["ctxT"] = a["ctx_1024"].transpose(2, 0, 1).reshape(D, B * TK)
    q = "L0_xattn_"
    out["a0_W"] = np.stack([a[q + n].T for n in ("Wq", "Wk", "Wv", "Wo")], 1)
    out["a0_cols"] = np.stack([a[q + n] for n in ("bq", "bk", "bv", "bo")], 1)
    out["a0_bo"], out["a0_bv"] = a[q + "bo"], a[q + "bv"]
    mask, pad = a["mask_SxS2_bk1"], a["mask_BxS2_bf0"]
    out["a0_am"], out["a0_amT"], out["a0_pad"], out["a0_padT"] = mask, mask.T, pad.reshape(-1), pad.T
    q = "L1_xattn_"
    out["a1_W"] = np.stack([a[q + n + "_w"].T for n in "qkvo"] + [a[q + n + "_w"][swap].T for n in "qk"], 1)
    out["a1_cols"] = np.stack([a[q + n + "_b"] for n in "qkvo"] + [a[q + n + "_b"][swap] for n in "qk"], 1)
    out["a1_bo"], out["a1_bv"] = a[q + "o_b"], a[q + "v_b"]
    out["e0_Wg"] = a["L0_ffn_Wg"].T
    out["e0_W1"] = a["L0_ffn_W1"].transpose(1, 0, 2)
    out["e0_W2"] = a["L0_ffn_W2"].reshape(E0, F0 // 128, 128, D).transpose(2, 0, 1, 3)
    f = {k: np.concatenate([a["L1_ffn_" + k], a["L1_ffn_s" + k][None]]) for k in ("w1", "w3", "b1", "b3", "w2", "b2")}
    w2 = np.zeros((E1 + 1, 256, D), np.float32)
    w2[:, :F1], w2[:, F1] = f["w2"], f["b2"]
    out["e1_Wg"] = a["L1_ffn_gate_w"].T
    out["e1_W1"] = np.concatenate([f["w1"], f["w3"]], 2).transpose(1, 0, 2)
    out["e1_W2"] = w2.reshape(E1 + 1, 2, 128, D).transpose(2, 0, 1, 3)
    out["e1_B"] = np.concatenate([f["b1"], f["b3"]], 1).reshape(NBP, -1)
    out["e1_gb"] = a["L1_ffn_gate_b"]
    return {k: np.ascontiguousarray(t) for k, t in out.items()}


def kernel(**inputs):
    import concourse.bacc as bacc
    from concourse.bass_utils import run_bass_kernel_spmd

    nc = bacc.Bacc("TRN2", target_bir_lowering=False, num_devices=1)
    arrays = layout(inputs)
    dram = {k: nc.dram_tensor(f"in_{k}", t.shape, mybir.dt.from_np(t.dtype), kind="ExternalInput").ap()
            for k, t in arrays.items()}
    dram["out"] = nc.dram_tensor("out_x", (B, T, D), F32, kind="ExternalOutput").ap()
    build(nc, dram)
    r = run_bass_kernel_spmd(nc, [{f"in_{k}": t for k, t in arrays.items()}], core_ids=[0])
    return r.results[0]["out_x"]
```
